# Optimizing a Trainium2 kernel written in Bass

```python
import numpy as np
import jax
import jax.numpy as jnp

def _softmax(x, axis=-1):
    return jax.nn.softmax(x, axis=axis)

def _gelu(x):
    return jax.nn.gelu(x, approximate=True)

def _silu(x):
    return jax.nn.silu(x)

def _sigmoid(x):
    return jax.nn.sigmoid(x)

def _layernorm(x, axis=-1, eps=1e-05):
    m = jnp.mean(x, axis=axis, keepdims=True)
    v = jnp.var(x, axis=axis, keepdims=True)
    return (x - m) / jnp.sqrt(v + eps)

def _scatter_add(tgt, idx, src, axis=0):
    return tgt.at[idx].add(src)

def _segment_sum(src, seg, n):
    return jax.ops.segment_sum(src, seg, n)
kernel_name = 'mk_flamingo_gated_d1_seqx_r4_26f096'

def setup_inputs(seed: int=0):
    np.random.seed(seed)
    _w = jnp.asarray

    def _rec_inputs():
        import jax
        import jax.numpy as jnp
        _rk = jax.random.key(seed)
        x = -0.0003929 + 0.9999 * jax.random.normal(jax.random.fold_in(_rk, 1), (8, 112, 512), jnp.float32)
        _lenS = 112 - jax.random.randint(jax.random.fold_in(_rk, 7), (8,), 0, max(1, 112 // 4) + 1, jnp.int32)
        _lenS2 = 375 - jax.random.randint(jax.random.fold_in(_rk, 8), (8,), 0, max(1, 375 // 4) + 1, jnp.int32)
        _ctx_2048P = jax.random.normal(jax.random.fold_in(_rk, 11), (8, 16, 512), jnp.float32)
        _ctx_2048c = jax.random.dirichlet(jax.random.fold_in(_rk, 511), 0.3 * jnp.ones((16,), jnp.float32), (8, 375))
        _ctx_2048t = jnp.einsum('bsk,bkd->bsd', _ctx_2048c, _ctx_2048P)
        _ctx_2048t = _ctx_2048t * jax.lax.rsqrt(jnp.mean(jnp.square(_ctx_2048t)) + 1e-12) * 0.953939
        ctx_2048 = 1.72703e-05 + 1.00003 * (_ctx_2048t + 0.3 * jax.random.normal(jax.random.fold_in(_rk, 611), (8, 375, 512), jnp.float32))
        _g = jax.random.normal(jax.random.fold_in(_rk, 9001), (2, 1), jnp.float32)
        _g = jnp.sign(_g) * jnp.maximum(jnp.abs(_g), 1.0) + (_g == 0) * 1.0
        g_xattn = _g[0]
        g_ffn = _g[1]
        return (x, ctx_2048, g_xattn, g_ffn)
    x, ctx_2048, g_xattn, g_ffn = _rec_inputs()

    def _L0_xattn_setup():
        import jax, jax.numpy as jnp
        import numpy as np
        DIM = 512
        H = 16
        D = 128
        INNER = H * D
        N_IMG = 257
        EPS = 1e-06

        def rms_norm(x, scale, eps=EPS):
            ms = jnp.mean(jnp.square(x), axis=-1, keepdims=True)
            return x * jax.lax.rsqrt(ms + eps) * scale

        def sdpa(q, k, v):
            scale = 1.0 / jnp.sqrt(jnp.asarray(D, q.dtype))
            scores = jnp.einsum('bshd,blhd->bhsl', q, k) * scale
            attn = jax.nn.softmax(scores, axis=-1)
            return jnp.einsum('bhsl,blhd->bshd', attn, v)
        key = jax.random.key(seed)
        ks = jax.random.split(key, 16)
        std = 1.0 / np.sqrt(DIM)
        inp = {'x': jax.random.normal(ks[0], (2, 1024, DIM), jnp.float32), 'context': jax.random.normal(ks[1], (2, 769, DIM), jnp.float32), 'q_w': jax.random.normal(ks[2], (DIM, INNER), jnp.float32) * std, 'q_b': jnp.zeros((INNER,), jnp.float32), 'k_w': jax.random.normal(ks[3], (DIM, INNER), jnp.float32) * std, 'k_b': jnp.zeros((INNER,), jnp.float32), 'v_w': jax.random.normal(ks[4], (DIM, INNER), jnp.float32) * std, 'v_b': jnp.zeros((INNER,), jnp.float32), 'ki_w': jax.random.normal(ks[5], (DIM, INNER), jnp.float32) * std, 'ki_b': jnp.zeros((INNER,), jnp.float32), 'vi_w': jax.random.normal(ks[6], (DIM, INNER), jnp.float32) * std, 'vi_b': jnp.zeros((INNER,), jnp.float32), 'o_w': jax.random.normal(ks[7], (INNER, DIM), jnp.float32) * std, 'o_b': jnp.zeros((DIM,), jnp.float32), 'nq_s': jnp.ones((INNER,), jnp.float32), 'nkt_s': jnp.ones((INNER,), jnp.float32), 'nki_s': jnp.ones((INNER,), jnp.float32)}
        return inp
    _L0_xattn_all = _L0_xattn_setup()
    _L0_xattn_in = {k: v for k, v in _L0_xattn_all.items() if k in ('q_w', 'q_b', 'k_w', 'k_b', 'v_w', 'v_b', 'ki_w', 'ki_b', 'vi_w', 'vi_b', 'o_w', 'o_b', 'nq_s', 'nkt_s', 'nki_s')}
    del _L0_xattn_all

    def _L0_ffn_setup():
        import jax, jax.numpy as jnp
        import numpy as np
        E = 64
        K = 8
        H = 512
        I = 192
        CAP = 128

        def _moe(hidden_states, gate_w, wg, wu, wd):
            B, S, Hd = hidden_states.shape
            x = hidden_states.reshape(-1, Hd)
            T = x.shape[0]
            logits = x @ gate_w.T
            probs = jax.nn.softmax(logits.astype(jnp.float32), axis=-1)
            w, sel = jax.lax.top_k(probs, K)
            w = w / jnp.sum(w, axis=-1, keepdims=True)
            w = w.astype(x.dtype)
            eid = sel.reshape(-1)
            tok = jnp.repeat(jnp.arange(T), K)
            oh = jax.nn.one_hot(eid, E, dtype=jnp.int32)
            pos = jnp.sum(jnp.cumsum(oh, axis=0) * oh, axis=-1) - 1
            valid = pos < CAP
            slot = jnp.where(valid, pos, CAP)
            xin = jnp.zeros((E, CAP + 1, Hd), x.dtype).at[eid, slot].set(x[tok])
            inp = xin[:, :CAP]
            h = jax.nn.silu(jnp.einsum('ech,ehi->eci', inp, wg)) * jnp.einsum('ech,ehi->eci', inp, wu)
            out = jnp.einsum('eci,eih->ech', h, wd)
            out_pad = jnp.concatenate([out, jnp.zeros((E, 1, Hd), out.dtype)], axis=1)
            g = out_pad[eid, slot] * (w.reshape(-1) * valid.astype(w.dtype))[:, None]
            y = jnp.zeros((T, Hd), x.dtype).at[tok].add(g)
            return y.reshape(B, S, Hd)
        key = jax.random.key(seed)
        k1, k2, k3, k4, k5 = jax.random.split(key, 5)
        hidden_states = jax.random.normal(k1, (1, 512, H), dtype=jnp.float32)
        gate_w = jax.random.normal(k2, (E, H), dtype=jnp.float32) * 0.02
        wg = jax.random.normal(k3, (E, H, I), dtype=jnp.float32) * 0.02
        wu = jax.random.normal(k4, (E, H, I), dtype=jnp.float32) * 0.02
        wd = jax.random.normal(k5, (E, I, H), dtype=jnp.float32) * 0.02
        return {'hidden_states': hidden_states, 'gate_w': gate_w, 'wg': wg, 'wu': wu, 'wd': wd}
    _L0_ffn_all = _L0_ffn_setup()
    _L0_ffn_in = {k: v for k, v in _L0_ffn_all.items() if k in ('gate_w', 'wg', 'wu', 'wd')}
    del _L0_ffn_all
    return {'x': x, 'ctx_2048': ctx_2048, 'g_xattn': g_xattn, 'g_ffn': g_ffn, 'L0_xattn_q_w': _L0_xattn_in['q_w'], 'L0_xattn_q_b': _L0_xattn_in['q_b'], 'L0_xattn_k_w': _L0_xattn_in['k_w'], 'L0_xattn_k_b': _L0_xattn_in['k_b'], 'L0_xattn_v_w': _L0_xattn_in['v_w'], 'L0_xattn_v_b': _L0_xattn_in['v_b'], 'L0_xattn_ki_w': _L0_xattn_in['ki_w'], 'L0_xattn_ki_b': _L0_xattn_in['ki_b'], 'L0_xattn_vi_w': _L0_xattn_in['vi_w'], 'L0_xattn_vi_b': _L0_xattn_in['vi_b'], 'L0_xattn_o_w': _L0_xattn_in['o_w'], 'L0_xattn_o_b': _L0_xattn_in['o_b'], 'L0_xattn_nq_s': _L0_xattn_in['nq_s'], 'L0_xattn_nkt_s': _L0_xattn_in['nkt_s'], 'L0_xattn_nki_s': _L0_xattn_in['nki_s'], 'L0_ffn_gate_w': _L0_ffn_in['gate_w'], 'L0_ffn_wg': _L0_ffn_in['wg'], 'L0_ffn_wu': _L0_ffn_in['wu'], 'L0_ffn_wd': _L0_ffn_in['wd']}

def reference(x, ctx_2048, g_xattn, g_ffn, L0_xattn_q_w, L0_xattn_q_b, L0_xattn_k_w, L0_xattn_k_b, L0_xattn_v_w, L0_xattn_v_b, L0_xattn_ki_w, L0_xattn_ki_b, L0_xattn_vi_w, L0_xattn_vi_b, L0_xattn_o_w, L0_xattn_o_b, L0_xattn_nq_s, L0_xattn_nkt_s, L0_xattn_nki_s, L0_ffn_gate_w, L0_ffn_wg, L0_ffn_wu, L0_ffn_wd):
    import jax
    import jax.numpy as jnp

    def _L0_xattn_ref(x, context, q_w, q_b, k_w, k_b, v_w, v_b, ki_w, ki_b, vi_w, vi_b, o_w, o_b, nq_s, nkt_s, nki_s):
        import jax, jax.numpy as jnp
        import numpy as np
        DIM = 512
        H = 16
        D = 128
        INNER = H * D
        N_IMG = 257
        EPS = 1e-06

        def rms_norm(x, scale, eps=EPS):
            ms = jnp.mean(jnp.square(x), axis=-1, keepdims=True)
            return x * jax.lax.rsqrt(ms + eps) * scale

        def sdpa(q, k, v):
            scale = 1.0 / jnp.sqrt(jnp.asarray(D, q.dtype))
            scores = jnp.einsum('bshd,blhd->bhsl', q, k) * scale
            attn = jax.nn.softmax(scores, axis=-1)
            return jnp.einsum('bhsl,blhd->bshd', attn, v)
        B, S, _ = x.shape
        img_ctx = context[:, :N_IMG]
        txt_ctx = context[:, N_IMG:]
        q = rms_norm(x @ q_w + q_b, nq_s).reshape(B, S, H, D)
        k_txt = rms_norm(txt_ctx @ k_w + k_b, nkt_s).reshape(B, -1, H, D)
        v_txt = (txt_ctx @ v_w + v_b).reshape(B, -1, H, D)
        out_txt = sdpa(q, k_txt, v_txt)
        k_img = rms_norm(img_ctx @ ki_w + ki_b, nki_s).reshape(B, -1, H, D)
        v_img = (img_ctx @ vi_w + vi_b).reshape(B, -1, H, D)
        out_img = sdpa(q, k_img, v_img)
        out = (out_txt + out_img).reshape(B, S, INNER)
        return out @ o_w + o_b

    def _L0_ffn_ref(hidden_states, gate_w, wg, wu, wd):
        import jax, jax.numpy as jnp
        import numpy as np
        E = 64
        K = 8
        H = 512
        I = 192
        CAP = 128

        def _moe(hidden_states, gate_w, wg, wu, wd):
            B, S, Hd = hidden_states.shape
            x = hidden_states.reshape(-1, Hd)
            T = x.shape[0]
            logits = x @ gate_w.T
            probs = jax.nn.softmax(logits.astype(jnp.float32), axis=-1)
            w, sel = jax.lax.top_k(probs, K)
            w = w / jnp.sum(w, axis=-1, keepdims=True)
            w = w.astype(x.dtype)
            eid = sel.reshape(-1)
            tok = jnp.repeat(jnp.arange(T), K)
            oh = jax.nn.one_hot(eid, E, dtype=jnp.int32)
            pos = jnp.sum(jnp.cumsum(oh, axis=0) * oh, axis=-1) - 1
            valid = pos < CAP
            slot = jnp.where(valid, pos, CAP)
            xin = jnp.zeros((E, CAP + 1, Hd), x.dtype).at[eid, slot].set(x[tok])
            inp = xin[:, :CAP]
            h = jax.nn.silu(jnp.einsum('ech,ehi->eci', inp, wg)) * jnp.einsum('ech,ehi->eci', inp, wu)
            out = jnp.einsum('eci,eih->ech', h, wd)
            out_pad = jnp.concatenate([out, jnp.zeros((E, 1, Hd), out.dtype)], axis=1)
            g = out_pad[eid, slot] * (w.reshape(-1) * valid.astype(w.dtype))[:, None]
            y = jnp.zeros((T, Hd), x.dtype).at[tok].add(g)
            return y.reshape(B, S, Hd)
        return _moe(hidden_states, gate_w, wg, wu, wd)
    x = x + jnp.tanh(g_xattn[0]) * _L0_xattn_ref(_layernorm(x, axis=-1), ctx_2048, L0_xattn_q_w, L0_xattn_q_b, L0_xattn_k_w, L0_xattn_k_b, L0_xattn_v_w, L0_xattn_v_b, L0_xattn_ki_w, L0_xattn_ki_b, L0_xattn_vi_w, L0_xattn_vi_b, L0_xattn_o_w, L0_xattn_o_b, L0_xattn_nq_s, L0_xattn_nkt_s, L0_xattn_nki_s)
    x = x + jnp.tanh(g_ffn[0]) * _L0_ffn_ref(_layernorm(x, axis=-1), L0_ffn_gate_w, L0_ffn_wg, L0_ffn_wu, L0_ffn_wd)
    return x

_drawn_inputs = setup_inputs


def setup_inputs(seed=0):
    import zlib

    import numpy as np

    out = dict(_drawn_inputs(seed))
    spreads = {'L0_xattn_q_b': (0.0, 0.285),
     'L0_xattn_k_b': (0.0, 0.8),
     'L0_xattn_v_b': (0.0, 0.1),
     'L0_xattn_ki_b': (0.0, 0.8),
     'L0_xattn_vi_b': (0.0, 0.1),
     'L0_xattn_o_b': (0.0, 0.1),
     'L0_xattn_nq_s': (1.0, 0.2),
     'L0_xattn_nkt_s': (1.0, 0.2),
     'L0_xattn_nki_s': (1.0, 0.2)}
    factors = {'L0_ffn_gate_w': 8.0, 'L0_ffn_wg': 7.587, 'L0_ffn_wu': 7.521, 'L0_ffn_wd': 7.522}
    for name, (base, spread) in spreads.items():
        noise = np.random.default_rng([zlib.crc32(name.encode()), seed]).standard_normal(out[name].shape)
        drawn = base * np.exp(spread * noise) if base else spread * noise
        out[name] = jnp.asarray(drawn.astype(out[name].dtype))
    for name, factor in factors.items():
        out[name] = (out[name] * factor).astype(out[name].dtype)
    return out
```

```python
from contextlib import ExitStack

import concourse.bass as bass
from concourse import mybir

ALU = mybir.AluOpType
ACT = mybir.ActivationFunctionType
AX = mybir.AxisListType
F32 = mybir.dt.float32
BF16 = mybir.dt.bfloat16
U32 = mybir.dt.uint32

P = 128
B, S, DIM = 8, 112, 512
LCTX, N_IMG = 375, 257
N_TXT = LCTX - N_IMG
H, D = 16, 128
INNER = H * D
KT = DIM // P
CH = LCTX // 3
NREM = CH - N_TXT
HG = 4
NG = H // HG
E, TOPK, FF, CAP = 64, 8, 192, 128
FC = 96
FT = FF // FC
SLOTS = E * CAP
LN_EPS, RMS_EPS = 1e-5, 1e-6
VEC = 8
W_SLOTS = 3
NCHUNK = 4


def build(nc, x, ctx_in, g_xattn, g_ffn, q_w, q_b, k_w, k_b, v_w, v_b, ki_w, ki_b, vi_w, vi_b,
          o_w, o_b, nq_s, nkt_s, nki_s, gate_w, wg, wu, wd, out):
    with ExitStack() as top:
        build_in(nc, top, x, ctx_in, g_xattn, g_ffn, q_w, q_b, k_w, k_b, v_w, v_b, ki_w, ki_b,
                 vi_w, vi_b, o_w, o_b, nq_s, nkt_s, nki_s, gate_w, wg, wu, wd, out)


def after(eng, sem, value):
    if not isinstance(value, int) or value > 0:
        eng.wait_ge(sem, value)


def build_in(nc, top, x, ctx_in, g_xattn, g_ffn, q_w, q_b, k_w, k_b, v_w, v_b, ki_w, ki_b,
             vi_w, vi_b, o_w, o_b, nq_s, nkt_s, nki_s, gate_w, wg, wu, wd, out):
    def sem(name):
        return top.enter_context(nc.semaphore(name))

    def dram(name, shape, dt):
        return nc.dram_tensor(name, shape, dt, kind="Internal").ap()

    ctxT_d = dram("ctxT_d", [B, P, 2 * KT * LCTX], BF16)
    pt_d = dram("pt_d", [B * NG, P, HG * 6 * S], BF16)
    vrem_d = dram("vrem_d", [B, NREM, NG, 2 * 512], BF16)
    x2_d = dram("x2_d", [B, S, DIM], F32)
    idx_d = dram("idx_d", [B, S, TOPK], U32)
    w8_d = dram("w8_d", [B, S, TOPK], F32)
    xin_d = dram("xin_d", [SLOTS, 2 * DIM], BF16)
    y_d = dram("y_d", [SLOTS + 1, DIM], F32)

    def sb(stack, name, shape, dt):
        return stack.enter_context(nc.sbuf_tensor(name, shape, dt))

    ident = sb(top, "ident", [P, P], F32)
    identb = sb(top, "identb", [P, P], BF16)
    ones = sb(top, "ones", [P, P], F32)
    onesb = sb(top, "onesb", [S, S], BF16)
    trib = sb(top, "trib", [S, S], BF16)
    cols = sb(top, "cols", [P, VEC * H], F32)
    vecs_raw = sb(top, "vecs_raw", [P, P], F32)
    slot1 = sb(top, "slot1", [S, E], F32)
    eid_i = sb(top, "eid_i", [S, E], mybir.dt.int32)
    zeros = sb(top, "zeros", [P, 2 * DIM], BF16)
    mhalf = sb(top, "mhalf", [P, 4], F32)
    ln_eps = sb(top, "ln_eps", [P, 1], F32)
    tg = sb(top, "tg", [P, 2], F32)
    g_raw = sb(top, "g_raw", [P, 2], F32)

    s_const = sem("s_const")
    s_vecs_in = sem("s_vecs_in")
    s_vecs_turned = sem("s_vecs_turned")
    s_cols = sem("s_cols")
    s_g_in = sem("s_g_in")
    s_tanh = sem("s_tanh")
    s_zeroed = sem("s_zeroed")
    s_w_in = [sem(f"s_w_in{i}") for i in range(2)]
    s_w_hi = sem("s_w_hi")
    s_w_lo = sem("s_w_lo")
    s_ctx_in = sem("s_ctx_in")
    s_x_in = sem("s_x_in")
    s_ctx_turned = sem("s_ctx_turned")
    s_ctx_hi = sem("s_ctx_hi")
    s_ctx_lo = sem("s_ctx_lo")
    s_ctx_saved = sem("s_ctx_saved")
    s_ln_stats = sem("s_ln_stats")
    s_ln_aggr = sem("s_ln_aggr")
    s_ln_var = sem("s_ln_var")
    s_ln_rstd = sem("s_ln_rstd")
    s_xn = sem("s_xn")
    s_xn_turned = sem("s_xn_turned")
    s_xn_hi = sem("s_xn_hi")
    s_xn_lo = sem("s_xn_lo")
    s_k_made = sem("s_k_made")
    s_q_made = sem("s_q_made")
    s_k_out = sem("s_k_out")
    s_q_out = sem("s_q_out")
    s_kq_hi = sem("s_kq_hi")
    s_kq_split = sem("s_kq_split")
    s_square = sem("s_square")
    s_squared = sem("s_squared")
    s_sums = sem("s_sums")
    s_ms = sem("s_ms")
    s_rms = sem("s_rms")
    s_rdiag = sem("s_rdiag")
    s_rrow = sem("s_rrow")
    s_rrow_out = sem("s_rrow_out")
    s_s_made = sem("s_s_made")
    s_s_scaled = sem("s_s_scaled")
    s_nmax = sem("s_nmax")
    s_exp = sem("s_exp")
    s_rcp = sem("s_rcp")
    s_p = sem("s_p")
    s_p_turned = sem("s_p_turned")
    s_p_hi = sem("s_p_hi")
    s_p_lo = sem("s_p_lo")
    s_p_saved = [sem(f"s_p_saved{i}") for i in range(4)]

    with ExitStack() as mem:
        w_raw = [sb(mem, f"w_raw{i}", [P, INNER], F32) for i in range(2)]
        w_hi = [sb(mem, f"w_hi{i}", [P, KT, INNER], BF16) for i in range(W_SLOTS)]
        w_lo = [sb(mem, f"w_lo{i}", [P, KT, INNER], BF16) for i in range(W_SLOTS)]
        K_SLOT, KI_SLOT, Q_SLOT = 0, 1, 2
        V_SLOT, VI_SLOT, O_SLOT = 0, 1, 2
        with nc.Block() as block, ExitStack() as ph1, ExitStack() as ps1:
            ctx_raw = sb(ph1, "ctx_raw", [P, 3, DIM], F32)
            ctxT = sb(ph1, "ctxT", [P, 2, KT, LCTX], BF16)
            x_raw = sb(ph1, "x_raw", [S, DIM], F32)
            stats = sb(ph1, "stats", [S, 6], F32)
            mv = sb(ph1, "mv", [S, 2], F32)
            rstd = sb(ph1, "rstd", [S, 1], F32)
            xn = sb(ph1, "xn", [S, DIM], F32)
            xnT = sb(ph1, "xnT", [P, 2, KT, S], BF16)
            kT = sb(ph1, "kT", [P, H, 2, LCTX], BF16)
            qT = sb(ph1, "qT", [P, H, 2, S], BF16)
            RKQ = 2
            kq = sb(ph1, "kq", [P, RKQ, LCTX + S], F32)
            sq = sb(ph1, "sq", [P, LCTX + S], F32)
            sq_sum = sb(ph1, "sq_sum", [P, LCTX + S], F32)
            ms = sb(ph1, "ms", [P, 4], F32)
            rms = sb(ph1, "rms", [P, 4], F32)
            q_scale = sb(ph1, "q_scale", [S, 1], F32)
            rdiag = sb(ph1, "rdiag", [CH, 3, CH], F32)
            rrow = sb(ph1, "rrow", [S, LCTX], F32)
            RS = 4
            prob = sb(ph1, "prob", [S, RS, LCTX], F32)
            pause = sb(ph1, "pause", [1, 1], F32)
            mx = sb(ph1, "mx", [S, RS, 2], F32)
            nmx = sb(ph1, "nmx", [S, RS, 2], F32)
            psum_row = sb(ph1, "psum_row", [S, RS, 2], F32)
            rcp = sb(ph1, "rcp", [S, RS, 2], F32)
            ptb = sb(ph1, "ptb", [P, 4, 2, 3 * S], BF16)

            def pb(name, shape, dt=F32):
                return ps1.enter_context(nc.psum_tensor(name, shape, dt))

            pk = [pb(f"pk{i}", [P, 512]) for i in range(2)]
            pq = pb("pq", [P, 512])
            ps = [pb(f"ps{i}", [P, 512]) for i in range(2)]
            pt = [pb(f"pt{i}", [P, 512]) for i in range(2)]
            pm = pb("pm", [P, 512])

            w_order = [(k_w, K_SLOT), (ki_w, KI_SLOT), (q_w, Q_SLOT),
                       (v_w, V_SLOT), (vi_w, VI_SLOT), (o_w, O_SLOT)]

            def w_view(w):
                if w is o_w:
                    return w.rearrange("(c h d) n -> c d h n", c=NCHUNK, d=D)
                return w.rearrange("(c p) n -> c p n", p=P)

            def w_chunks(first, last):
                return [(n, w_order[n // NCHUNK][0], w_order[n // NCHUNK][1], n % NCHUNK)
                        for n in range(first, last)]

            def load_weights(sp, first, last):
                for n, w, slot, c in w_chunks(first, last):
                    after(sp, s_w_lo, n - 1)
                    dst = w_raw[n % 2][:, :]
                    if w is o_w:
                        dst = dst.rearrange("p (h n) -> p h n", h=H // NCHUNK)
                    sp.dma_start(dst, w_view(w)[c]).then_inc(s_w_in[n % 2], 16)

            def weights_hi(act, n, slot, c):
                act.wait_ge(s_w_in[n % 2], 16 * (n // 2 + 1))
                nc.scalar.copy(w_hi[slot][:, c, :], w_raw[n % 2][:, :]).then_inc(s_w_hi, 1)

            def weights_lo(dve, n, slot, c):
                dve.wait_ge(s_w_hi, n + 1)
                nc.vector.tensor_tensor(w_lo[slot][:, c, :], w_raw[n % 2][:, :], w_hi[slot][:, c, :],
                                        ALU.subtract).then_inc(s_w_lo, 1)

            def vec(v, h):
                return cols[:, v * H + h:v * H + h + 1]
            QB, KB, KIB, NQ, NKT, NKI, VB, VIB = range(VEC)

            def load_batch(sp, b):
                after(sp, s_ctx_turned, b * KT)
                sp.dma_start(ctx_raw[0:N_TXT, 0, :], ctx_in[b, N_IMG:LCTX, :]).then_inc(s_ctx_in, 16)
                sp.dma_start(ctx_raw[N_TXT:CH, 0, :], ctx_in[b, 2 * CH:N_IMG, :]).then_inc(s_ctx_in, 16)
                sp.dma_start(ctx_raw[0:CH, 1:3, :],
                             ctx_in[b, 0:2 * CH, :].rearrange("(c p) d -> p c d", p=CH)).then_inc(s_ctx_in, 16)
                after(sp, s_xn, b)
                sp.dma_start(x_raw[:, :], x[b]).then_inc(s_x_in, 16)

            def save_batch(sp, b):
                sp.wait_ge(s_ctx_lo, b * KT + KT)
                sp.dma_start(ctxT_d[b], ctxT[:, :, :, :].rearrange("p a k l -> p (a k l)")).then_inc(s_ctx_saved, 16)

            def save_prob(sp, b, h):
                    sp.wait_ge(s_p_lo, b * H + h + 1)
                    sp.dma_start(pt_d[b * NG + h // HG][:, (h % HG) * 6 * S:(h % HG + 1) * 6 * S],
                                 ptb[:, h % 4, :, :].rearrange("p a s -> p (a s)")).then_inc(s_p_saved[h % 4], 16)

            def save_probs(sp, b):
                for h in range(H):
                    save_prob(sp, b, h)

            @block.sync
            def _(sp):
                vectors = [q_b, k_b, ki_b, nq_s, nkt_s, nki_s, v_b, vi_b]
                for v, a in enumerate(vectors):
                    sp.dma_start(vecs_raw[v * H:(v + 1) * H, :], a.rearrange("(h d) -> h d", d=D)).then_inc(s_vecs_in, 16)
                for i, g in enumerate([g_xattn, g_ffn]):
                    sp.dma_start(g_raw[:, i:i + 1], g.rearrange("(a b) -> a b", a=1).broadcast_to([P, 1])).then_inc(s_g_in, 16)
                load_batch(sp, 0)
                load_weights(sp, 0, 3 * NCHUNK)
                save_batch(sp, 0)
                sp.wait_ge(s_const, 1)
                for i in range(8):
                    sp.dma_start(xin_d.rearrange("(g a p) n -> g p a n", g=8, p=P)[i],
                                 zeros[:, :].unsqueeze(1).broadcast_to([P, SLOTS // 8 // P, 2 * DIM])).then_inc(s_zeroed, 16)
                sp.dma_start(y_d[SLOTS:SLOTS + 1, :],
                             zeros[0:1, :].bitcast(F32)).then_inc(s_zeroed, 16)
                load_batch(sp, 1)
                with sp.Fori(1, B - 1) as b:
                    save_batch(sp, b)
                    load_batch(sp, b + 1)
                    save_probs(sp, b - 1)
                save_batch(sp, B - 1)
                save_probs(sp, B - 2)
                load_weights(sp, 3 * NCHUNK, 3 * NCHUNK + 2)
                for h in range(H):
                    if 3 * NCHUNK + 2 + h < 6 * NCHUNK:
                        load_weights(sp, 3 * NCHUNK + 2 + h, 3 * NCHUNK + 3 + h)
                    save_prob(sp, B - 1, h)
                sp.wait_ge(s_ctx_saved, 16 * B)
                sp.wait_ge(s_zeroed, 16 * 9)
                for i in range(4):
                    sp.wait_ge(s_p_saved[i], 16 * B * H // 4)

            @block.gpsimd
            def _(pool):
                nc.gpsimd.memset(zeros[:, :], 0.0).then_inc(s_const, 1)
                nc.gpsimd.memset(ident[:, :], 0.0).then_inc(s_const, 1)
                nc.gpsimd.memset(ones[:, :], 1.0).then_inc(s_const, 1)
                nc.gpsimd.memset(onesb[:, :], 1.0).then_inc(s_const, 1)
                nc.gpsimd.memset(ptb[:, :, :, :], 0.0).then_inc(s_const, 1)
                nc.gpsimd.memset(ms[:, :], 1.0).then_inc(s_const, 1)
                nc.gpsimd.memset(mhalf[:, :], -0.5)
                nc.gpsimd.memset(ln_eps[:, :], LN_EPS)
                pool.wait_ge(s_const, 6)
                nc.gpsimd.affine_select(out=ident[:, :], in_=ident[:, :], compare_op=ALU.not_equal, fill=1.0,
                                        base=0, pattern=[[-1, P]], channel_multiplier=1).then_inc(s_const, 1)
                nc.gpsimd.affine_select(out=trib[:, :], in_=onesb[:, :], compare_op=ALU.is_ge, fill=0.0,
                                        base=-1, pattern=[[1, S]], channel_multiplier=-1).then_inc(s_const, 1)
                nc.gpsimd.iota(eid_i[:, :], pattern=[[CAP, E]], base=1, channel_multiplier=0).then_inc(s_const, 1)
                pool.wait_ge(s_const, 9)
                nc.gpsimd.tensor_copy(identb[:, :], ident[:, :]).then_inc(s_const, 1)
                nc.gpsimd.tensor_copy(slot1[:, :], eid_i[:, :]).then_inc(s_const, 1)

                def ln_power(b):
                    pool.wait_ge(s_ln_aggr, b + 1)
                    nc.gpsimd.tensor_tensor(rstd[:, :], mv[:, 1:2], ln_eps[0:S, :], ALU.add).then_inc(s_ln_var, 1)
                    pool.wait_ge(s_ln_var, b + 1)
                    nc.gpsimd.tensor_tensor(rstd[:, :], rstd[:, :], mhalf[0:S, 0:1], ALU.pow).then_inc(s_ln_rstd, 1)

                def squares(b):
                    for h in range(H):
                        n = b * H + h
                        pool.wait_ge(s_k_out, n + 1)
                        pool.wait_ge(s_q_out, n + 1)
                        src = kq[:, h % RKQ, :]
                        if h == 0:
                            after(pool, s_sums, b)
                            nc.gpsimd.tensor_tensor(sq_sum[:, :], src, src, ALU.mult).then_inc(s_squared, 1)
                        else:
                            pool.wait_ge(s_squared, n)
                            nc.gpsimd.tensor_tensor(sq[:, :], src, src, ALU.mult).then_inc(s_square, 1)
                            pool.wait_ge(s_square, b * (H - 1) + h)
                            nc.gpsimd.tensor_tensor(sq_sum[:, :], sq_sum[:, :], sq[:, :], ALU.add).then_inc(s_squared, 1)
                    pool.wait_ge(s_ms, b + 1)
                    nc.gpsimd.tensor_tensor(rms[:, :], ms[:, :], mhalf[:, :], ALU.pow).then_inc(s_rms, 1)

                ln_power(0)
                squares(0)
                with pool.Fori(1, B) as b:
                    ln_power(b)
                    squares(b)

            def split_matmul(pe, dst, lhs, rhs, first, last):
                pe.matmul(dst, lhs[0], rhs[0], start=first, stop=False)
                pe.matmul(dst, lhs[0], rhs[1], start=False, stop=False)
                return pe.matmul(dst, lhs[1], rhs[0], start=False, stop=last)

            def turn_batch(pe, b):
                pe.wait_ge(s_ctx_in, 48 * b + 48)
                for k in range(KT):
                    if k < 2:
                        after(pe, s_k_out, b * H - 1 + k)
                    else:
                        pe.wait_ge(s_ctx_lo, b * KT + k - 1)
                    for c in range(3):
                        mm = pe.transpose(pk[k % 2][:, c * CH:(c + 1) * CH],
                                          ctx_raw[0:CH, c, k * P:(k + 1) * P], ident[0:CH, 0:CH])
                    mm.then_inc(s_ctx_turned, 1)
                pe.wait_ge(s_xn, b + 1)
                after(pe, s_q_out, b * H)
                for k in range(KT):
                    mm = pe.transpose(pq[:, k * S:(k + 1) * S], xn[:, k * P:(k + 1) * P], ident[0:S, 0:S])
                mm.then_inc(s_xn_turned, 1)

            def project_head(pe, b, h):
                n = b * H + h
                if h < 2:
                    pe.wait_ge(s_ctx_lo, b * KT + KT)
                else:
                    pe.wait_ge(s_k_out, n - 1)
                for slot, lo, hi in [(K_SLOT, 0, N_TXT), (KI_SLOT, N_TXT, LCTX)]:
                    for k in range(KT):
                        mm = split_matmul(pe, pk[h % 2][:, lo:hi],
                                          (w_hi[slot][:, k, h * D:(h + 1) * D], w_lo[slot][:, k, h * D:(h + 1) * D]),
                                          (ctxT[:, 0, k, lo:hi], ctxT[:, 1, k, lo:hi]), k == 0, k == KT - 1)
                mm.then_inc(s_k_made, 1)
                if h == 0:
                    pe.wait_ge(s_xn_lo, b + 1)
                else:
                    pe.wait_ge(s_q_out, n)
                for k in range(KT):
                    mm = split_matmul(pe, pq[:, 0:S],
                                      (w_hi[Q_SLOT][:, k, h * D:(h + 1) * D], w_lo[Q_SLOT][:, k, h * D:(h + 1) * D]),
                                      (xnT[:, 0, k, :], xnT[:, 1, k, :]), k == 0, k == KT - 1)
                mm.then_inc(s_q_made, 1)

            def score_head(pe, b, h):
                n = b * H + h
                pe.wait_ge(s_kq_split, n + 1)
                after(pe, s_s_scaled, n - 1)
                mm = split_matmul(pe, ps[h % 2][0:S, 0:LCTX], (qT[:, h, 0, :], qT[:, h, 1, :]),
                                  (kT[:, h, 0, :], kT[:, h, 1, :]), True, True)
                mm.then_inc(s_s_made, 1)

            def turn_probs(pe, b, h):
                n = b * H + h
                pe.wait_ge(s_p, n + 1)
                after(pe, s_p_lo, n - 1)
                for c in range(3):
                    mm = pe.transpose(pt[h % 2][0:CH, c * S:(c + 1) * S],
                                      prob[:, h % RS, c * CH:(c + 1) * CH], ident[0:S, 0:S])
                mm.then_inc(s_p_turned, 1)

            def sum_squares(pe, b):
                pe.wait_ge(s_squared, (b + 1) * H)
                after(pe, s_rrow_out, b)
                for c in range(3):
                    pe.matmul(pm[0:CH, c:c + 1], sq_sum[:, c * CH:(c + 1) * CH], ones[:, 0:1], start=True, stop=True)
                pe.matmul(pm[0:S, 3:4], sq_sum[:, LCTX:LCTX + S], ones[:, 0:1], start=True, stop=True).then_inc(s_sums, 1)

            def key_row(pe, b):
                pe.wait_ge(s_rdiag, b + 1)
                pe.matmul(pm[0:S, 0:LCTX], ones[0:CH, 0:S], rdiag[:, :, :].rearrange("p c l -> p (c l)"),
                          start=True, stop=True).then_inc(s_rrow, 1)

            LAG = 2

            def pe_batch(pe, b, project, score):
                if project:
                    turn_batch(pe, b)
                if score:
                    key_row(pe, b - 1)
                for h in range(H + LAG):
                    if score and h < H:
                        score_head(pe, b - 1, h)
                    if project and h < H:
                        project_head(pe, b, h)
                    if score and h >= LAG:
                        turn_probs(pe, b - 1, h - LAG)
                if project:
                    sum_squares(pe, b)

            @block.tensor
            def _(pe):
                pe.wait_ge(s_const, 7)
                pe.wait_ge(s_vecs_in, 16 * VEC)
                pe.transpose(pm[:, 0:P], vecs_raw[:, :], ident[:, :]).then_inc(s_vecs_turned, 1)
                pe.wait_ge(s_cols, 1)
                pe.wait_ge(s_w_lo, 3 * NCHUNK)
                pe_batch(pe, 0, True, False)
                pe_batch(pe, 1, True, True)
                with pe.Fori(2, B) as b:
                    pe_batch(pe, b, True, True)
                pe_batch(pe, B, False, True)

            def act_turned(act, b):
                for k in range(KT):
                    act.wait_ge(s_ctx_turned, b * KT + k + 1)
                    if k == 0:
                        after(act, s_ctx_saved, 16 * b)
                    nc.scalar.copy(ctxT[:, 0, k, :], pk[k % 2][:, 0:LCTX]).then_inc(s_ctx_hi, 1)
                act.wait_ge(s_xn_turned, b + 1)
                nc.scalar.copy(xnT[:, 0, :, :].rearrange("p k s -> p (k s)"), pq[:, 0:KT * S]).then_inc(s_xn_hi, 1)

            def act_project(act, b, h):
                n = b * H + h
                act.wait_ge(s_k_made, n + 1)
                after(act, s_kq_split, n - RKQ + 1)
                after(act, s_squared, n - RKQ + 1)
                nc.scalar.activation(kq[:, h % RKQ, 0:N_TXT], pk[h % 2][:, 0:N_TXT], ACT.Identity, bias=vec(KB, h))
                nc.scalar.activation(kq[:, h % RKQ, N_TXT:LCTX], pk[h % 2][:, N_TXT:LCTX], ACT.Identity,
                                     bias=vec(KIB, h)).then_inc(s_k_out, 1)
                act.wait_ge(s_q_made, n + 1)
                nc.scalar.activation(kq[:, h % RKQ, LCTX:LCTX + S], pq[:, 0:S], ACT.Identity,
                                     bias=vec(QB, h)).then_inc(s_q_out, 1)

            def act_exp(act, b, h):
                n = b * H + h
                act.wait_ge(s_nmax, n + 1)
                r = h % RS
                nc.scalar.activation(prob[:, r, 0:N_TXT], prob[:, r, 0:N_TXT], ACT.Exp, bias=nmx[:, r, 0:1],
                                     scale=q_scale[:, 0:1], accum_out=psum_row[:, r, 0:1])
                nc.scalar.activation(prob[:, r, N_TXT:LCTX], prob[:, r, N_TXT:LCTX], ACT.Exp, bias=nmx[:, r, 1:2],
                                     scale=q_scale[:, 0:1], accum_out=psum_row[:, r, 1:2]).then_inc(s_exp, 1)

            def act_probs_hi(act, b, h):
                n = b * H + h
                act.wait_ge(s_p_turned, n + 1)
                after(act, s_p_saved[h % 4], 16 * (b * (H // 4) + h // 4))
                nc.scalar.copy(ptb[0:CH, h % 4, 0, :], pt[h % 2][0:CH, 0:3 * S]).then_inc(s_p_hi, 1)

            def act_batch(act, b, project, score, extra=None):
                if project:
                    act_turned(act, b)
                if score:
                    act.wait_ge(s_rrow, b)
                    nc.scalar.copy(rrow[:, :], pm[0:S, 0:LCTX]).then_inc(s_rrow_out, 1)
                for h in range(H + LAG):
                    if project and h < H:
                        act_project(act, b, h)
                    if score and h < H:
                        act_exp(act, b - 1, h)
                    if score and h >= LAG:
                        act_probs_hi(act, b - 1, h - LAG)
                    if extra and h < len(extra):
                        weights_hi(act, *extra[h])

            chunks1 = [(n, slot, c) for n, _, slot, c in w_chunks(0, 3 * NCHUNK)]
            chunks2 = [(n, slot, c) for n, _, slot, c in w_chunks(3 * NCHUNK, 6 * NCHUNK)]

            @block.scalar
            def _(act):
                act.wait_ge(s_g_in, 32)
                nc.scalar.activation(tg[:, :], g_raw[:, :], ACT.Tanh).then_inc(s_tanh, 1)
                act.wait_ge(s_vecs_turned, 1)
                nc.scalar.copy(cols[:, :], pm[:, 0:P]).then_inc(s_cols, 1)
                act.wait_ge(s_cols, 1)
                for c in chunks1:
                    weights_hi(act, *c)
                act_batch(act, 0, True, False)
                act_batch(act, 1, True, True)
                with act.Fori(2, B) as b:
                    act_batch(act, b, True, True)
                act_batch(act, B, False, True, chunks2)

            def dve_norms(dve, b):
                dve.wait_ge(s_sums, b + 1)
                nc.vector.tensor_scalar(ms[0:CH, 0:3], pm[0:CH, 0:3], 1.0 / INNER, RMS_EPS, ALU.mult, ALU.add)
                nc.vector.tensor_scalar(ms[0:S, 3:4], pm[0:S, 3:4], 1.0 / INNER, RMS_EPS, ALU.mult, ALU.add).then_inc(s_ms, 1)
                dve.wait_ge(s_rms, b + 1)
                for c in range(3):
                    nc.vector.tensor_scalar(rdiag[:, c, :], ident[0:CH, 0:CH], rms[0:CH, c:c + 1], None,
                                            ALU.mult)
                nc.vector.tensor_scalar(q_scale[:, :], rms[0:S, 3:4], float(D) ** -0.5, None,
                                        ALU.mult).then_inc(s_rdiag, 1)

            def dve_turned(dve, b):
                dve.wait_ge(s_x_in, 16 * b + 16)
                nc.vector.bn_stats(stats[:, :], x_raw[:, :]).then_inc(s_ln_stats, 1)
                dve.wait_ge(s_ln_stats, b + 1)
                nc.vector.memset(pause[:, :], 0.0)
                nc.vector.bn_aggr(mv[:, :], stats[:, :]).then_inc(s_ln_aggr, 1)
                dve.wait_ge(s_ln_rstd, b + 1)
                after(dve, s_xn_turned, b)
                nc.vector.tensor_scalar(xn[:, :], x_raw[:, :], mv[:, 0:1], rstd[:, 0:1], ALU.subtract,
                                        ALU.mult).then_inc(s_xn, 1)
                for k in range(KT):
                    dve.wait_ge(s_ctx_hi, b * KT + k + 1)
                    nc.vector.tensor_tensor(ctxT[:, 1, k, :], pk[k % 2][:, 0:LCTX], ctxT[:, 0, k, :],
                                            ALU.subtract).then_inc(s_ctx_lo, 1)
                dve.wait_ge(s_xn_hi, b + 1)
                nc.vector.tensor_tensor(xnT[:, 1, :, :].rearrange("p k s -> p (k s)"), pq[:, 0:KT * S],
                                        xnT[:, 0, :, :].rearrange("p k s -> p (k s)"),
                                        ALU.subtract).then_inc(s_xn_lo, 1)

            def dve_scale(dve, b, h):
                n = b * H + h
                r = h % RS
                dve.wait_ge(s_s_made, n + 1)
                after(dve, s_p_turned, n - RS + 1)
                nc.vector.memset(pause[:, :], 0.0)
                nc.vector.tensor_tensor_reduce(out=prob[:, r, 0:N_TXT], in0=ps[h % 2][0:S, 0:N_TXT],
                                               in1=rrow[:, 0:N_TXT], scale=1.0, scalar=-3.0e38, op0=ALU.mult,
                                               op1=ALU.max, accum_out=mx[:, r, 0:1])
                nc.vector.tensor_tensor_reduce(out=prob[:, r, N_TXT:LCTX], in0=ps[h % 2][0:S, N_TXT:LCTX],
                                               in1=rrow[:, N_TXT:LCTX], scale=1.0, scalar=-3.0e38, op0=ALU.mult,
                                               op1=ALU.max, accum_out=mx[:, r, 1:2]).then_inc(s_s_scaled, 1)
                dve.wait_ge(s_s_scaled, n + 1)
                nc.vector.tensor_scalar(nmx[:, r, :], mx[:, r, :], q_scale[:, 0:1], -1.0, ALU.mult,
                                        ALU.mult).then_inc(s_nmax, 1)

            def dve_split(dve, b, h, scores):
                n = b * H + h
                dve.wait_ge(s_k_out, n + 1)
                dve.wait_ge(s_q_out, n + 1)
                if scores:
                    dve.wait_ge(s_s_made, n - H + 1)
                src = kq[:, h % RKQ, :]
                parts = [(kT[:, h, :, 0:N_TXT], src[:, 0:N_TXT], vec(NKT, h)),
                         (kT[:, h, :, N_TXT:LCTX], src[:, N_TXT:LCTX], vec(NKI, h)),
                         (qT[:, h, :, :], src[:, LCTX:LCTX + S], vec(NQ, h))]
                for dst, v, scale in parts:
                    last = nc.vector.tensor_scalar(dst[:, 0, :], v, scale, None, ALU.mult)
                last.then_inc(s_kq_hi, 1)
                dve.wait_ge(s_kq_hi, n + 1)
                for dst, v, scale in parts:
                    last = nc.vector.scalar_tensor_tensor(dst[:, 1, :], v, scale, dst[:, 0, :], ALU.mult,
                                                          ALU.subtract)
                last.then_inc(s_kq_split, 1)

            def dve_normalise(dve, b, h):
                n = b * H + h
                r = h % RS
                dve.wait_ge(s_exp, n + 1)
                nc.vector.reciprocal(rcp[:, r, :], psum_row[:, r, :]).then_inc(s_rcp, 1)
                dve.wait_ge(s_rcp, n + 1)
                nc.vector.tensor_scalar(prob[:, r, 0:N_TXT], prob[:, r, 0:N_TXT], rcp[:, r, 0:1], None, ALU.mult)
                nc.vector.tensor_scalar(prob[:, r, N_TXT:LCTX], prob[:, r, N_TXT:LCTX], rcp[:, r, 1:2], None,
                                        ALU.mult).then_inc(s_p, 1)

            def dve_probs_lo(dve, b, h):
                n = b * H + h
                dve.wait_ge(s_p_hi, n + 1)
                nc.vector.tensor_tensor(ptb[0:CH, h % 4, 1, :], pt[h % 2][0:CH, 0:3 * S], ptb[0:CH, h % 4, 0, :],
                                        ALU.subtract).then_inc(s_p_lo, 1)

            def dve_batch(dve, b, project, score, extra=None):
                if project:
                    dve_turned(dve, b)
                if score:
                    dve.wait_ge(s_rrow_out, b)
                for h in range(H + LAG):
                    if score and h < H:
                        dve_scale(dve, b - 1, h)
                    if project and h < H:
                        dve_split(dve, b, h, score)
                    if score and 1 <= h <= H:
                        dve_normalise(dve, b - 1, h - 1)
                    if score and h >= LAG:
                        dve_probs_lo(dve, b - 1, h - LAG)
                    if extra and h < len(extra):
                        weights_lo(dve, *extra[h])
                if project:
                    dve_norms(dve, b)

            @block.vector
            def _(dve):
                for c in chunks1:
                    weights_lo(dve, *c)
                dve.wait_ge(s_cols, 1)
                dve.wait_ge(s_const, 7)
                dve_batch(dve, 0, True, False)
                dve_batch(dve, 1, True, True)
                with dve.Fori(2, B) as b:
                    dve_batch(dve, b, True, True)
                dve_batch(dve, B, False, True, chunks2)


        s2 = {}

        def sem2(name):
            s2[name] = sem(name)
            return s2[name]
        s_rem_in = sem2("s_rem_in")
        s_rem_turned = sem2("s_rem_turned")
        s_rem_hi = sem2("s_rem_hi")
        s_rem_lo = sem2("s_rem_lo")
        s_vrem_made = sem2("s_vrem_made")
        s_vrem_hi = sem2("s_vrem_hi")
        s_vrem_lo = sem2("s_vrem_lo")
        s_vrem_saved = sem2("s_vrem_saved")
        s_gw_in = sem2("s_gw_in")
        s_gw_turned = sem2("s_gw_turned")
        s_gwT = sem2("s_gwT")
        s_vb_rep = sem2("s_vb_rep")
        s_ob_made = sem2("s_ob_made")
        s_ob_in = sem2("s_ob_in")
        s_ob_sum = sem2("s_ob_sum")
        s_obrow = sem2("s_obrow")
        s_ctxT_in = sem2("s_ctxT_in")
        s_p_in = [sem2(f"s_p_in{i}") for i in range(2)]
        s_vrem_in = [sem2(f"s_vrem_in{i}") for i in range(2)]
        s_v_made = sem2("s_v_made")
        s_v_hi = sem2("s_v_hi")
        s_v_lo = sem2("s_v_lo")
        s_att = sem2("s_att")
        s_att_hi = sem2("s_att_hi")
        s_att_lo = sem2("s_att_lo")
        s_o_made = sem2("s_o_made")
        s_xr_in = sem2("s_xr_in")
        s_xr = sem2("s_xr")
        s_x2 = sem2("s_x2")
        s_x2_saved = sem2("s_x2_saved")
        s_x2_stats = sem2("s_x2_stats")
        s_x2_aggr = sem2("s_x2_aggr")
        s_x2_var = sem2("s_x2_var")
        s_x2_rstd = sem2("s_x2_rstd")
        s_xn2 = sem2("s_xn2")
        s_xd_hi = sem2("s_xd_hi")
        s_xd = sem2("s_xd")
        s_xn2_turned = sem2("s_xn2_turned")
        s_xn2T = sem2("s_xn2T")
        s_logits = sem2("s_logits")
        s_lmax = sem2("s_lmax")
        s_lnmax = sem2("s_lnmax")
        s_lexp = sem2("s_lexp")
        s_route = sem2("s_route")
        s_sel = sem2("s_sel")
        s_pos = sem2("s_pos")
        s_idx = sem2("s_idx")
        s_idx_saved = sem2("s_idx_saved")
        s_dispatched = sem2("s_dispatched")
        ROUTE_STEPS = 14

        with nc.Block() as block, ExitStack() as ph2, ExitStack() as ps2:
            ctxT = sb(ph2, "ctxT2", [P, 2, KT, LCTX], BF16)
            rem_raw = sb(ph2, "rem_raw", [B * NREM, DIM], F32)
            remT = sb(ph2, "remT", [P, 2, KT * B * NREM], BF16)
            vrem = sb(ph2, "vrem", [B * NREM, NG, 2, 512], BF16)
            gw_raw = sb(ph2, "gw_raw", [E, DIM], F32)
            gwT = sb(ph2, "gwT", [P, KT, E], F32)
            vb_rep = sb(ph2, "vb_rep", [P, 2, H, S], BF16)
            vb_sum = sb(ph2, "vb_sum", [P, H], F32)
            obrow = sb(ph2, "obrow", [S, DIM], F32)
            v_sb = sb(ph2, "v_sb", [CH, 2, 3, 2, 512], BF16)
            pin = sb(ph2, "pin", [P, 2, HG, 2, 3 * S], BF16)
            outT = sb(ph2, "outT", [P, H, 2, S], BF16)
            xr_in = sb(ph2, "xr_in", [S, DIM], F32)
            xr = sb(ph2, "xr", [S, DIM], F32)
            x2 = sb(ph2, "x2", [S, DIM], F32)
            stats2 = sb(ph2, "stats2", [S, 6], F32)
            mv2 = sb(ph2, "mv2", [S, 2], F32)
            rstd2 = sb(ph2, "rstd2", [S, 1], F32)
            xn2 = sb(ph2, "xn2", [S, DIM], F32)
            xd = sb(ph2, "xd", [S, 2, KT, P], BF16)
            xn2T = sb(ph2, "xn2T", [P, KT * S], F32)
            lmax = sb(ph2, "lmax", [S, 2], F32)
            ex = sb(ph2, "ex", [S, E], F32)
            top8 = sb(ph2, "top8", [S, TOPK], F32)
            left = sb(ph2, "left", [S, E], F32)
            selb = sb(ph2, "selb", [S, E], BF16)
            cumb = sb(ph2, "cumb", [S, E], BF16)
            wsum = sb(ph2, "wsum", [S, 3], F32)
            slot = sb(ph2, "slot", [S, E], F32)
            val = sb(ph2, "val", [S, E], F32)
            key = sb(ph2, "key", [S, E], F32)
            wsel = sb(ph2, "wsel", [S, E], F32)
            key8 = sb(ph2, "key8", [S, TOPK], F32)
            match = sb(ph2, "match", [S, E], F32)
            none8 = sb(ph2, "none8", [S, TOPK], F32)
            w8 = sb(ph2, "w8", [S, TOPK], F32)
            idx = sb(ph2, "idx", [S, TOPK], U32)
            pause = sb(ph2, "pause2", [1, 1], F32)
            pool_pause = sb(ph2, "pool_pause", [1, 2], F32)

            def pb2(name, shape, dt=F32):
                return ps2.enter_context(nc.psum_tensor(name, shape, dt))
            pv = [pb2(f"pv{i}", [P, 512]) for i in range(2)]
            pa = [pb2(f"pa{i}", [P, 512]) for i in range(2)]
            po = pb2("po", [P, 512])
            pg = pb2("pg", [P, 512])
            pl = pb2("pl", [P, 512])
            pp = pb2("pp", [P, 512])
            NR = B * NREM

            def load_group(sp, b, g):
                n = b * NG + g
                after(sp, s_att, n - 1)
                sp.dma_start(pin[:, g % 2, :, :, :].rearrange("p h a s -> p (h a s)"), pt_d[n]).then_inc(s_p_in[g % 2], 16)
                sp.dma_start(v_sb[N_TXT:CH, g % 2, 0, :, :].rearrange("p a n -> p (a n)"),
                             vrem_d[b, :, g, :]).then_inc(s_vrem_in[g % 2], 16)

            def load_values(sp, b):
                after(sp, s_v_made, 12 * b)
                sp.dma_start(ctxT[:, :, :, :].rearrange("p a k l -> p (a k l)"), ctxT_d[b]).then_inc(s_ctxT_in, 16)

            def save_route(sp, b):
                sp.wait_ge(s_x2, b + 1)
                sp.dma_start(x2_d[b], x2[:, :]).then_inc(s_x2_saved, 16)
                after(sp, s_xr, b)
                sp.wait_ge(s_idx, b + 1)
                sp.dma_start(idx_d[b], idx[:, :]).then_inc(s_idx_saved, 16)
                sp.dma_start(w8_d[b], w8[:, :]).then_inc(s_idx_saved, 16)

            def load_x(sp, b):
                after(sp, s_xr, b)
                sp.dma_start(xr_in[:, :], x[b]).then_inc(s_xr_in, 16)

            def sp_batch(sp, b, values, route):
                if values:
                    load_values(sp, b)
                    load_group(sp, b, 0)
                    load_group(sp, b, 1)
                if route:
                    load_x(sp, b - 1)
                if values:
                    load_group(sp, b, 2)
                    load_group(sp, b, 3)
                if route:
                    save_route(sp, b - 1)

            @block.sync
            def _(sp):
                for b in range(B):
                    sp.dma_start(rem_raw[b * NREM:(b + 1) * NREM, :], ctx_in[b, 2 * CH:N_IMG, :]).then_inc(s_rem_in, 16)
                sp.dma_start(gw_raw[:, :], gate_w).then_inc(s_gw_in, 16)
                sp.dma_start(obrow[:, :], o_b.rearrange("(a n) -> a n", a=1).broadcast_to([S, DIM])).then_inc(s_ob_in, 16)
                sp.wait_ge(s_vrem_lo, NG)
                sp.dma_start(vrem_d.rearrange("b r g n -> (b r) (g n)"),
                             vrem[:, :, :, :].rearrange("p g a n -> p (g a n)")).then_inc(s_vrem_saved, 16)
                sp.wait_ge(s_vrem_saved, 16)
                sp_batch(sp, 0, True, False)
                sp_batch(sp, 1, True, True)
                with sp.Fori(2, B) as b:
                    sp_batch(sp, b, True, True)
                sp_batch(sp, B, False, True)
                sp.wait_ge(s_x2_saved, 16 * B)
                sp.wait_ge(s_idx_saved, 32 * B)

            def project_values(pe, b, g):
                for c in range(3):
                    n = 3 * (b * NG + g) + c
                    rows = N_TXT if c == 0 else CH
                    w = V_SLOT if c == 0 else VI_SLOT
                    after(pe, s_v_lo, n - 1)
                    for k in range(KT):
                        mm = split_matmul(pe, pv[(3 * g + c) % 2][0:rows, :],
                                          (ctxT[:, 0, k, c * CH:c * CH + rows], ctxT[:, 1, k, c * CH:c * CH + rows]),
                                          (w_hi[w][:, k, g * 512:(g + 1) * 512], w_lo[w][:, k, g * 512:(g + 1) * 512]),
                                          k == 0, k == KT - 1)
                    mm.then_inc(s_v_made, 1)

            def attend(pe, b, g):
                n = b * NG + g
                pe.wait_ge(s_v_lo, 3 * n + 3)
                pe.wait_ge(s_p_in[g % 2], 16 * (b * (NG // 2) + g // 2 + 1))
                pe.wait_ge(s_vrem_in[g % 2], 16 * (b * (NG // 2) + g // 2 + 1))
                after(pe, s_att_lo, n - 1)
                for hh in range(HG):
                    for c in range(3):
                        mm = split_matmul(pe, pa[g % 2][:, hh * S:(hh + 1) * S],
                                          (v_sb[:, g % 2, c, 0, hh * D:(hh + 1) * D],
                                           v_sb[:, g % 2, c, 1, hh * D:(hh + 1) * D]),
                                          (pin[0:CH, g % 2, hh, 0, c * S:(c + 1) * S],
                                           pin[0:CH, g % 2, hh, 1, c * S:(c + 1) * S]), c == 0, c == 2)
                mm.then_inc(s_att, 1)

            def project_out(pe, b):
                pe.wait_ge(s_att_lo, NG * b + NG)
                after(pe, s_x2, b)
                for h in range(H):
                    mm = split_matmul(pe, po[0:S, :], (outT[:, h, 0, :], outT[:, h, 1, :]),
                                      (w_hi[O_SLOT][:, h // HG, (h % HG) * 512:(h % HG + 1) * 512],
                                       w_lo[O_SLOT][:, h // HG, (h % HG) * 512:(h % HG + 1) * 512]), h == 0, h == H - 1)
                mm.then_inc(s_o_made, 1)

            def turn_route(pe, b):
                pe.wait_ge(s_xn2, b + 1)
                after(pe, s_xn2T, b)
                for k in range(KT):
                    mm = pe.transpose(pg[:, k * S:(k + 1) * S], xn2[:, k * P:(k + 1) * P], ident[0:S, 0:S])
                mm.then_inc(s_xn2_turned, 1)

            def make_logits(pe, b):
                pe.wait_ge(s_xn2T, b + 1)
                after(pe, s_lexp, b)
                for k in range(KT):
                    mm = pe.matmul(pl[0:S, 0:E], xn2T[:, k * S:(k + 1) * S], gwT[:, k, :], start=k == 0,
                                   stop=k == KT - 1)
                mm.then_inc(s_logits, 1)

            def make_positions(pe, b):
                pe.wait_ge(s_sel, b + 1)
                pe.matmul(pp[0:S, 0:E], trib[:, :], selb[:, :], start=True, stop=False)
                pe.matmul(pp[0:S, 0:E], onesb[:, :], cumb[:, :], start=False, stop=True).then_inc(s_pos, 1)

            def pe_batch2(pe, b, values, route):
                if values:
                    pe.wait_ge(s_ctxT_in, 16 * b + 16)
                    project_values(pe, b, 0)
                if route:
                    project_out(pe, b - 1)
                if values:
                    project_values(pe, b, 1)
                    attend(pe, b, 0)
                if route:
                    turn_route(pe, b - 1)
                if values:
                    project_values(pe, b, 2)
                if route:
                    make_logits(pe, b - 1)
                if values:
                    attend(pe, b, 1)
                    project_values(pe, b, 3)
                if route:
                    make_positions(pe, b - 1)
                if values:
                    attend(pe, b, 2)
                    attend(pe, b, 3)

            @block.tensor
            def _(pe):
                pe.wait_ge(s_rem_in, 16 * B)
                for k in range(KT):
                    mm = pe.transpose(pg[:, k * NR:(k + 1) * NR], rem_raw[:, k * P:(k + 1) * P], ident[0:NR, 0:NR])
                mm.then_inc(s_rem_turned, 1)
                pe.wait_ge(s_gw_in, 16)
                for k in range(KT):
                    mm = pe.transpose(pl[:, k * E:(k + 1) * E], gw_raw[:, k * P:(k + 1) * P], ident[0:E, 0:E])
                mm.then_inc(s_gw_turned, 1)
                pe.wait_ge(s_rem_lo, 1)
                for g in range(NG):
                    after(pe, s_vrem_lo, g - 1)
                    for k in range(KT):
                        mm = split_matmul(pe, pv[g % 2][0:NR, :],
                                          (remT[:, 0, k * NR:(k + 1) * NR], remT[:, 1, k * NR:(k + 1) * NR]),
                                          (w_hi[VI_SLOT][:, k, g * 512:(g + 1) * 512],
                                           w_lo[VI_SLOT][:, k, g * 512:(g + 1) * 512]), k == 0, k == KT - 1)
                    mm.then_inc(s_vrem_made, 1)
                pe.wait_ge(s_vb_rep, 1)
                for h in range(H):
                    mm = split_matmul(pe, po[0:S, :], (vb_rep[:, 0, h, :], vb_rep[:, 1, h, :]),
                                      (w_hi[O_SLOT][:, h // HG, (h % HG) * 512:(h % HG + 1) * 512],
                                       w_lo[O_SLOT][:, h // HG, (h % HG) * 512:(h % HG + 1) * 512]), h == 0, h == H - 1)
                mm.then_inc(s_ob_made, 1)
                pe.wait_ge(s_vrem_lo, NG)
                pe.wait_ge(s_gwT, 1)
                pe.wait_ge(s_obrow, 1)
                pe_batch2(pe, 0, True, False)
                pe_batch2(pe, 1, True, True)
                with pe.Fori(2, B) as b:
                    pe_batch2(pe, b, True, True)
                pe_batch2(pe, B, False, True)

            def act_values(act, b, g):
                for c in range(3):
                    n = 3 * (b * NG + g) + c
                    rows = N_TXT if c == 0 else CH
                    act.wait_ge(s_v_made, n + 1)
                    nc.scalar.copy(v_sb[0:rows, g % 2, c, 0, :], pv[(3 * g + c) % 2][0:rows, :]).then_inc(s_v_hi, 1)

            def act_attend(act, b, g):
                act.wait_ge(s_att, b * NG + g + 1)
                nc.scalar.copy(outT[:, g * HG:(g + 1) * HG, 0, :],
                               pa[g % 2][:, 0:HG * S].rearrange("p (h s) -> p h s", h=HG)).then_inc(s_att_hi, 1)

            def act_batch2(act, b, values, route):
                if values:
                    act_values(act, b, 0)
                    act_values(act, b, 1)
                    act_attend(act, b, 0)
                if route:
                    act.wait_ge(s_xn2_turned, b)
                    nc.scalar.copy(xn2T[:, :], pg[:, 0:KT * S]).then_inc(s_xn2T, 1)
                if values:
                    act_values(act, b, 2)
                if route:
                    act.wait_ge(s_lnmax, b)
                    nc.scalar.activation(ex[:, :], pl[0:S, 0:E], ACT.Exp, bias=lmax[:, 1:2]).then_inc(s_lexp, 1)
                if values:
                    act_attend(act, b, 1)
                    act_values(act, b, 3)
                    act_attend(act, b, 2)
                    act_attend(act, b, 3)

            @block.scalar
            def _(act):
                act.wait_ge(s_rem_turned, 1)
                nc.scalar.copy(remT[:, 0, :], pg[:, 0:KT * NR]).then_inc(s_rem_hi, 1)
                act.wait_ge(s_gw_turned, 1)
                nc.scalar.copy(gwT[:, :, :].rearrange("p k e -> p (k e)"), pl[:, 0:KT * E]).then_inc(s_gwT, 1)
                for g in range(NG):
                    act.wait_ge(s_vrem_made, g + 1)
                    nc.scalar.copy(vrem[:, g, 0, :], pv[g % 2][0:NR, :]).then_inc(s_vrem_hi, 1)
                act_batch2(act, 0, True, False)
                act_batch2(act, 1, True, True)
                with act.Fori(2, B) as b:
                    act_batch2(act, b, True, True)
                act_batch2(act, B, False, True)

            def dve_values(dve, b, g):
                for c in range(3):
                    n = 3 * (b * NG + g) + c
                    rows = N_TXT if c == 0 else CH
                    dve.wait_ge(s_v_hi, n + 1)
                    nc.vector.tensor_tensor(v_sb[0:rows, g % 2, c, 1, :], pv[(3 * g + c) % 2][0:rows, :],
                                            v_sb[0:rows, g % 2, c, 0, :], ALU.subtract).then_inc(s_v_lo, 1)

            def dve_attend(dve, b, g):
                dve.wait_ge(s_att_hi, b * NG + g + 1)
                nc.vector.tensor_tensor(outT[:, g * HG:(g + 1) * HG, 1, :],
                                        pa[g % 2][:, 0:HG * S].rearrange("p (h s) -> p h s", h=HG),
                                        outT[:, g * HG:(g + 1) * HG, 0, :], ALU.subtract).then_inc(s_att_lo, 1)

            def dve_residual(dve, b):
                dve.wait_ge(s_o_made, b + 1)
                dve.wait_ge(s_xr, b + 1)
                after(dve, s_x2_saved, 16 * b)
                nc.vector.scalar_tensor_tensor(x2[:, :], po[0:S, :], tg[0:S, 0:1], xr[:, :], ALU.mult,
                                               ALU.add).then_inc(s_x2, 1)
                dve.wait_ge(s_x2, b + 1)
                nc.vector.bn_stats(stats2[:, :], x2[:, :]).then_inc(s_x2_stats, 1)
                dve.wait_ge(s_x2_stats, b + 1)
                nc.vector.memset(pause[:, :], 0.0)
                nc.vector.bn_aggr(mv2[:, :], stats2[:, :]).then_inc(s_x2_aggr, 1)

            def dve_normalise2(dve, b):
                dve.wait_ge(s_x2_rstd, b + 1)
                after(dve, s_xn2_turned, b)
                nc.vector.tensor_scalar(xn2[:, :], x2[:, :], mv2[:, 0:1], rstd2[:, 0:1], ALU.subtract,
                                        ALU.mult).then_inc(s_xn2, 1)
                dve.wait_ge(s_xn2, b + 1)
                after(dve, s_dispatched, 16 * TOPK * b)
                by_tile = xn2[:, :].rearrange("s (p c) -> s c p", c=KT)
                nc.vector.tensor_copy(xd[:, 0, :, :], by_tile).then_inc(s_xd_hi, 1)
                dve.wait_ge(s_xd_hi, b + 1)
                nc.vector.tensor_tensor(xd[:, 1, :, :], by_tile, xd[:, 0, :, :], ALU.subtract).then_inc(s_xd, 1)

            def dve_select(dve, b):
                dve.wait_ge(s_logits, b + 1)
                nc.vector.tensor_reduce(lmax[:, 0:1], pl[0:S, 0:E], AX.X, ALU.max).then_inc(s_lmax, 1)
                dve.wait_ge(s_lmax, b + 1)
                nc.vector.tensor_scalar(lmax[:, 1:2], lmax[:, 0:1], -1.0, None, ALU.mult).then_inc(s_lnmax, 1)

            def dve_choose(dve, b, link):
                dve.wait_ge(s_lexp, b + 1)
                nc.vector.memset(pause[:, :], 0.0)
                link(nc.vector.max(top8[:, :], ex[:, :]))
                nc.vector.memset(pause[:, :], 0.0)
                link(nc.vector.match_replace(left[:, :], top8[:, :], ex[:, :], -1.0))
                nc.vector.tensor_reduce(wsum[:, 0:1], top8[:, :], AX.X, ALU.add)
                if not (isinstance(b, int) and b == 0):
                    dve.wait_ge(s_pos, b)
                    link(nc.vector.tensor_tensor(cumb[:, :], cumb[:, :], selb[:, :], ALU.add))
                else:
                    link(nc.vector.memset(cumb[:, :], 0.0))
                nc.vector.tensor_scalar(selb[:, :], left[:, :], 0.0, None, ALU.is_lt).then_inc(s_sel, 1)
                link(nc.vector.reciprocal(wsum[:, 1:2], wsum[:, 0:1]))
                link(nc.vector.tensor_scalar(wsum[:, 2:3], wsum[:, 1:2], tg[0:S, 1:2], None, ALU.mult))

            def dve_slots(dve, b, link):
                dve.wait_ge(s_pos, b + 1)
                nc.vector.tensor_tensor(slot[:, :], pp[0:S, 0:E], slot1[:, :], ALU.add)
                link(nc.vector.scalar_tensor_tensor(val[:, :], pp[0:S, 0:E], float(CAP), selb[:, :], ALU.is_lt, ALU.mult))
                nc.vector.scalar_tensor_tensor(wsel[:, :], ex[:, :], wsum[:, 2:3], val[:, :], ALU.mult, ALU.mult)
                link(nc.vector.tensor_tensor(key[:, :], slot[:, :], val[:, :], ALU.mult))
                nc.vector.memset(pause[:, :], 0.0)
                link(nc.vector.max(key8[:, :], key[:, :]))
                after(dve, s_idx_saved, 32 * b)
                after(dve, s_dispatched, 16 * TOPK * b)
                link(nc.vector.tensor_scalar(none8[:, :], key8[:, :], 0.0, float(SLOTS + 1), ALU.is_equal, ALU.mult))
                link(nc.vector.scalar_tensor_tensor(idx[:, :], key8[:, :], -1.0, none8[:, :], ALU.add, ALU.add))
                for k in range(TOPK):
                    last = nc.vector.scalar_tensor_tensor(match[:, :], key[:, :], key8[:, k:k + 1], wsel[:, :],
                                                          ALU.is_equal, ALU.mult, accum_out=w8[:, k:k + 1])
                    if k < TOPK - 1:
                        link2(dve, b, k, last)
                last.then_inc(s_idx, 1)

            s_match = sem2("s_match")

            def link2(dve, b, k, ins):
                ins.then_inc(s_match, 1)
                dve.wait_ge(s_match, b * (TOPK - 1) + k + 1)

            def linker(dve, b):
                count = [0]

                def link(ins):
                    count[0] += 1
                    assert count[0] <= ROUTE_STEPS
                    ins.then_inc(s_route, 1)
                    dve.wait_ge(s_route, b * ROUTE_STEPS + count[0])
                return link, count

            def dve_batch2(dve, b, values, route):
                if values:
                    dve_values(dve, b, 0)
                if route:
                    dve_residual(dve, b - 1)
                if values:
                    dve_values(dve, b, 1)
                if route:
                    dve_normalise2(dve, b - 1)
                if values:
                    dve_attend(dve, b, 0)
                    dve_values(dve, b, 2)
                if route:
                    dve_select(dve, b - 1)
                if values:
                    dve_attend(dve, b, 1)
                if route:
                    link, count = linker(dve, b - 1)
                    dve_choose(dve, b - 1, link)
                if values:
                    dve_values(dve, b, 3)
                if route:
                    dve_slots(dve, b - 1, link)
                    while count[0] < ROUTE_STEPS:
                        link(nc.vector.memset(pause[:, :], 0.0))
                if values:
                    dve_attend(dve, b, 2)
                    dve_attend(dve, b, 3)

            @block.vector
            def _(dve):
                nc.vector.tensor_tensor(vb_sum[:, :], cols[:, VB * H:(VB + 1) * H], cols[:, VIB * H:(VIB + 1) * H],
                                        ALU.add).then_inc(s_ob_sum, 1)
                dve.wait_ge(s_ob_sum, 1)
                vb_wide = vb_sum[:, :].unsqueeze(2).broadcast_to([P, H, S])
                nc.vector.tensor_copy(vb_rep[:, 0, :, :], vb_wide).then_inc(s_ob_sum, 1)
                dve.wait_ge(s_ob_sum, 2)
                nc.vector.tensor_tensor(vb_rep[:, 1, :, :], vb_wide, vb_rep[:, 0, :, :], ALU.subtract).then_inc(s_vb_rep, 1)
                dve.wait_ge(s_rem_hi, 1)
                nc.vector.tensor_tensor(remT[:, 1, :], pg[:, 0:KT * NR], remT[:, 0, :], ALU.subtract).then_inc(s_rem_lo, 1)
                for g in range(NG):
                    dve.wait_ge(s_vrem_hi, g + 1)
                    nc.vector.tensor_tensor(vrem[:, g, 1, :], pv[g % 2][0:NR, :], vrem[:, g, 0, :],
                                            ALU.subtract).then_inc(s_vrem_lo, 1)
                dve.wait_ge(s_ob_made, 1)
                dve.wait_ge(s_ob_in, 16)
                nc.vector.tensor_tensor(obrow[:, :], po[0:S, :], obrow[:, :], ALU.add).then_inc(s_ob_sum, 1)
                dve.wait_ge(s_ob_sum, 3)
                nc.vector.tensor_scalar(obrow[:, :], obrow[:, :], tg[0:S, 0:1], None, ALU.mult).then_inc(s_obrow, 1)
                dve_batch2(dve, 0, True, False)
                dve_batch2(dve, 1, True, True)
                with dve.Fori(2, B) as b:
                    dve_batch2(dve, b, True, True)
                dve_batch2(dve, B, False, True)

            def pool_route(pool, b):
                pool.wait_ge(s_xr_in, 16 * b + 16)
                after(pool, s_x2, b)
                nc.gpsimd.tensor_tensor(xr[:, :], xr_in[:, :], obrow[:, :], ALU.add).then_inc(s_xr, 1)
                pool.wait_ge(s_x2_aggr, b + 1)
                nc.gpsimd.tensor_tensor(rstd2[:, :], mv2[:, 1:2], ln_eps[0:S, :], ALU.add).then_inc(s_x2_var, 1)
                pool.wait_ge(s_x2_var, b + 1)
                nc.gpsimd.tensor_tensor(rstd2[:, :], rstd2[:, :], mhalf[0:S, 0:1], ALU.pow).then_inc(s_x2_rstd, 1)
                pool.wait_ge(s_xd, b + 1)
                pool.wait_ge(s_idx, b + 1)
                nc.gpsimd.tensor_tensor(pool_pause[:, 0:1], mhalf[0:1, 0:1], mhalf[0:1, 1:2], ALU.add)
                for k in range(TOPK):
                    nc.gpsimd.indirect_dma_start(
                        xin_d, bass.IndirectOffsetOnAxis(ap=idx[:, k:k + 1], axis=0),
                        xd[:, :, :, :].rearrange("s a c p -> s (a c p)"), None,
                        bounds_check=SLOTS - 1, oob_is_err=False).then_inc(s_dispatched, 16)

            @block.gpsimd
            def _(pool):
                pool.wait_ge(s_obrow, 1)
                pool_route(pool, 0)
                with pool.Fori(1, B) as b:
                    pool_route(pool, b)
                pool.wait_ge(s_dispatched, 16 * TOPK * B)

    NRAW = 4
    s_ew_in = [sem(f"s_ew_in{i}") for i in range(NRAW)]
    s_rows_in = [sem(f"s_rows_in{i}") for i in range(2)]
    s_gu_hi = sem("s_gu_hi")
    s_gu_lo = sem("s_gu_lo")
    s_d_hi = sem("s_d_hi")
    s_d_lo = sem("s_d_lo")
    s_rows_turned = sem("s_rows_turned")
    s_rowsT = sem("s_rowsT")
    s_gu_made = sem("s_gu_made")
    s_silu = sem("s_silu")
    s_hid = sem("s_hid")
    s_hid_turned = sem("s_hid_turned")
    s_hid_hi = sem("s_hid_hi")
    s_hid_lo = sem("s_hid_lo")
    s_y_made = sem("s_y_made")
    s_y_out = sem("s_y_out")
    s_y_saved = [sem(f"s_y_saved{i}") for i in range(2)]
    with nc.Block() as block, ExitStack() as ph3, ExitStack() as ps3:
        raw_gu = sb(ph3, "raw_gu", [P, NRAW, KT, 2 * FF], F32)
        raw_d = sb(ph3, "raw_d", [FC, NRAW, FT * DIM], F32)
        gu = sb(ph3, "gu", [P, 2, 2, KT, 2 * FF], BF16)
        dn = sb(ph3, "dn", [FC, 2, 2, FT * DIM], BF16)
        rows = sb(ph3, "rows", [P, 2, 2 * DIM], BF16)
        rowsT = sb(ph3, "rowsT", [P, 2, 2 * KT, P], BF16)
        sg = sb(ph3, "sg", [P, FF], F32)
        hid = sb(ph3, "hid", [P, 2, FF], F32)
        hidT = sb(ph3, "hidT", [FC, 2, FT, P], BF16)
        ybuf = sb(ph3, "ybuf", [P, 2, DIM], F32)

        def pb3(name, shape, dt=F32):
            return ps3.enter_context(nc.psum_tensor(name, shape, dt))
        px = [pb3(f"px{i}", [P, 2 * KT, P], BF16) for i in range(2)]
        pgu = [pb3(f"pgu{i}", [P, 512]) for i in range(2)]
        ph = [pb3(f"ph{i}", [P, 512]) for i in range(2)]
        py = [pb3(f"py{i}", [P, 512]) for i in range(2)]

        UNROLL = 4
        FIRST = 3
        LAST = E - 2
        assert (LAST - FIRST + 1) % UNROLL == 0

        def steps(eng, body):
            for e in range(FIRST):
                body(e, e)
            with eng.Fori(0, (LAST - FIRST + 1) // UNROLL) as i:
                for j in range(UNROLL):
                    body(i * UNROLL + (FIRST + j), FIRST + j)
            for e in range(LAST + 1, E + 1):
                body(e, e)

        def is_first(e):
            return isinstance(e, int) and e == 0

        def in_range(e, ahead):
            return not isinstance(e, int) or 0 <= e + ahead < E

        def ring(e, j, ahead, size):
            return (j + ahead) % size

        def uses(e, j, size):
            return e // size + 1 if isinstance(e, int) else None

        def count_of(e_base, j, size):
            if isinstance(e_base, int):
                return j // size + 1
            return e_base * (UNROLL // size) + (j // size + 1)

        def walk(eng, body):
            def turn(i, j):
                body(lambda a, off=0: (i * UNROLL + j + off) * a if isinstance(i, int) else i * (UNROLL * a) + (j + off) * a,
                     lambda size, off=0: count_of(i, j + off, size), j, not isinstance(i, int))
            for e in range(FIRST):
                turn(0, e)
            with eng.Fori(0, (LAST - FIRST + 1) // UNROLL) as i:
                for j in range(FIRST, FIRST + UNROLL):
                    turn(i, j)
            for e in range(LAST + 1, E + 1):
                turn(0, e)

        @block.sync
        def _(sp):
            def load_expert(e, n, c, j):
                after(sp, s_gu_lo, n(1, -NRAW + 1))
                after(sp, s_d_lo, n(1, -NRAW + 1))
                r = j % NRAW
                sp.dma_start(raw_gu[:, r, :, 0:FF], wg[e].rearrange("(p c) i -> p c i", c=KT)).then_inc(s_ew_in[r], 16)
                sp.dma_start(raw_gu[:, r, :, FF:2 * FF], wu[e].rearrange("(p c) i -> p c i", c=KT)).then_inc(s_ew_in[r], 16)
                sp.dma_start(raw_d[:, r, :], wd[e].rearrange("(p c) n -> p (c n)", c=FT)).then_inc(s_ew_in[r], 16)
                after(sp, s_rows_turned, n(1, -1))
                sp.dma_start(rows[:, j % 2, :], xin_d.rearrange("(e c) n -> e c n", c=CAP)[e]).then_inc(s_rows_in[j % 2], 16)

            def save_expert(e, n, j):
                sp.wait_ge(s_y_out, n(1, 1))
                sp.dma_start(y_d[0:SLOTS, :].rearrange("(e c) n -> e c n", c=CAP)[e], ybuf[:, j % 2, :]).then_inc(s_y_saved[j % 2], 16)

            AHEAD = 3

            def body(n, c, j, looped):
                e = n(1)
                if looped or e + AHEAD < E:
                    load_expert(n(1, AHEAD), lambda a, off=0: n(a, AHEAD + off), None, j + AHEAD)
                if looped or 0 <= e - 1:
                    save_expert(n(1, -1), lambda a, off=0: n(a, off - 1), j - 1)
            for e in range(AHEAD):
                load_expert(e, lambda a, off=0: (e + off) * a, None, e)
            for e in range(FIRST):
                body(lambda a, off=0: (e + off) * a, None, e, False)
            turns = (E - AHEAD - FIRST) // UNROLL
            with sp.Fori(0, turns) as i:
                for j in range(FIRST, FIRST + UNROLL):
                    body(lambda a, off=0: i * (UNROLL * a) + (j + off) * a, None, j, True)
            for e in range(FIRST + turns * UNROLL, E + 1):
                body(lambda a, off=0: (e + off) * a, None, e, False)
            for i in range(2):
                sp.wait_ge(s_y_saved[i], 16 * E // 2)

        @block.tensor
        def _(pe):
            def turn_rows(n, c, j):
                pe.wait_ge(s_rows_in[j % 2], c * 16)
                after(pe, s_rowsT, n(1, -1))
                for q in range(2 * KT):
                    mm = pe.transpose(px[j % 2][:, q, :], rows[:, j % 2, q * P:(q + 1) * P], identb[:, :])
                mm.then_inc(s_rows_turned, 1)

            def body(n, c, j, looped):
                e = n(1)
                here, before, ahead = looped or e < E, looped or e >= 1, looped or e + 1 < E
                if not looped and e == 0:
                    turn_rows(n, c(2), j)
                if before:
                    pe.wait_ge(s_hid, n(1))
                    after(pe, s_hid_lo, n(1, -2))
                    for q in range(FT):
                        hv = hid[:, (j - 1) % 2, :].rearrange("s (p c) -> s c p", c=FT)
                        mm = pe.transpose(ph[(j - 1) % 2][0:FC, q * P:(q + 1) * P], hv[:, q, :], ident[:, :])
                    mm.then_inc(s_hid_turned, 1)
                if ahead:
                    turn_rows(lambda a, off=0: n(a, 1 + off), c(2, 1), j + 1)
                if here:
                    pe.wait_ge(s_rowsT, n(1, 1))
                    pe.wait_ge(s_gu_lo, n(1, 1))
                    after(pe, s_hid, n(1, -1))
                    for k in range(KT):
                        mm = split_matmul(pe, pgu[j % 2][:, 0:2 * FF], (rowsT[:, j % 2, k, :], rowsT[:, j % 2, KT + k, :]),
                                          (gu[:, j % 2, 0, k, :], gu[:, j % 2, 1, k, :]), k == 0, k == KT - 1)
                    mm.then_inc(s_gu_made, 1)
                if before:
                    p = (j - 1) % 2
                    pe.wait_ge(s_hid_lo, n(1))
                    pe.wait_ge(s_d_lo, n(1))
                    after(pe, s_y_out, n(1, -2))
                    for q in range(FT):
                        mm = split_matmul(pe, py[p][:, :], (hidT[:, 0, q, :], hidT[:, 1, q, :]),
                                          (dn[:, p, 0, q * DIM:(q + 1) * DIM], dn[:, p, 1, q * DIM:(q + 1) * DIM]),
                                          q == 0, q == FT - 1)
                    mm.then_inc(s_y_made, 1)
            walk(pe, body)

        @block.scalar
        def _(act):
            def split(n, j):
                r, p = j % NRAW, j % 2
                act.wait_ge(s_ew_in[r], n_in(n, j))
                after(act, s_gu_made, n(1, -1))
                nc.scalar.copy(gu[:, p, 0, :, :].rearrange("p k n -> p (k n)"),
                               raw_gu[:, r, :, :].rearrange("p k n -> p (k n)")).then_inc(s_gu_hi, 1)

            def n_in(n, j):
                return None

            def body(n, c, j, looped):
                e = n(1)
                here, before, ahead = looped or e < E, looped or e >= 1, looped or e + 1 < E

                def hi(off):
                    r, p = (j + off) % NRAW, (j + off) % 2
                    act.wait_ge(s_ew_in[r], 48 * c(NRAW, off))
                    after(act, s_gu_made, n(1, off - 1))
                    nc.scalar.copy(gu[:, p, 0, :, :].rearrange("p k n -> p (k n)"),
                                   raw_gu[:, r, :, :].rearrange("p k n -> p (k n)")).then_inc(s_gu_hi, 1)

                def turned(off):
                    p = (j + off) % 2
                    act.wait_ge(s_rows_turned, n(1, off + 1))
                    after(act, s_gu_made, n(1, off - 1))
                    nc.scalar.copy(rowsT[:, p, :, :], px[p][:, :, :]).then_inc(s_rowsT, 1)
                if not looped and e == 0:
                    turned(0)
                    hi(0)
                if before:
                    act.wait_ge(s_hid_turned, n(1))
                    after(act, s_y_made, n(1, -1))
                    nc.scalar.copy(hidT[:, 0, :, :], ph[(j - 1) % 2][0:FC, 0:FT * P].rearrange("p (c s) -> p c s", c=FT)).then_inc(s_hid_hi, 1)
                if ahead:
                    turned(1)
                if here:
                    act.wait_ge(s_gu_made, n(1, 1))
                    after(act, s_hid, n(1))
                    nc.scalar.activation(sg[:, :], pgu[j % 2][:, 0:FF], ACT.Silu).then_inc(s_silu, 1)
                if ahead:
                    hi(1)
            walk(act, body)

        @block.vector
        def _(dve):
            def body(n, c, j, looped):
                e = n(1)
                here, before, ahead = looped or e < E, looped or e >= 1, looped or e + 1 < E

                def lo(off):
                    r, p = (j + off) % NRAW, (j + off) % 2
                    dve.wait_ge(s_gu_hi, n(1, off + 1))
                    nc.vector.tensor_tensor(gu[:, p, 1, :, :].rearrange("p k n -> p (k n)"),
                                            raw_gu[:, r, :, :].rearrange("p k n -> p (k n)"),
                                            gu[:, p, 0, :, :].rearrange("p k n -> p (k n)"), ALU.subtract).then_inc(s_gu_lo, 1)

                def d_hi(off):
                    r, p = (j + off) % NRAW, (j + off) % 2
                    dve.wait_ge(s_ew_in[r], 48 * c(NRAW, off))
                    after(dve, s_y_made, n(1, off - 1))
                    nc.vector.tensor_copy(dn[:, p, 0, :], raw_d[:, r, :]).then_inc(s_d_hi, 1)
                if not looped and e == 0:
                    d_hi(0)
                    lo(0)
                if before:
                    dve.wait_ge(s_hid_hi, n(1))
                    nc.vector.tensor_tensor(hidT[:, 1, :, :], ph[(j - 1) % 2][0:FC, 0:FT * P].rearrange("p (c s) -> p c s", c=FT),
                                            hidT[:, 0, :, :], ALU.subtract).then_inc(s_hid_lo, 1)
                if here:
                    dve.wait_ge(s_silu, n(1, 1))
                    after(dve, s_hid_turned, n(1, -1))
                    nc.vector.tensor_tensor(hid[:, j % 2, :], sg[:, :], pgu[j % 2][:, FF:2 * FF], ALU.mult).then_inc(s_hid, 1)
                if before:
                    p = (j - 1) % 2
                    dve.wait_ge(s_y_made, n(1))
                    if looped or e >= 3:
                        dve.wait_ge(s_y_saved[p], 16 * c(2, -3))
                    nc.vector.tensor_copy(ybuf[:, p, :], py[p][:, :]).then_inc(s_y_out, 1)
                if ahead:
                    d_hi(1)
                    lo(1)
            walk(dve, body)

        @block.gpsimd
        def _(pool):
            def body(n, c, j, looped):
                e = n(1)
                if looped or e < E:
                    r, p = j % NRAW, j % 2
                    pool.wait_ge(s_d_hi, n(1, 1))
                    nc.gpsimd.tensor_tensor(dn[:, p, 1, :], raw_d[:, r, :], dn[:, p, 0, :], ALU.subtract).then_inc(s_d_lo, 1)
            walk(pool, body)

    s_c_in = [sem(f"s_c_in{i}") for i in range(2)]
    s_gathered = [sem(f"s_gathered{i}") for i in range(2)]
    s_sum = sem("s_sum")
    s_pause = sem("s_pause")
    s_done = sem("s_done")
    s_out = [sem(f"s_out{i}") for i in range(2)]
    with nc.Block() as block, ExitStack() as ph4:
        acc = sb(ph4, "acc", [S, 2, DIM], F32)
        got = sb(ph4, "got", [S, 2, TOPK, DIM], F32)
        idx4 = sb(ph4, "idx4", [S, 2, TOPK], U32)
        w84 = sb(ph4, "w84", [S, 2, TOPK], F32)
        pool_pause4 = sb(ph4, "pool_pause4", [1, 1], F32)
        PAIRS = B // 2

        @block.sync
        def _(sp):
            def load(i, j):
                b = i * 2 + j
                after(sp, s_out[j], 16 * i)
                sp.dma_start(acc[:, j, :], x2_d[b]).then_inc(s_c_in[j], 16)
                sp.dma_start(idx4[:, j, :], idx_d[b]).then_inc(s_c_in[j], 16)
                sp.dma_start(w84[:, j, :], w8_d[b]).then_inc(s_c_in[j], 16)

            def store(i, j):
                sp.wait_ge(s_done, i * 2 + (j + 1))
                sp.dma_start(out[i * 2 + j], acc[:, j, :]).then_inc(s_out[j], 16)
            load(0, 0)
            load(0, 1)
            with sp.Fori(1, PAIRS) as i:
                for j in range(2):
                    store(i - 1, j)
                    load(i, j)
            for j in range(2):
                store(PAIRS - 1, j)
            for j in range(2):
                sp.wait_ge(s_out[j], 16 * PAIRS)

        @block.gpsimd
        def _(pool):
            def gather(i, j):
                pool.wait_ge(s_c_in[j], 48 * i + 48)
                after(pool, s_done, i * 2 - 1 + j)
                after(pool, s_pause, i * 2 + j)
                nc.gpsimd.tensor_tensor(pool_pause4[:, :], mhalf[0:1, 0:1], mhalf[0:1, 1:2], ALU.add).then_inc(s_pause, 1)
                for k in range(TOPK):
                    nc.gpsimd.indirect_dma_start(
                        got[:, j, k, :], None, y_d, bass.IndirectOffsetOnAxis(ap=idx4[:, j, k:k + 1], axis=0),
                        bounds_check=SLOTS, oob_is_err=False).then_inc(s_gathered[j], 16)
            gather(0, 0)
            gather(0, 1)
            with pool.Fori(1, PAIRS) as i:
                for j in range(2):
                    gather(i, j)

        @block.vector
        def _(dve):
            def weigh(i, j):
                b = i * 2 + j
                dve.wait_ge(s_c_in[j], 48 * i + 48)
                dve.wait_ge(s_gathered[j], 16 * TOPK * (i + 1))
                for k in range(TOPK):
                    last = nc.vector.scalar_tensor_tensor(acc[:, j, :], got[:, j, k, :], w84[:, j, k:k + 1],
                                                          acc[:, j, :], ALU.mult, ALU.add)
                    if k < TOPK - 1:
                        last.then_inc(s_sum, 1)
                        dve.wait_ge(s_sum, b * (TOPK - 1) + k + 1)
                last.then_inc(s_done, 1)
            weigh(0, 0)
            weigh(0, 1)
            with dve.Fori(1, PAIRS) as i:
                for j in range(2):
                    weigh(i, j)


_INS = ['x', 'ctx_2048', 'g_xattn', 'g_ffn', 'L0_xattn_q_w', 'L0_xattn_q_b', 'L0_xattn_k_w', 'L0_xattn_k_b',
        'L0_xattn_v_w', 'L0_xattn_v_b', 'L0_xattn_ki_w', 'L0_xattn_ki_b', 'L0_xattn_vi_w', 'L0_xattn_vi_b',
        'L0_xattn_o_w', 'L0_xattn_o_b', 'L0_xattn_nq_s', 'L0_xattn_nkt_s', 'L0_xattn_nki_s', 'L0_ffn_gate_w',
        'L0_ffn_wg', 'L0_ffn_wu', 'L0_ffn_wd']


def kernel(**inputs):
    import numpy as _np
    import concourse.bacc as _bacc
    from concourse import mybir as _mybir
    from concourse.bass_utils import run_bass_kernel_spmd as _run

    nc = _bacc.Bacc("TRN2", target_bir_lowering=False, num_devices=1)
    arrays, args = {}, []
    for name in _INS:
        a = _np.ascontiguousarray(inputs[name])
        arrays[f"in_{name}"] = a
        args.append(nc.dram_tensor(f"in_{name}", a.shape, _mybir.dt.from_np(a.dtype), kind="ExternalInput").ap())
    args.append(nc.dram_tensor("out_y", (B, S, DIM), F32, kind="ExternalOutput").ap())
    build(nc, *args)
    r = _run(nc, [arrays], core_ids=[0])
    return r.results[0]["out_y"]
```

```python
from contextlib import ExitStack

import concourse.bass as bass
from concourse import mybir

ALU = mybir.AluOpType
ACT = mybir.ActivationFunctionType
AX = mybir.AxisListType
F32 = mybir.dt.float32
BF16 = mybir.dt.bfloat16
U32 = mybir.dt.uint32
U16 = mybir.dt.uint16

P = 128
B, S, DIM = 8, 112, 512
LCTX, N_IMG = 375, 257
N_TXT = LCTX - N_IMG
H, D = 16, 128
INNER = H * D
KT = DIM // P
CH = LCTX // 3
NREM = CH - N_TXT
HG = 4
NG = H // HG
E, TOPK, FF, CAP = 64, 8, 192, 128
FC = 96
FT = FF // FC
SLOTS = E * CAP
TOKENS = B * S
ROW = 2 * DIM + 2 * E + 4
LN_EPS, RMS_EPS = 1e-5, 1e-6
VEC = 8
W_SLOTS = 3
W_STAGES = 3
NCHUNK = 4


def build(nc, x, ctx_in, g_xattn, g_ffn, q_w, q_b, k_w, k_b, v_w, v_b, ki_w, ki_b, vi_w, vi_b,
          o_w, o_b, nq_s, nkt_s, nki_s, gate_w, wg, wu, wd, out):
    with ExitStack() as top:
        build_in(nc, top, x, ctx_in, g_xattn, g_ffn, q_w, q_b, k_w, k_b, v_w, v_b, ki_w, ki_b,
                 vi_w, vi_b, o_w, o_b, nq_s, nkt_s, nki_s, gate_w, wg, wu, wd, out)


def after(eng, sem, value):
    if not isinstance(value, int) or value > 0:
        eng.wait_ge(sem, value)


def build_in(nc, top, x, ctx_in, g_xattn, g_ffn, q_w, q_b, k_w, k_b, v_w, v_b, ki_w, ki_b,
             vi_w, vi_b, o_w, o_b, nq_s, nkt_s, nki_s, gate_w, wg, wu, wd, out):
    def sem(name):
        return top.enter_context(nc.semaphore(name))

    def dram(name, shape, dt):
        return nc.dram_tensor(name, shape, dt, kind="Internal").ap()

    ctxT_d = dram("ctxT_d", [B, P, 2 * KT * LCTX], BF16)
    pt_d = dram("pt_d", [B * NG, P, HG * 6 * S], BF16)
    vrem_d = dram("vrem_d", [B, NREM, NG, 2 * 512], BF16)
    xin_d = dram("xin_d", [SLOTS, ROW], U16)
    acc_d = dram("acc_d", [TOKENS + CAP, DIM], F32)

    def sb(stack, name, shape, dt):
        return stack.enter_context(nc.sbuf_tensor(name, shape, dt))

    ident = sb(top, "ident", [P, P], F32)
    identb = sb(top, "identb", [P, P], BF16)
    ones = sb(top, "ones", [P, P], F32)
    onesb = sb(top, "onesb", [S, S], BF16)
    trib = sb(top, "trib", [S, S], BF16)
    cols = sb(top, "cols", [P, VEC * H], F32)
    kb_scaled = sb(top, "kb_scaled", [P, 2, H], F32)
    vecs_raw = sb(top, "vecs_raw", [P, P], F32)
    slot1 = sb(top, "slot1", [S, E], F32)
    eid_i = sb(top, "eid_i", [S, E], mybir.dt.int32)
    zeros = sb(top, "zeros", [P, ROW], U16)
    tok1 = sb(top, "tok1", [P, 1], F32)
    empty_row = sb(top, "empty_row", [P, 1], F32)
    tok_i = sb(top, "tok_i", [P, 1], mybir.dt.int32)
    mhalf = sb(top, "mhalf", [P, 4], F32)
    ln_eps = sb(top, "ln_eps", [P, 1], F32)
    tg = sb(top, "tg", [P, 2], F32)
    g_raw = sb(top, "g_raw", [P, 2], F32)

    s_const = sem("s_const")
    s_vecs_in = sem("s_vecs_in")
    s_vecs_turned = sem("s_vecs_turned")
    s_cols = sem("s_cols")
    s_g_in = sem("s_g_in")
    s_tanh = sem("s_tanh")
    s_zeroed = sem("s_zeroed")
    s_w_in = [sem(f"s_w_in{i}") for i in range(W_STAGES)]
    s_w_hi = [sem(f"s_w_hi{i}") for i in range(W_STAGES)]
    s_w_lo = [sem(f"s_w_lo{i}") for i in range(W_STAGES)]
    s_ctx_in = sem("s_ctx_in")
    s_x_in = sem("s_x_in")
    s_ctx_turned = sem("s_ctx_turned")
    s_ctx_hi = sem("s_ctx_hi")
    s_ctx_lo = sem("s_ctx_lo")
    s_ctx_saved = sem("s_ctx_saved")
    s_ln_stats = sem("s_ln_stats")
    s_ln_aggr = sem("s_ln_aggr")
    s_ln_var = sem("s_ln_var")
    s_ln_rstd = sem("s_ln_rstd")
    s_xn = sem("s_xn")
    s_xn_turned = sem("s_xn_turned")
    s_xn_hi = sem("s_xn_hi")
    s_xn_lo = sem("s_xn_lo")
    s_k_made = sem("s_k_made")
    s_q_made = sem("s_q_made")
    s_k_out = sem("s_k_out")
    s_k_hi = sem("s_k_hi")
    s_kb_scaled = sem("s_kb_scaled")
    s_q_out = sem("s_q_out")
    s_kq_hi = sem("s_kq_hi")
    s_kq_split = sem("s_kq_split")
    s_square = sem("s_square")
    s_squared = sem("s_squared")
    s_sums = sem("s_sums")
    s_ms = sem("s_ms")
    s_rms = sem("s_rms")
    s_rdiag = sem("s_rdiag")
    s_rrow = sem("s_rrow")
    s_rrow_out = sem("s_rrow_out")
    s_s_made = sem("s_s_made")
    s_s_scaled = sem("s_s_scaled")
    s_nmax = sem("s_nmax")
    s_exp = sem("s_exp")
    s_rcp = sem("s_rcp")
    s_p = sem("s_p")
    s_p_turned = sem("s_p_turned")
    s_p_hi = sem("s_p_hi")
    s_p_lo = sem("s_p_lo")
    s_p_saved = [sem(f"s_p_saved{i}") for i in range(4)]

    with ExitStack() as mem:
        w_raw = [sb(mem, f"w_raw{i}", [P, INNER], F32) for i in range(W_STAGES)]
        w_hi = [sb(mem, f"w_hi{i}", [P, KT, INNER], BF16) for i in range(W_SLOTS)]
        w_lo = [sb(mem, f"w_lo{i}", [P, KT, INNER], BF16) for i in range(W_SLOTS)]
        K_SLOT, KI_SLOT, Q_SLOT = 0, 1, 2
        V_SLOT, VI_SLOT, O_SLOT = 0, 1, 2
        with nc.Block() as block, ExitStack() as ph1, ExitStack() as ps1:
            ctx_raw = sb(ph1, "ctx_raw", [P, 3, DIM], F32)
            ctxT = sb(ph1, "ctxT", [P, 2, KT, LCTX], BF16)
            x_raw = sb(ph1, "x_raw", [S, DIM], F32)
            stats = sb(ph1, "stats", [S, 6], F32)
            mv = sb(ph1, "mv", [S, 2], F32)
            rstd = sb(ph1, "rstd", [S, 1], F32)
            xn = sb(ph1, "xn", [S, DIM], F32)
            xnT = sb(ph1, "xnT", [P, 2, KT, S], BF16)
            kT = sb(ph1, "kT", [P, H, 2, LCTX], BF16)
            qT = sb(ph1, "qT", [P, H, 2, S], BF16)
            RKQ = 2
            kq = sb(ph1, "kq", [P, RKQ, LCTX + S], F32)
            sq = sb(ph1, "sq", [P, LCTX + S], F32)
            sq_sum = sb(ph1, "sq_sum", [P, LCTX + S], F32)
            ms = sb(ph1, "ms", [P, 4], F32)
            rms = sb(ph1, "rms", [P, 4], F32)
            q_scale = sb(ph1, "q_scale", [S, 1], F32)
            rdiag = sb(ph1, "rdiag", [CH, 3, CH], F32)
            rrow = sb(ph1, "rrow", [S, LCTX], F32)
            RS = 4
            prob = sb(ph1, "prob", [S, RS, LCTX], F32)
            pause = sb(ph1, "pause", [1, 1], F32)
            pause_ln = sb(ph1, "pause_ln", [1, 1], F32)
            mx = sb(ph1, "mx", [S, RS, 2], F32)
            nmx = sb(ph1, "nmx", [S, RS, 2], F32)
            psum_row = sb(ph1, "psum_row", [S, RS, 2], F32)
            rcp = sb(ph1, "rcp", [S, RS, 2], F32)
            ptb = sb(ph1, "ptb", [P, 4, 2, 3 * S], BF16)

            def pb(name, shape, dt=F32):
                return ps1.enter_context(nc.psum_tensor(name, shape, dt))

            pk = [pb(f"pk{i}", [P, 512]) for i in range(2)]
            pq = pb("pq", [P, 512])
            ps = [pb(f"ps{i}", [P, 512]) for i in range(2)]
            pt = [pb(f"pt{i}", [P, 512]) for i in range(2)]
            pm = pb("pm", [P, 512])

            w_plan = [(w, slot, c) for c in range(NCHUNK) for w, slot in
                      [(k_w, K_SLOT), (ki_w, KI_SLOT), (q_w, Q_SLOT)]]
            w_plan += [(w, slot, c) for c in range(NCHUNK) for w, slot in [(v_w, V_SLOT), (vi_w, VI_SLOT)]]
            w_plan += [(o_w, O_SLOT, c) for c in range(NCHUNK)]
            W_HALF = 3 * NCHUNK

            def w_part(part, n):
                w, slot, c = w_plan[n]
                if w is o_w:
                    return part[slot][:, c, :].rearrange("p (h n) -> p h n", n=DIM)
                return part[slot][:, :, c * 512:(c + 1) * 512]

            def w_staged(n):
                return w_raw[n % W_STAGES][:, :].rearrange("p (k n) -> p k n", n=512)

            def load_weights(sp, n):
                w, slot, c = w_plan[n]
                if w is o_w:
                    src = w.rearrange("(c h d) n -> c d h n", c=NCHUNK, d=D)[c]
                else:
                    src = w.rearrange("(k p) (c n) -> c p k n", p=P, n=512)[c]
                after(sp, s_w_lo[n % W_STAGES], n // W_STAGES)
                sp.dma_start(w_staged(n), src).then_inc(s_w_in[n % W_STAGES], 16)

            def weights_hi(act, n):
                act.wait_ge(s_w_in[n % W_STAGES], 16 * (n // W_STAGES + 1))
                nc.scalar.copy(w_part(w_hi, n), w_staged(n)).then_inc(s_w_hi[n % W_STAGES], 1)

            def weights_lo(eng, n):
                eng.wait_ge(s_w_hi[n % W_STAGES], n // W_STAGES + 1)
                eng.tensor_tensor(w_part(w_lo, n), w_staged(n), w_part(w_hi, n),
                                  ALU.subtract).then_inc(s_w_lo[n % W_STAGES], 1)

            def weights_ready(pe, group):
                for i in range(W_STAGES):
                    pe.wait_ge(s_w_lo[i], group + 1)

            def vec(v, h):
                return cols[:, v * H + h:v * H + h + 1]
            QB, KB, KIB, NQ, NKT, NKI, VB, VIB = range(VEC)

            def load_batch(sp, b):
                after(sp, s_ctx_turned, b * KT)
                sp.dma_start(ctx_raw[0:N_TXT, 0, :], ctx_in[b, N_IMG:LCTX, :]).then_inc(s_ctx_in, 16)
                sp.dma_start(ctx_raw[N_TXT:CH, 0, :], ctx_in[b, 2 * CH:N_IMG, :]).then_inc(s_ctx_in, 16)
                sp.dma_start(ctx_raw[0:CH, 1:3, :],
                             ctx_in[b, 0:2 * CH, :].rearrange("(c p) d -> p c d", p=CH)).then_inc(s_ctx_in, 16)
                after(sp, s_xn, b)
                sp.dma_start(x_raw[:, :], x[b]).then_inc(s_x_in, 16)

            def save_batch(sp, b):
                sp.wait_ge(s_ctx_lo, b * KT + KT)
                sp.dma_start(ctxT_d[b], ctxT[:, :, :, :].rearrange("p a k l -> p (a k l)")).then_inc(s_ctx_saved, 16)

            def zero_rows(sp, b):
                sp.dma_start(xin_d.rearrange("(g a p) n -> g p a n", g=B, p=P)[b],
                             zeros[:, :].unsqueeze(1).broadcast_to([P, SLOTS // B // P, ROW])).then_inc(s_zeroed, 16)

            def save_prob(sp, b, h):
                    sp.wait_ge(s_p_lo, b * H + h + 1)
                    sp.dma_start(pt_d[b * NG + h // HG][:, (h % HG) * 6 * S:(h % HG + 1) * 6 * S],
                                 ptb[:, h % 4, :, :].rearrange("p a s -> p (a s)")).then_inc(s_p_saved[h % 4], 16)

            def save_probs(sp, b):
                for h in range(H):
                    save_prob(sp, b, h)

            @block.sync
            def _(sp):
                vectors = [q_b, k_b, ki_b, nq_s, nkt_s, nki_s, v_b, vi_b]
                for v, a in enumerate(vectors):
                    sp.dma_start(vecs_raw[v * H:(v + 1) * H, :], a.rearrange("(h d) -> h d", d=D)).then_inc(s_vecs_in, 16)
                for i, g in enumerate([g_xattn, g_ffn]):
                    sp.dma_start(g_raw[:, i:i + 1], g.rearrange("(a b) -> a b", a=1).broadcast_to([P, 1])).then_inc(s_g_in, 16)
                load_batch(sp, 0)
                for n in range(W_HALF):
                    load_weights(sp, n)
                save_batch(sp, 0)
                sp.wait_ge(s_const, 1)
                sp.dma_start(acc_d[TOKENS:TOKENS + CAP, :], zeros[:, 0:2 * DIM].bitcast(F32)).then_inc(s_zeroed, 16)
                load_batch(sp, 1)
                zero_rows(sp, 0)
                with sp.Fori(1, B - 1) as b:
                    save_batch(sp, b)
                    load_batch(sp, b + 1)
                    zero_rows(sp, b)
                    save_probs(sp, b - 1)
                save_batch(sp, B - 1)
                zero_rows(sp, B - 1)
                save_probs(sp, B - 2)
                for n in range(W_HALF, W_HALF + W_STAGES):
                    load_weights(sp, n)
                for h in range(H):
                    if W_HALF + W_STAGES + h < 2 * W_HALF:
                        load_weights(sp, W_HALF + W_STAGES + h)
                    save_prob(sp, B - 1, h)
                sp.wait_ge(s_ctx_saved, 16 * B)
                sp.wait_ge(s_zeroed, 16 * (B + 1))
                for i in range(4):
                    sp.wait_ge(s_p_saved[i], 16 * B * H // 4)

            @block.gpsimd
            def _(pool):
                nc.gpsimd.memset(zeros[:, :], 0).then_inc(s_const, 1)
                nc.gpsimd.memset(ident[:, :], 0.0).then_inc(s_const, 1)
                nc.gpsimd.memset(ones[:, :], 1.0).then_inc(s_const, 1)
                nc.gpsimd.memset(onesb[:, :], 1.0).then_inc(s_const, 1)
                nc.gpsimd.memset(ptb[:, :, :, :], 0.0).then_inc(s_const, 1)
                nc.gpsimd.memset(ms[:, :], 1.0).then_inc(s_const, 1)
                nc.gpsimd.memset(mhalf[:, :], -0.5)
                nc.gpsimd.memset(ln_eps[:, :], LN_EPS)
                pool.wait_ge(s_const, 6)
                nc.gpsimd.affine_select(out=ident[:, :], in_=ident[:, :], compare_op=ALU.not_equal, fill=1.0,
                                        base=0, pattern=[[-1, P]], channel_multiplier=1).then_inc(s_const, 1)
                nc.gpsimd.affine_select(out=trib[:, :], in_=onesb[:, :], compare_op=ALU.is_ge, fill=0.0,
                                        base=-1, pattern=[[1, S]], channel_multiplier=-1).then_inc(s_const, 1)
                nc.gpsimd.iota(eid_i[:, :], pattern=[[CAP, E]], base=1, channel_multiplier=0).then_inc(s_const, 1)
                nc.gpsimd.iota(tok_i[:, :], pattern=[[0, 1]], base=1, channel_multiplier=1).then_inc(s_const, 1)
                pool.wait_ge(s_const, 10)
                nc.gpsimd.tensor_copy(identb[:, :], ident[:, :]).then_inc(s_const, 1)
                nc.gpsimd.tensor_copy(slot1[:, :], eid_i[:, :]).then_inc(s_const, 1)
                nc.gpsimd.tensor_copy(tok1[:, :], tok_i[:, :]).then_inc(s_const, 1)
                pool.wait_ge(s_const, 13)
                nc.gpsimd.tensor_scalar(empty_row[:, :], tok1[:, :], float(TOKENS), 1.0, ALU.add, ALU.mult).then_inc(s_const, 1)

                def ln_power(b):
                    pool.wait_ge(s_ln_aggr, b + 1)
                    nc.gpsimd.tensor_tensor(rstd[:, :], mv[:, 1:2], ln_eps[0:S, :], ALU.add).then_inc(s_ln_var, 1)
                    pool.wait_ge(s_ln_var, b + 1)
                    nc.gpsimd.tensor_tensor(rstd[:, :], rstd[:, :], mhalf[0:S, 0:1], ALU.pow).then_inc(s_ln_rstd, 1)

                LN_HEAD = 8

                def squares(b, ln_next):
                    for h in range(H):
                        n = b * H + h
                        pool.wait_ge(s_k_out, n + 1)
                        pool.wait_ge(s_q_out, n + 1)
                        src = kq[:, h % RKQ, :]
                        if h == 0:
                            after(pool, s_sums, b)
                            nc.gpsimd.tensor_tensor(sq_sum[:, :], src, src, ALU.mult).then_inc(s_squared, 1)
                        else:
                            pool.wait_ge(s_squared, n)
                            nc.gpsimd.tensor_tensor(sq[:, :], src, src, ALU.mult).then_inc(s_square, 1)
                            pool.wait_ge(s_square, b * (H - 1) + h)
                            nc.gpsimd.tensor_tensor(sq_sum[:, :], sq_sum[:, :], sq[:, :], ALU.add).then_inc(s_squared, 1)
                        if ln_next and h == LN_HEAD:
                            ln_power(b + 1)
                    pool.wait_ge(s_ms, b + 1)
                    nc.gpsimd.tensor_tensor(rms[:, :], ms[:, :], mhalf[:, :], ALU.pow).then_inc(s_rms, 1)

                ln_power(0)
                squares(0, True)
                with pool.Fori(1, B - 1) as b:
                    squares(b, True)
                squares(B - 1, False)
                for n in range(W_HALF, 2 * W_HALF):
                    if n % W_STAGES == W_STAGES - 1:
                        weights_lo(nc.gpsimd, n)

            def split_matmul(pe, dst, lhs, rhs, first, last):
                pe.matmul(dst, lhs[0], rhs[0], start=first, stop=False)
                pe.matmul(dst, lhs[0], rhs[1], start=False, stop=False)
                return pe.matmul(dst, lhs[1], rhs[0], start=False, stop=last)

            def turn_batch(pe, b):
                pe.wait_ge(s_ctx_in, 48 * b + 48)
                for k in range(KT):
                    if k < 2:
                        after(pe, s_k_hi, b * H - 1 + k)
                    else:
                        pe.wait_ge(s_ctx_lo, b * KT + k - 1)
                    for c in range(3):
                        mm = pe.transpose(pk[k % 2][:, c * CH:(c + 1) * CH],
                                          ctx_raw[0:CH, c, k * P:(k + 1) * P], ident[0:CH, 0:CH])
                    mm.then_inc(s_ctx_turned, 1)
                pe.wait_ge(s_xn, b + 1)
                after(pe, s_q_out, b * H)
                for k in range(KT):
                    mm = pe.transpose(pq[:, k * S:(k + 1) * S], xn[:, k * P:(k + 1) * P], ident[0:S, 0:S])
                mm.then_inc(s_xn_turned, 1)

            def project_head(pe, b, h):
                n = b * H + h
                if h % HG == 0 and isinstance(b, int) and b == 0:
                    weights_ready(pe, h // HG)
                if h < 2:
                    pe.wait_ge(s_ctx_lo, b * KT + KT)
                else:
                    pe.wait_ge(s_k_hi, n - 1)
                for slot, lo, hi in [(K_SLOT, 0, N_TXT), (KI_SLOT, N_TXT, LCTX)]:
                    for k in range(KT):
                        mm = split_matmul(pe, pk[h % 2][:, lo:hi],
                                          (w_hi[slot][:, k, h * D:(h + 1) * D], w_lo[slot][:, k, h * D:(h + 1) * D]),
                                          (ctxT[:, 0, k, lo:hi], ctxT[:, 1, k, lo:hi]), k == 0, k == KT - 1)
                mm.then_inc(s_k_made, 1)
                if h == 0:
                    pe.wait_ge(s_xn_lo, b + 1)
                else:
                    pe.wait_ge(s_q_out, n)
                for k in range(KT):
                    mm = split_matmul(pe, pq[:, 0:S],
                                      (w_hi[Q_SLOT][:, k, h * D:(h + 1) * D], w_lo[Q_SLOT][:, k, h * D:(h + 1) * D]),
                                      (xnT[:, 0, k, :], xnT[:, 1, k, :]), k == 0, k == KT - 1)
                mm.then_inc(s_q_made, 1)

            def score_head(pe, b, h):
                n = b * H + h
                pe.wait_ge(s_kq_split, n + 1)
                after(pe, s_s_scaled, n - 1)
                mm = split_matmul(pe, ps[h % 2][0:S, 0:LCTX], (qT[:, h, 0, :], qT[:, h, 1, :]),
                                  (kT[:, h, 0, :], kT[:, h, 1, :]), True, True)
                mm.then_inc(s_s_made, 1)

            def turn_probs(pe, b, h):
                n = b * H + h
                pe.wait_ge(s_p, n + 1)
                after(pe, s_p_lo, n - 1)
                for c in range(3):
                    mm = pe.transpose(pt[h % 2][0:CH, c * S:(c + 1) * S],
                                      prob[:, h % RS, c * CH:(c + 1) * CH], ident[0:S, 0:S])
                mm.then_inc(s_p_turned, 1)

            def sum_squares(pe, b):
                pe.wait_ge(s_squared, (b + 1) * H)
                after(pe, s_rrow_out, b)
                for c in range(3):
                    pe.matmul(pm[0:CH, c:c + 1], sq_sum[:, c * CH:(c + 1) * CH], ones[:, 0:1], start=True, stop=True)
                pe.matmul(pm[0:S, 3:4], sq_sum[:, LCTX:LCTX + S], ones[:, 0:1], start=True, stop=True).then_inc(s_sums, 1)

            def key_row(pe, b):
                pe.wait_ge(s_rdiag, b + 1)
                pe.matmul(pm[0:S, 0:LCTX], ones[0:CH, 0:S], rdiag[:, :, :].rearrange("p c l -> p (c l)"),
                          start=True, stop=True).then_inc(s_rrow, 1)

            LAG = 2

            def pe_batch(pe, b, project, score):
                if score:
                    key_row(pe, b - 1)
                for h in range(H):
                    if score:
                        score_head(pe, b - 1, h)
                    if project:
                        project_head(pe, b, h)
                    if score and h >= LAG:
                        turn_probs(pe, b - 1, h - LAG)
                if project and not is_last(b):
                    turn_batch(pe, b + 1)
                if score:
                    for h in range(H - LAG, H):
                        turn_probs(pe, b - 1, h)
                if project:
                    sum_squares(pe, b)

            def is_last(b):
                return isinstance(b, int) and b == B - 1

            def all_batches(eng, batch):
                batch(eng, 0, True, False)
                batch(eng, 1, True, True)
                with eng.Fori(2, B - 1) as b:
                    batch(eng, b, True, True)
                batch(eng, B - 1, True, True)
                batch(eng, B, False, True)

            @block.tensor
            def _(pe):
                pe.wait_ge(s_const, 7)
                pe.wait_ge(s_vecs_in, 16 * VEC)
                pe.transpose(pm[:, 0:P], vecs_raw[:, :], ident[:, :]).then_inc(s_vecs_turned, 1)
                pe.wait_ge(s_cols, 1)
                turn_batch(pe, 0)
                all_batches(pe, pe_batch)

            def act_turned(act, b):
                for k in range(KT):
                    act.wait_ge(s_ctx_turned, b * KT + k + 1)
                    if k == 0:
                        after(act, s_ctx_saved, 16 * b)
                    nc.scalar.copy(ctxT[:, 0, k, :], pk[k % 2][:, 0:LCTX]).then_inc(s_ctx_hi, 1)
                act.wait_ge(s_xn_turned, b + 1)
                nc.scalar.copy(xnT[:, 0, :, :].rearrange("p k s -> p (k s)"), pq[:, 0:KT * S]).then_inc(s_xn_hi, 1)

            def act_project(act, b, h, score):
                n = b * H + h
                act.wait_ge(s_k_made, n + 1)
                after(act, s_kq_split, n - RKQ + 1)
                after(act, s_squared, n - RKQ + 1)
                parts = [(0, N_TXT, KB, NKT, 0), (N_TXT, LCTX, KIB, NKI, 1)]
                for lo, hi, bias, _, _ in parts:
                    last = nc.scalar.activation(kq[:, h % RKQ, lo:hi], pk[h % 2][:, lo:hi], ACT.Identity,
                                                bias=vec(bias, h))
                last.then_inc(s_k_out, 1)
                if score:
                    act.wait_ge(s_s_made, n - H + 1)
                for lo, hi, _, scale, i in parts:
                    last = nc.scalar.activation(kT[:, h, 0, lo:hi], pk[h % 2][:, lo:hi], ACT.Identity,
                                                bias=kb_scaled[:, i, h:h + 1], scale=vec(scale, h))
                last.then_inc(s_k_hi, 1)
                act.wait_ge(s_q_made, n + 1)
                nc.scalar.activation(kq[:, h % RKQ, LCTX:LCTX + S], pq[:, 0:S], ACT.Identity,
                                     bias=vec(QB, h)).then_inc(s_q_out, 1)

            def act_exp(act, b, h):
                n = b * H + h
                act.wait_ge(s_nmax, n + 1)
                r = h % RS
                nc.scalar.activation(prob[:, r, 0:N_TXT], prob[:, r, 0:N_TXT], ACT.Exp, bias=nmx[:, r, 0:1],
                                     scale=q_scale[:, 0:1], accum_out=psum_row[:, r, 0:1])
                nc.scalar.activation(prob[:, r, N_TXT:LCTX], prob[:, r, N_TXT:LCTX], ACT.Exp, bias=nmx[:, r, 1:2],
                                     scale=q_scale[:, 0:1], accum_out=psum_row[:, r, 1:2]).then_inc(s_exp, 1)

            def act_probs_hi(act, b, h):
                n = b * H + h
                act.wait_ge(s_p_turned, n + 1)
                after(act, s_p_saved[h % 4], 16 * (b * (H // 4) + h // 4))
                nc.scalar.copy(ptb[0:CH, h % 4, 0, :], pt[h % 2][0:CH, 0:3 * S]).then_inc(s_p_hi, 1)

            def act_batch(act, b, project, score):
                if score:
                    act.wait_ge(s_rrow, b)
                    nc.scalar.copy(rrow[:, :], pm[0:S, 0:LCTX]).then_inc(s_rrow_out, 1)
                for h in range(H):
                    if not score:
                        split_ahead(act, weights_hi, h)
                    if project:
                        act_project(act, b, h, score)
                    if score:
                        act_exp(act, b - 1, h)
                    if score and h >= LAG:
                        act_probs_hi(act, b - 1, h - LAG)
                    if not project and h < W_HALF:
                        weights_hi(act, W_HALF + h)
                if project and not is_last(b):
                    act_turned(act, b + 1)
                if score:
                    for h in range(H - LAG, H):
                        act_probs_hi(act, b - 1, h)

            def split_ahead(eng, split, h):
                if h % HG == 0 and h // HG + 1 < NG:
                    for i in range(W_STAGES):
                        split(eng, (h // HG + 1) * W_STAGES + i)

            @block.scalar
            def _(act):
                act.wait_ge(s_g_in, 32)
                nc.scalar.activation(tg[:, :], g_raw[:, :], ACT.Tanh).then_inc(s_tanh, 1)
                act.wait_ge(s_vecs_turned, 1)
                nc.scalar.copy(cols[:, :], pm[:, 0:P]).then_inc(s_cols, 1)
                act.wait_ge(s_cols, 1)
                act_turned(act, 0)
                for n in range(W_STAGES):
                    weights_hi(act, n)
                act.wait_ge(s_kb_scaled, 1)
                all_batches(act, act_batch)

            def dve_norms(dve, b):
                dve.wait_ge(s_sums, b + 1)
                nc.vector.tensor_scalar(ms[0:CH, 0:3], pm[0:CH, 0:3], 1.0 / INNER, RMS_EPS, ALU.mult, ALU.add)
                nc.vector.tensor_scalar(ms[0:S, 3:4], pm[0:S, 3:4], 1.0 / INNER, RMS_EPS, ALU.mult, ALU.add).then_inc(s_ms, 1)
                dve.wait_ge(s_rms, b + 1)
                for c in range(3):
                    nc.vector.tensor_scalar(rdiag[:, c, :], ident[0:CH, 0:CH], rms[0:CH, c:c + 1], None,
                                            ALU.mult)
                nc.vector.tensor_scalar(q_scale[:, :], rms[0:S, 3:4], float(D) ** -0.5, None,
                                        ALU.mult).then_inc(s_rdiag, 1)

            def dve_x_stats(dve, b):
                dve.wait_ge(s_x_in, 16 * b + 16)
                nc.vector.bn_stats(stats[:, :], x_raw[:, :]).then_inc(s_ln_stats, 1)
                dve.wait_ge(s_ln_stats, b + 1)
                nc.vector.memset(pause_ln[:, :], 0.0)
                nc.vector.bn_aggr(mv[:, :], stats[:, :]).then_inc(s_ln_aggr, 1)

            def dve_x_normalise(dve, b):
                dve.wait_ge(s_ln_rstd, b + 1)
                after(dve, s_xn_turned, b)
                nc.vector.tensor_scalar(xn[:, :], x_raw[:, :], mv[:, 0:1], rstd[:, 0:1], ALU.subtract,
                                        ALU.mult).then_inc(s_xn, 1)

            def dve_turned(dve, b):
                for k in range(KT):
                    dve.wait_ge(s_ctx_hi, b * KT + k + 1)
                    nc.vector.tensor_tensor(ctxT[:, 1, k, :], pk[k % 2][:, 0:LCTX], ctxT[:, 0, k, :],
                                            ALU.subtract).then_inc(s_ctx_lo, 1)
                dve.wait_ge(s_xn_hi, b + 1)
                nc.vector.tensor_tensor(xnT[:, 1, :, :].rearrange("p k s -> p (k s)"), pq[:, 0:KT * S],
                                        xnT[:, 0, :, :].rearrange("p k s -> p (k s)"),
                                        ALU.subtract).then_inc(s_xn_lo, 1)

            def dve_scale(dve, b, h):
                n = b * H + h
                r = h % RS
                dve.wait_ge(s_s_made, n + 1)
                after(dve, s_p_turned, n - RS + 1)
                nc.vector.memset(pause[:, :], 0.0)
                nc.vector.tensor_tensor_reduce(out=prob[:, r, 0:N_TXT], in0=ps[h % 2][0:S, 0:N_TXT],
                                               in1=rrow[:, 0:N_TXT], scale=1.0, scalar=-3.0e38, op0=ALU.mult,
                                               op1=ALU.max, accum_out=mx[:, r, 0:1])
                nc.vector.tensor_tensor_reduce(out=prob[:, r, N_TXT:LCTX], in0=ps[h % 2][0:S, N_TXT:LCTX],
                                               in1=rrow[:, N_TXT:LCTX], scale=1.0, scalar=-3.0e38, op0=ALU.mult,
                                               op1=ALU.max, accum_out=mx[:, r, 1:2]).then_inc(s_s_scaled, 1)
                dve.wait_ge(s_s_scaled, n + 1)
                nc.vector.tensor_scalar(nmx[:, r, :], mx[:, r, :], q_scale[:, 0:1], -1.0, ALU.mult,
                                        ALU.mult).then_inc(s_nmax, 1)

            def dve_split(dve, b, h, score):
                n = b * H + h
                src = kq[:, h % RKQ, :]
                parts = [(kT[:, h, :, 0:N_TXT], src[:, 0:N_TXT], vec(NKT, h)),
                         (kT[:, h, :, N_TXT:LCTX], src[:, N_TXT:LCTX], vec(NKI, h)),
                         (qT[:, h, :, :], src[:, LCTX:LCTX + S], vec(NQ, h))]
                if score:
                    dve.wait_ge(s_s_made, n - H + 1)
                dve.wait_ge(s_q_out, n + 1)
                dst, v, scale = parts[2]
                nc.vector.tensor_scalar(dst[:, 0, :], v, scale, None, ALU.mult).then_inc(s_kq_hi, 1)
                dve.wait_ge(s_k_hi, n + 1)
                dve.wait_ge(s_kq_hi, n + 1)
                for dst, v, scale in parts:
                    last = nc.vector.scalar_tensor_tensor(dst[:, 1, :], v, scale, dst[:, 0, :], ALU.mult,
                                                          ALU.subtract)
                last.then_inc(s_kq_split, 1)

            def dve_normalise(dve, b, h):
                n = b * H + h
                r = h % RS
                dve.wait_ge(s_exp, n + 1)
                nc.vector.reciprocal(rcp[:, r, :], psum_row[:, r, :]).then_inc(s_rcp, 1)
                dve.wait_ge(s_rcp, n + 1)
                nc.vector.tensor_scalar(prob[:, r, 0:N_TXT], prob[:, r, 0:N_TXT], rcp[:, r, 0:1], None, ALU.mult)
                nc.vector.tensor_scalar(prob[:, r, N_TXT:LCTX], prob[:, r, N_TXT:LCTX], rcp[:, r, 1:2], None,
                                        ALU.mult).then_inc(s_p, 1)

            def dve_probs_lo(dve, b, h):
                n = b * H + h
                dve.wait_ge(s_p_hi, n + 1)
                nc.vector.tensor_tensor(ptb[0:CH, h % 4, 1, :], pt[h % 2][0:CH, 0:3 * S], ptb[0:CH, h % 4, 0, :],
                                        ALU.subtract).then_inc(s_p_lo, 1)

            def dve_batch(dve, b, project, score):
                ahead = project and not is_last(b)
                if score:
                    dve.wait_ge(s_rrow_out, b)
                for h in range(H):
                    if not score:
                        split_ahead(dve, lambda _, n: weights_lo(nc.vector, n), h)
                    if score:
                        dve_scale(dve, b - 1, h)
                    if project:
                        dve_split(dve, b, h, score)
                    if score and h >= 1:
                        dve_normalise(dve, b - 1, h - 1)
                    if score and h >= LAG:
                        dve_probs_lo(dve, b - 1, h - LAG)
                    if ahead and h == LN_AT[0]:
                        dve_x_stats(dve, b + 1)
                    if ahead and h == LN_AT[1]:
                        dve_x_normalise(dve, b + 1)
                    n = W_HALF + h
                    if not project and h < W_HALF and n % W_STAGES < W_STAGES - 1:
                        weights_lo(nc.vector, n)
                if score:
                    dve_normalise(dve, b - 1, H - 1)
                if ahead:
                    dve_turned(dve, b + 1)
                if score:
                    for h in range(H - LAG, H):
                        dve_probs_lo(dve, b - 1, h)
                if project:
                    dve_norms(dve, b)

            LN_AT = (7, 13)

            @block.vector
            def _(dve):
                dve.wait_ge(s_const, 7)
                dve_x_stats(dve, 0)
                dve_x_normalise(dve, 0)
                dve_turned(dve, 0)
                for n in range(W_STAGES):
                    weights_lo(nc.vector, n)
                dve.wait_ge(s_cols, 1)
                nc.vector.tensor_tensor(kb_scaled[:, 0, :], cols[:, KB * H:(KB + 1) * H],
                                        cols[:, NKT * H:(NKT + 1) * H], ALU.mult)
                nc.vector.tensor_tensor(kb_scaled[:, 1, :], cols[:, KIB * H:(KIB + 1) * H],
                                        cols[:, NKI * H:(NKI + 1) * H], ALU.mult).then_inc(s_kb_scaled, 1)
                all_batches(dve, dve_batch)

        s2 = {}

        def sem2(name):
            s2[name] = sem(name)
            return s2[name]
        s_rem_in = sem2("s_rem_in")
        s_rem_turned = sem2("s_rem_turned")
        s_rem_hi = sem2("s_rem_hi")
        s_rem_lo = sem2("s_rem_lo")
        s_vrem_made = sem2("s_vrem_made")
        s_vrem_hi = sem2("s_vrem_hi")
        s_vrem_lo = sem2("s_vrem_lo")
        s_vrem_saved = sem2("s_vrem_saved")
        s_gw_in = sem2("s_gw_in")
        s_gw_turned = sem2("s_gw_turned")
        s_gwT = sem2("s_gwT")
        s_vb_rep = sem2("s_vb_rep")
        s_ob_made = sem2("s_ob_made")
        s_ob_in = sem2("s_ob_in")
        s_ob_sum = sem2("s_ob_sum")
        s_obrow = sem2("s_obrow")
        s_ctxT_in = sem2("s_ctxT_in")
        s_p_in = [sem2(f"s_p_in{i}") for i in range(2)]
        s_vrem_in = [sem2(f"s_vrem_in{i}") for i in range(2)]
        s_v_made = sem2("s_v_made")
        s_v_hi = sem2("s_v_hi")
        s_v_lo = sem2("s_v_lo")
        s_att = sem2("s_att")
        s_att_hi = sem2("s_att_hi")
        s_att_lo = sem2("s_att_lo")
        s_o_made = sem2("s_o_made")
        s_xr_in = sem2("s_xr_in")
        s_xr = sem2("s_xr")
        s_x2 = sem2("s_x2")
        s_x2_saved = sem2("s_x2_saved")
        s_x2_stats = sem2("s_x2_stats")
        s_x2_aggr = sem2("s_x2_aggr")
        s_x2_var = sem2("s_x2_var")
        s_x2_rstd = sem2("s_x2_rstd")
        s_xn2 = sem2("s_xn2")
        s_xd_hi = sem2("s_xd_hi")
        s_xd = sem2("s_xd")
        s_xn2_turned = sem2("s_xn2_turned")
        s_xn2T = sem2("s_xn2T")
        s_logits = sem2("s_logits")
        s_lmax = sem2("s_lmax")
        s_lnmax = sem2("s_lnmax")
        s_lexp = sem2("s_lexp")
        s_route = sem2("s_route")
        s_sel = sem2("s_sel")
        s_pos = sem2("s_pos")
        s_idx = sem2("s_idx")
        s_dispatched = sem2("s_dispatched")
        ROUTE_STEPS = 9

        with nc.Block() as block, ExitStack() as ph2, ExitStack() as ps2:
            ctxT = sb(ph2, "ctxT2", [P, 2, KT, LCTX], BF16)
            rem_raw = sb(ph2, "rem_raw", [B * NREM, DIM], F32)
            remT = sb(ph2, "remT", [P, 2, KT * B * NREM], BF16)
            vrem = sb(ph2, "vrem", [B * NREM, NG, 2, 512], BF16)
            gw_raw = sb(ph2, "gw_raw", [E, DIM], F32)
            gwT = sb(ph2, "gwT", [P, KT, E], F32)
            vb_rep = sb(ph2, "vb_rep", [P, 2, H, S], BF16)
            vb_sum = sb(ph2, "vb_sum", [P, H], F32)
            obrow = sb(ph2, "obrow", [S, DIM], F32)
            v_sb = sb(ph2, "v_sb", [CH, 2, 3, 2, 512], BF16)
            pin = sb(ph2, "pin", [P, 2, HG, 2, 3 * S], BF16)
            outT = sb(ph2, "outT", [P, H, 2, S], BF16)
            xr_in = sb(ph2, "xr_in", [S, DIM], F32)
            xr = sb(ph2, "xr", [S, DIM], F32)
            x2 = sb(ph2, "x2", [S, DIM], F32)
            stats2 = sb(ph2, "stats2", [S, 6], F32)
            mv2 = sb(ph2, "mv2", [S, 2], F32)
            rstd2 = sb(ph2, "rstd2", [S, 1], F32)
            xn2 = sb(ph2, "xn2", [S, DIM], F32)
            xd = sb(ph2, "xd", [S, ROW], U16)
            xd_hi = xd[:, 0:DIM].bitcast(BF16).rearrange("s (c p) -> s c p", c=KT)
            xd_lo = xd[:, DIM:2 * DIM].bitcast(BF16).rearrange("s (c p) -> s c p", c=KT)
            xd_w = xd[:, 2 * DIM:2 * DIM + 2 * E].bitcast(F32)
            xd_tok = xd[:, ROW - 4:ROW - 2].bitcast(F32)
            tokf = sb(ph2, "tokf", [S, 1], F32)
            xn2T = sb(ph2, "xn2T", [P, KT * S], F32)
            lmax = sb(ph2, "lmax", [S, 2], F32)
            ex = sb(ph2, "ex", [S, E], F32)
            top8 = sb(ph2, "top8", [S, TOPK], F32)
            left = sb(ph2, "left", [S, E], F32)
            selb = sb(ph2, "selb", [S, E], BF16)
            cumb = sb(ph2, "cumb", [S, E], BF16)
            wsum = sb(ph2, "wsum", [S, 3], F32)
            slot = sb(ph2, "slot", [S, E], F32)
            val = sb(ph2, "val", [S, E], F32)
            key = sb(ph2, "key", [S, E], F32)
            key8 = sb(ph2, "key8", [S, TOPK], F32)
            none8 = sb(ph2, "none8", [S, TOPK], F32)
            idx = sb(ph2, "idx", [S, TOPK], U32)
            pause = sb(ph2, "pause2", [1, 1], F32)
            pool_pause = sb(ph2, "pool_pause", [1, 2], F32)

            def pb2(name, shape, dt=F32):
                return ps2.enter_context(nc.psum_tensor(name, shape, dt))
            pv = [pb2(f"pv{i}", [P, 512]) for i in range(2)]
            pa = [pb2(f"pa{i}", [P, 512]) for i in range(2)]
            po = pb2("po", [P, 512])
            pg = pb2("pg", [P, 512])
            pl = pb2("pl", [P, 512])
            pp = pb2("pp", [P, 512])
            NR = B * NREM

            def load_group(sp, b, g):
                n = b * NG + g
                after(sp, s_att, n - 1)
                sp.dma_start(pin[:, g % 2, :, :, :].rearrange("p h a s -> p (h a s)"), pt_d[n]).then_inc(s_p_in[g % 2], 16)
                sp.dma_start(v_sb[N_TXT:CH, g % 2, 0, :, :].rearrange("p a n -> p (a n)"),
                             vrem_d[b, :, g, :]).then_inc(s_vrem_in[g % 2], 16)

            def load_values(sp, b):
                after(sp, s_v_made, 12 * b)
                sp.dma_start(ctxT[:, :, :, :].rearrange("p a k l -> p (a k l)"), ctxT_d[b]).then_inc(s_ctxT_in, 16)

            def save_route(sp, b):
                sp.wait_ge(s_x2, b + 1)
                sp.dma_start(acc_d[0:TOKENS, :].rearrange("(b s) n -> b s n", b=B)[b], x2[:, :]).then_inc(s_x2_saved, 16)

            def load_x(sp, b):
                after(sp, s_xr, b)
                sp.dma_start(xr_in[:, :], x[b]).then_inc(s_xr_in, 16)

            def sp_batch(sp, b, values, route):
                if values:
                    load_values(sp, b)
                    load_group(sp, b, 0)
                    load_group(sp, b, 1)
                if route:
                    load_x(sp, b - 1)
                if values:
                    load_group(sp, b, 2)
                    load_group(sp, b, 3)
                if route:
                    save_route(sp, b - 1)

            @block.sync
            def _(sp):
                for b in range(B):
                    sp.dma_start(rem_raw[b * NREM:(b + 1) * NREM, :], ctx_in[b, 2 * CH:N_IMG, :]).then_inc(s_rem_in, 16)
                sp.dma_start(gw_raw[:, :], gate_w).then_inc(s_gw_in, 16)
                sp.dma_start(obrow[:, :], o_b.rearrange("(a n) -> a n", a=1).broadcast_to([S, DIM])).then_inc(s_ob_in, 16)
                sp.wait_ge(s_vrem_lo, NG)
                sp.dma_start(vrem_d.rearrange("b r g n -> (b r) (g n)"),
                             vrem[:, :, :, :].rearrange("p g a n -> p (g a n)")).then_inc(s_vrem_saved, 16)
                sp.wait_ge(s_vrem_saved, 16)
                sp_batch(sp, 0, True, False)
                sp_batch(sp, 1, True, True)
                with sp.Fori(2, B) as b:
                    sp_batch(sp, b, True, True)
                sp_batch(sp, B, False, True)
                sp.wait_ge(s_x2_saved, 16 * B)

            def project_values(pe, b, g):
                for c in range(3):
                    n = 3 * (b * NG + g) + c
                    rows = N_TXT if c == 0 else CH
                    w = V_SLOT if c == 0 else VI_SLOT
                    after(pe, s_v_lo, n - 1)
                    for k in range(KT):
                        mm = split_matmul(pe, pv[(3 * g + c) % 2][0:rows, :],
                                          (ctxT[:, 0, k, c * CH:c * CH + rows], ctxT[:, 1, k, c * CH:c * CH + rows]),
                                          (w_hi[w][:, k, g * 512:(g + 1) * 512], w_lo[w][:, k, g * 512:(g + 1) * 512]),
                                          k == 0, k == KT - 1)
                    mm.then_inc(s_v_made, 1)

            def attend(pe, b, g):
                n = b * NG + g
                pe.wait_ge(s_v_lo, 3 * n + 3)
                pe.wait_ge(s_p_in[g % 2], 16 * (b * (NG // 2) + g // 2 + 1))
                pe.wait_ge(s_vrem_in[g % 2], 16 * (b * (NG // 2) + g // 2 + 1))
                after(pe, s_att_lo, n - 1)
                for hh in range(HG):
                    for c in range(3):
                        mm = split_matmul(pe, pa[g % 2][:, hh * S:(hh + 1) * S],
                                          (v_sb[:, g % 2, c, 0, hh * D:(hh + 1) * D],
                                           v_sb[:, g % 2, c, 1, hh * D:(hh + 1) * D]),
                                          (pin[0:CH, g % 2, hh, 0, c * S:(c + 1) * S],
                                           pin[0:CH, g % 2, hh, 1, c * S:(c + 1) * S]), c == 0, c == 2)
                mm.then_inc(s_att, 1)

            def project_out(pe, b):
                pe.wait_ge(s_att_lo, NG * b + NG)
                after(pe, s_x2, b)
                for h in range(H):
                    mm = split_matmul(pe, po[0:S, :], (outT[:, h, 0, :], outT[:, h, 1, :]),
                                      (w_hi[O_SLOT][:, h // HG, (h % HG) * 512:(h % HG + 1) * 512],
                                       w_lo[O_SLOT][:, h // HG, (h % HG) * 512:(h % HG + 1) * 512]), h == 0, h == H - 1)
                mm.then_inc(s_o_made, 1)

            def turn_route(pe, b):
                pe.wait_ge(s_xn2, b + 1)
                after(pe, s_xn2T, b)
                for k in range(KT):
                    mm = pe.transpose(pg[:, k * S:(k + 1) * S], xn2[:, k * P:(k + 1) * P], ident[0:S, 0:S])
                mm.then_inc(s_xn2_turned, 1)

            def make_logits(pe, b):
                pe.wait_ge(s_xn2T, b + 1)
                after(pe, s_lexp, b)
                for k in range(KT):
                    mm = pe.matmul(pl[0:S, 0:E], xn2T[:, k * S:(k + 1) * S], gwT[:, k, :], start=k == 0,
                                   stop=k == KT - 1)
                mm.then_inc(s_logits, 1)

            def make_positions(pe, b):
                pe.wait_ge(s_sel, b + 1)
                pe.matmul(pp[0:S, 0:E], trib[:, :], selb[:, :], start=True, stop=False)
                pe.matmul(pp[0:S, 0:E], onesb[:, :], cumb[:, :], start=False, stop=True).then_inc(s_pos, 1)

            def pe_batch2(pe, b, values, route):
                if values:
                    pe.wait_ge(s_ctxT_in, 16 * b + 16)
                    project_values(pe, b, 0)
                if route:
                    project_out(pe, b - 1)
                if values:
                    project_values(pe, b, 1)
                    attend(pe, b, 0)
                if route:
                    turn_route(pe, b - 1)
                if values:
                    project_values(pe, b, 2)
                if route:
                    make_logits(pe, b - 1)
                if values:
                    attend(pe, b, 1)
                    project_values(pe, b, 3)
                if route:
                    make_positions(pe, b - 1)
                if values:
                    attend(pe, b, 2)
                    attend(pe, b, 3)

            @block.tensor
            def _(pe):
                pe.wait_ge(s_rem_in, 16 * B)
                for k in range(KT):
                    mm = pe.transpose(pg[:, k * NR:(k + 1) * NR], rem_raw[:, k * P:(k + 1) * P], ident[0:NR, 0:NR])
                mm.then_inc(s_rem_turned, 1)
                pe.wait_ge(s_gw_in, 16)
                for k in range(KT):
                    mm = pe.transpose(pl[:, k * E:(k + 1) * E], gw_raw[:, k * P:(k + 1) * P], ident[0:E, 0:E])
                mm.then_inc(s_gw_turned, 1)
                pe.wait_ge(s_rem_lo, 1)
                for g in range(NG):
                    after(pe, s_vrem_lo, g - 1)
                    for k in range(KT):
                        mm = split_matmul(pe, pv[g % 2][0:NR, :],
                                          (remT[:, 0, k * NR:(k + 1) * NR], remT[:, 1, k * NR:(k + 1) * NR]),
                                          (w_hi[VI_SLOT][:, k, g * 512:(g + 1) * 512],
                                           w_lo[VI_SLOT][:, k, g * 512:(g + 1) * 512]), k == 0, k == KT - 1)
                    mm.then_inc(s_vrem_made, 1)
                pe.wait_ge(s_vb_rep, 1)
                for h in range(H):
                    mm = split_matmul(pe, po[0:S, :], (vb_rep[:, 0, h, :], vb_rep[:, 1, h, :]),
                                      (w_hi[O_SLOT][:, h // HG, (h % HG) * 512:(h % HG + 1) * 512],
                                       w_lo[O_SLOT][:, h // HG, (h % HG) * 512:(h % HG + 1) * 512]), h == 0, h == H - 1)
                mm.then_inc(s_ob_made, 1)
                pe.wait_ge(s_vrem_lo, NG)
                pe.wait_ge(s_gwT, 1)
                pe.wait_ge(s_obrow, 1)
                pe_batch2(pe, 0, True, False)
                pe_batch2(pe, 1, True, True)
                with pe.Fori(2, B) as b:
                    pe_batch2(pe, b, True, True)
                pe_batch2(pe, B, False, True)

            def act_values(act, b, g):
                for c in range(3):
                    n = 3 * (b * NG + g) + c
                    rows = N_TXT if c == 0 else CH
                    act.wait_ge(s_v_made, n + 1)
                    nc.scalar.copy(v_sb[0:rows, g % 2, c, 0, :], pv[(3 * g + c) % 2][0:rows, :]).then_inc(s_v_hi, 1)

            def act_attend(act, b, g):
                act.wait_ge(s_att, b * NG + g + 1)
                nc.scalar.copy(outT[:, g * HG:(g + 1) * HG, 0, :],
                               pa[g % 2][:, 0:HG * S].rearrange("p (h s) -> p h s", h=HG)).then_inc(s_att_hi, 1)

            def act_batch2(act, b, values, route):
                if values:
                    act_values(act, b, 0)
                    act_values(act, b, 1)
                    act_attend(act, b, 0)
                if route:
                    act.wait_ge(s_xn2_turned, b)
                    nc.scalar.copy(xn2T[:, :], pg[:, 0:KT * S]).then_inc(s_xn2T, 1)
                if values:
                    act_values(act, b, 2)
                if route:
                    act.wait_ge(s_lnmax, b)
                    nc.scalar.activation(ex[:, :], pl[0:S, 0:E], ACT.Exp, bias=lmax[:, 1:2]).then_inc(s_lexp, 1)
                if values:
                    act_attend(act, b, 1)
                    act_values(act, b, 3)
                    act_attend(act, b, 2)
                    act_attend(act, b, 3)

            @block.scalar
            def _(act):
                act.wait_ge(s_rem_turned, 1)
                nc.scalar.copy(remT[:, 0, :], pg[:, 0:KT * NR]).then_inc(s_rem_hi, 1)
                act.wait_ge(s_gw_turned, 1)
                nc.scalar.copy(gwT[:, :, :].rearrange("p k e -> p (k e)"), pl[:, 0:KT * E]).then_inc(s_gwT, 1)
                for g in range(NG):
                    act.wait_ge(s_vrem_made, g + 1)
                    nc.scalar.copy(vrem[:, g, 0, :], pv[g % 2][0:NR, :]).then_inc(s_vrem_hi, 1)
                act_batch2(act, 0, True, False)
                act_batch2(act, 1, True, True)
                with act.Fori(2, B) as b:
                    act_batch2(act, b, True, True)
                act_batch2(act, B, False, True)

            def dve_values(dve, b, g):
                for c in range(3):
                    n = 3 * (b * NG + g) + c
                    rows = N_TXT if c == 0 else CH
                    dve.wait_ge(s_v_hi, n + 1)
                    nc.vector.tensor_tensor(v_sb[0:rows, g % 2, c, 1, :], pv[(3 * g + c) % 2][0:rows, :],
                                            v_sb[0:rows, g % 2, c, 0, :], ALU.subtract).then_inc(s_v_lo, 1)

            def dve_attend(dve, b, g):
                dve.wait_ge(s_att_hi, b * NG + g + 1)
                nc.vector.tensor_tensor(outT[:, g * HG:(g + 1) * HG, 1, :],
                                        pa[g % 2][:, 0:HG * S].rearrange("p (h s) -> p h s", h=HG),
                                        outT[:, g * HG:(g + 1) * HG, 0, :], ALU.subtract).then_inc(s_att_lo, 1)

            def dve_residual(dve, b):
                dve.wait_ge(s_o_made, b + 1)
                dve.wait_ge(s_xr, b + 1)
                after(dve, s_x2_saved, 16 * b)
                nc.vector.scalar_tensor_tensor(x2[:, :], po[0:S, :], tg[0:S, 0:1], xr[:, :], ALU.mult,
                                               ALU.add).then_inc(s_x2, 1)
                dve.wait_ge(s_x2, b + 1)
                nc.vector.bn_stats(stats2[:, :], x2[:, :]).then_inc(s_x2_stats, 1)
                dve.wait_ge(s_x2_stats, b + 1)
                nc.vector.memset(pause[:, :], 0.0)
                nc.vector.bn_aggr(mv2[:, :], stats2[:, :]).then_inc(s_x2_aggr, 1)

            def dve_normalise2(dve, b):
                dve.wait_ge(s_x2_rstd, b + 1)
                after(dve, s_xn2_turned, b)
                nc.vector.tensor_scalar(xn2[:, :], x2[:, :], mv2[:, 0:1], rstd2[:, 0:1], ALU.subtract,
                                        ALU.mult).then_inc(s_xn2, 1)
                dve.wait_ge(s_xn2, b + 1)
                after(dve, s_dispatched, 16 * TOPK * b)
                by_tile = xn2[:, :].rearrange("s (p c) -> s c p", c=KT)
                nc.vector.tensor_copy(xd_hi, by_tile)
                nc.vector.tensor_copy(xd_tok, tokf[:, :]).then_inc(s_xd_hi, 1)
                dve.wait_ge(s_xd_hi, b + 1)
                nc.vector.tensor_scalar(tokf[:, :], tokf[:, :], float(S), None, ALU.add)
                nc.vector.tensor_tensor(xd_lo, by_tile, xd_hi, ALU.subtract).then_inc(s_xd, 1)

            def dve_select(dve, b):
                dve.wait_ge(s_logits, b + 1)
                nc.vector.tensor_reduce(lmax[:, 0:1], pl[0:S, 0:E], AX.X, ALU.max).then_inc(s_lmax, 1)
                dve.wait_ge(s_lmax, b + 1)
                nc.vector.tensor_scalar(lmax[:, 1:2], lmax[:, 0:1], -1.0, None, ALU.mult).then_inc(s_lnmax, 1)

            def dve_choose(dve, b, link):
                dve.wait_ge(s_lexp, b + 1)
                nc.vector.memset(pause[:, :], 0.0)
                link(nc.vector.max(top8[:, :], ex[:, :]))
                nc.vector.memset(pause[:, :], 0.0)
                link(nc.vector.match_replace(left[:, :], top8[:, :], ex[:, :], -1.0))
                nc.vector.tensor_reduce(wsum[:, 0:1], top8[:, :], AX.X, ALU.add)
                if not (isinstance(b, int) and b == 0):
                    dve.wait_ge(s_pos, b)
                    link(nc.vector.tensor_tensor(cumb[:, :], cumb[:, :], selb[:, :], ALU.add))
                else:
                    link(nc.vector.memset(cumb[:, :], 0.0))
                nc.vector.tensor_scalar(selb[:, :], left[:, :], 0.0, None, ALU.is_lt).then_inc(s_sel, 1)
                link(nc.vector.reciprocal(wsum[:, 1:2], wsum[:, 0:1]))
                link(nc.vector.tensor_scalar(wsum[:, 2:3], wsum[:, 1:2], tg[0:S, 1:2], None, ALU.mult))

            def dve_slots(dve, b, link):
                dve.wait_ge(s_pos, b + 1)
                nc.vector.tensor_tensor(slot[:, :], pp[0:S, 0:E], slot1[:, :], ALU.add)
                link(nc.vector.scalar_tensor_tensor(val[:, :], pp[0:S, 0:E], float(CAP), selb[:, :], ALU.is_lt, ALU.mult))
                nc.vector.scalar_tensor_tensor(xd_w, ex[:, :], wsum[:, 2:3], val[:, :], ALU.mult, ALU.mult)
                link(nc.vector.tensor_tensor(key[:, :], slot[:, :], val[:, :], ALU.mult))
                nc.vector.memset(pause[:, :], 0.0)
                link(nc.vector.max(key8[:, :], key[:, :]))
                link(nc.vector.tensor_scalar(none8[:, :], key8[:, :], 0.0, float(SLOTS + 1), ALU.is_equal, ALU.mult))
                nc.vector.scalar_tensor_tensor(idx[:, :], key8[:, :], -1.0, none8[:, :], ALU.add, ALU.add).then_inc(s_idx, 1)

            def linker(dve, b):
                count = [0]

                def link(ins):
                    count[0] += 1
                    assert count[0] <= ROUTE_STEPS
                    ins.then_inc(s_route, 1)
                    dve.wait_ge(s_route, b * ROUTE_STEPS + count[0])
                return link, count

            def dve_batch2(dve, b, values, route):
                if values:
                    dve_values(dve, b, 0)
                if route:
                    dve_residual(dve, b - 1)
                if values:
                    dve_values(dve, b, 1)
                if route:
                    dve_normalise2(dve, b - 1)
                if values:
                    dve_attend(dve, b, 0)
                    dve_values(dve, b, 2)
                if route:
                    dve_select(dve, b - 1)
                if values:
                    dve_attend(dve, b, 1)
                if route:
                    link, count = linker(dve, b - 1)
                    dve_choose(dve, b - 1, link)
                if values:
                    dve_values(dve, b, 3)
                if route:
                    dve_slots(dve, b - 1, link)
                    assert count[0] == ROUTE_STEPS
                if values:
                    dve_attend(dve, b, 2)
                    dve_attend(dve, b, 3)

            @block.vector
            def _(dve):
                nc.vector.memset(xd[:, ROW - 4:ROW], 0).then_inc(s_ob_sum, 1)
                nc.vector.tensor_copy(tokf[:, :], tok1[0:S, :]).then_inc(s_ob_sum, 1)
                nc.vector.tensor_tensor(vb_sum[:, :], cols[:, VB * H:(VB + 1) * H], cols[:, VIB * H:(VIB + 1) * H],
                                        ALU.add).then_inc(s_ob_sum, 1)
                dve.wait_ge(s_ob_sum, 3)
                vb_wide = vb_sum[:, :].unsqueeze(2).broadcast_to([P, H, S])
                nc.vector.tensor_copy(vb_rep[:, 0, :, :], vb_wide).then_inc(s_ob_sum, 1)
                dve.wait_ge(s_ob_sum, 4)
                nc.vector.tensor_tensor(vb_rep[:, 1, :, :], vb_wide, vb_rep[:, 0, :, :], ALU.subtract).then_inc(s_vb_rep, 1)
                dve.wait_ge(s_rem_hi, 1)
                nc.vector.tensor_tensor(remT[:, 1, :], pg[:, 0:KT * NR], remT[:, 0, :], ALU.subtract).then_inc(s_rem_lo, 1)
                for g in range(NG):
                    dve.wait_ge(s_vrem_hi, g + 1)
                    nc.vector.tensor_tensor(vrem[:, g, 1, :], pv[g % 2][0:NR, :], vrem[:, g, 0, :],
                                            ALU.subtract).then_inc(s_vrem_lo, 1)
                dve.wait_ge(s_ob_made, 1)
                dve.wait_ge(s_ob_in, 16)
                nc.vector.tensor_tensor(obrow[:, :], po[0:S, :], obrow[:, :], ALU.add).then_inc(s_ob_sum, 1)
                dve.wait_ge(s_ob_sum, 5)
                nc.vector.tensor_scalar(obrow[:, :], obrow[:, :], tg[0:S, 0:1], None, ALU.mult).then_inc(s_obrow, 1)
                dve_batch2(dve, 0, True, False)
                dve_batch2(dve, 1, True, True)
                with dve.Fori(2, B) as b:
                    dve_batch2(dve, b, True, True)
                dve_batch2(dve, B, False, True)

            def pool_route(pool, b):
                pool.wait_ge(s_xr_in, 16 * b + 16)
                after(pool, s_x2, b)
                nc.gpsimd.tensor_tensor(xr[:, :], xr_in[:, :], obrow[:, :], ALU.add).then_inc(s_xr, 1)
                pool.wait_ge(s_x2_aggr, b + 1)
                nc.gpsimd.tensor_tensor(rstd2[:, :], mv2[:, 1:2], ln_eps[0:S, :], ALU.add).then_inc(s_x2_var, 1)
                pool.wait_ge(s_x2_var, b + 1)
                nc.gpsimd.tensor_tensor(rstd2[:, :], rstd2[:, :], mhalf[0:S, 0:1], ALU.pow).then_inc(s_x2_rstd, 1)
                pool.wait_ge(s_xd, b + 1)
                pool.wait_ge(s_idx, b + 1)
                nc.gpsimd.tensor_tensor(pool_pause[:, 0:1], mhalf[0:1, 0:1], mhalf[0:1, 1:2], ALU.add)
                for k in range(TOPK):
                    nc.gpsimd.indirect_dma_start(
                        xin_d, bass.IndirectOffsetOnAxis(ap=idx[:, k:k + 1], axis=0),
                        xd[:, :], None,
                        bounds_check=SLOTS - 1, oob_is_err=False).then_inc(s_dispatched, 16)

            @block.gpsimd
            def _(pool):
                pool.wait_ge(s_obrow, 1)
                pool_route(pool, 0)
                with pool.Fori(1, B) as b:
                    pool_route(pool, b)
                pool.wait_ge(s_dispatched, 16 * TOPK * B)

    NRAW = 4
    s_ew_in = [sem(f"s_ew_in{i}") for i in range(NRAW)]
    s_rows_in = [sem(f"s_rows_in{i}") for i in range(4)]
    s_gu_hi = sem("s_gu_hi")
    s_gu_lo = sem("s_gu_lo")
    s_d_hi = sem("s_d_hi")
    s_d_lo = sem("s_d_lo")
    s_rows_turned = sem("s_rows_turned")
    s_rowsT = sem("s_rowsT")
    s_gu_made = sem("s_gu_made")
    s_silu = sem("s_silu")
    s_hid = sem("s_hid")
    s_hid_turned = sem("s_hid_turned")
    s_hid_hi = sem("s_hid_hi")
    s_hid_lo = sem("s_hid_lo")
    s_y_made = sem("s_y_made")
    s_y_out = sem("s_y_out")
    s_empty = sem("s_empty")
    s_target = sem("s_target")
    s_y_added = sem("s_y_added")
    s_pause = sem("s_pause")
    s_out = sem("s_out")
    with nc.Block() as block, ExitStack() as ph3, ExitStack() as ps3:
        raw_gu = sb(ph3, "raw_gu", [P, NRAW, KT, 2 * FF], F32)
        raw_d = sb(ph3, "raw_d", [FC, NRAW, FT * DIM], F32)
        gu = sb(ph3, "gu", [P, 2, 2, KT, 2 * FF], BF16)
        dn = sb(ph3, "dn", [FC, NRAW, 2, FT * DIM], BF16)
        rows = sb(ph3, "rows", [P, NRAW, ROW], U16)
        empty = sb(ph3, "empty", [P, 1], F32)
        target = sb(ph3, "target", [P, NRAW, 1], U32)
        w_slot = sb(ph3, "w_slot", [P, NRAW, 1], F32)
        pool_pause3 = sb(ph3, "pool_pause3", [1, 1], F32)
        rowsT = sb(ph3, "rowsT", [P, 2, 2 * KT, P], BF16)
        sg = sb(ph3, "sg", [P, FF], F32)
        hid = sb(ph3, "hid", [P, 2, FF], F32)
        hidT = sb(ph3, "hidT", [FC, 2, FT, P], BF16)
        ybuf = sb(ph3, "ybuf", [P, NRAW, DIM], F32)

        def pb3(name, shape, dt=F32):
            return ps3.enter_context(nc.psum_tensor(name, shape, dt))
        px = [pb3(f"px{i}", [P, 2 * KT, P], BF16) for i in range(2)]
        pgu = [pb3(f"pgu{i}", [P, 512]) for i in range(2)]
        ph = [pb3(f"ph{i}", [P, 512]) for i in range(2)]
        py = [pb3(f"py{i}", [P, 512]) for i in range(2)]

        UNROLL = 4
        FIRST = 3
        LAST = E - 2
        assert (LAST - FIRST + 1) % UNROLL == 0

        def count_of(e_base, j, size):
            if isinstance(e_base, int):
                return j // size + 1
            return e_base * (UNROLL // size) + (j // size + 1)

        def walk(eng, body):
            def turn(i, j):
                body(lambda a, off=0: (i * UNROLL + j + off) * a if isinstance(i, int) else i * (UNROLL * a) + (j + off) * a,
                     lambda size, off=0: count_of(i, j + off, size), j, not isinstance(i, int))
            for e in range(FIRST):
                turn(0, e)
            with eng.Fori(0, (LAST - FIRST + 1) // UNROLL) as i:
                for j in range(FIRST, FIRST + UNROLL):
                    turn(i, j)
            for e in range(LAST + 1, E + 1):
                turn(0, e)

        @block.sync
        def _(sp):
            def load_expert(e, n, c, j):
                after(sp, s_gu_lo, n(1, -NRAW + 1))
                after(sp, s_d_lo, n(1, -NRAW + 1))
                r = j % NRAW
                sp.dma_start(raw_gu[:, r, :, 0:FF], wg[e].rearrange("(p c) i -> p c i", c=KT)).then_inc(s_ew_in[r], 16)
                sp.dma_start(raw_gu[:, r, :, FF:2 * FF], wu[e].rearrange("(p c) i -> p c i", c=KT)).then_inc(s_ew_in[r], 16)
                sp.dma_start(raw_d[:, r, :], wd[e].rearrange("(p c) n -> p (c n)", c=FT)).then_inc(s_ew_in[r], 16)
                after(sp, s_target, n(1, -NRAW + 1))
                after(sp, s_rows_turned, n(1, -NRAW + 1))
                sp.dma_start(rows[:, r, :], xin_d.rearrange("(e c) n -> e c n", c=CAP)[e]).then_inc(s_rows_in[r], 16)

            AHEAD = 3

            def body(n, c, j, looped):
                e = n(1)
                if looped or e + AHEAD < E:
                    load_expert(n(1, AHEAD), lambda a, off=0: n(a, AHEAD + off), None, j + AHEAD)
            for e in range(AHEAD):
                load_expert(e, lambda a, off=0: (e + off) * a, None, e)
            for e in range(FIRST):
                body(lambda a, off=0: (e + off) * a, None, e, False)
            turns = (E - AHEAD - FIRST) // UNROLL
            with sp.Fori(0, turns) as i:
                for j in range(FIRST, FIRST + UNROLL):
                    body(lambda a, off=0: i * (UNROLL * a) + (j + off) * a, None, j, True)
            for e in range(FIRST + turns * UNROLL, E + 1):
                body(lambda a, off=0: (e + off) * a, None, e, False)
            sp.wait_ge(s_y_added, 16 * E)
            sp.dma_start(out.rearrange("b s n -> (b s) n"), acc_d[0:TOKENS, :]).then_inc(s_out, 16)
            sp.wait_ge(s_out, 16)

        @block.tensor
        def _(pe):
            def turn_rows(n, c, j):
                pe.wait_ge(s_rows_in[j % NRAW], c * 16)
                after(pe, s_rowsT, n(1, -1))
                for q in range(2 * KT):
                    mm = pe.transpose(px[j % 2][:, q, :], rows[:, j % NRAW, q * P:(q + 1) * P].bitcast(BF16), identb[:, :])
                mm.then_inc(s_rows_turned, 1)

            def body(n, c, j, looped):
                e = n(1)
                here, before, ahead = looped or e < E, looped or e >= 1, looped or e + 1 < E
                if not looped and e == 0:
                    turn_rows(n, c(NRAW), j)
                if before:
                    pe.wait_ge(s_hid, n(1))
                    after(pe, s_hid_lo, n(1, -2))
                    for q in range(FT):
                        hv = hid[:, (j - 1) % 2, :].rearrange("s (p c) -> s c p", c=FT)
                        mm = pe.transpose(ph[(j - 1) % 2][0:FC, q * P:(q + 1) * P], hv[:, q, :], ident[:, :])
                    mm.then_inc(s_hid_turned, 1)
                if ahead:
                    turn_rows(lambda a, off=0: n(a, 1 + off), c(NRAW, 1), j + 1)
                if here:
                    pe.wait_ge(s_rowsT, n(1, 1))
                    pe.wait_ge(s_gu_lo, n(1, 1))
                    after(pe, s_hid, n(1, -1))
                    for k in range(KT):
                        mm = split_matmul(pe, pgu[j % 2][:, 0:2 * FF], (rowsT[:, j % 2, k, :], rowsT[:, j % 2, KT + k, :]),
                                          (gu[:, j % 2, 0, k, :], gu[:, j % 2, 1, k, :]), k == 0, k == KT - 1)
                    mm.then_inc(s_gu_made, 1)
                if before:
                    p = (j - 1) % 2
                    pe.wait_ge(s_hid_lo, n(1))
                    pe.wait_ge(s_d_lo, n(1))
                    after(pe, s_y_out, n(1, -2))
                    for q in range(FT):
                        mm = split_matmul(pe, py[p][:, :], (hidT[:, 0, q, :], hidT[:, 1, q, :]),
                                          (dn[:, (j - 1) % NRAW, 0, q * DIM:(q + 1) * DIM],
                                           dn[:, (j - 1) % NRAW, 1, q * DIM:(q + 1) * DIM]),
                                          q == 0, q == FT - 1)
                    mm.then_inc(s_y_made, 1)
            walk(pe, body)

        @block.scalar
        def _(act):
            def body(n, c, j, looped):
                e = n(1)
                here, before, ahead = looped or e < E, looped or e >= 1, looped or e + 1 < E

                def hi(off):
                    r, p = (j + off) % NRAW, (j + off) % 2
                    act.wait_ge(s_ew_in[r], 48 * c(NRAW, off))
                    after(act, s_gu_made, n(1, off - 1))
                    nc.scalar.copy(gu[:, p, 0, :, :].rearrange("p k n -> p (k n)"),
                                   raw_gu[:, r, :, :].rearrange("p k n -> p (k n)")).then_inc(s_gu_hi, 1)

                def turned(off):
                    p = (j + off) % 2
                    act.wait_ge(s_rows_turned, n(1, off + 1))
                    after(act, s_gu_made, n(1, off - 1))
                    nc.scalar.copy(rowsT[:, p, :, :], px[p][:, :, :]).then_inc(s_rowsT, 1)
                if not looped and e == 0:
                    turned(0)
                    hi(0)
                if before:
                    act.wait_ge(s_hid_turned, n(1))
                    after(act, s_y_made, n(1, -1))
                    nc.scalar.copy(hidT[:, 0, :, :], ph[(j - 1) % 2][0:FC, 0:FT * P].rearrange("p (c s) -> p c s", c=FT)).then_inc(s_hid_hi, 1)
                if ahead:
                    hi(1)
                    turned(1)
                if here:
                    act.wait_ge(s_gu_made, n(1, 1))
                    after(act, s_hid, n(1))
                    nc.scalar.activation(sg[:, :], pgu[j % 2][:, 0:FF], ACT.Silu).then_inc(s_silu, 1)
            walk(act, body)

        @block.vector
        def _(dve):
            def body(n, c, j, looped):
                e = n(1)
                here, before, ahead = looped or e < E, looped or e >= 1, looped or e + 1 < E

                def lo(off):
                    r, p = (j + off) % NRAW, (j + off) % 2
                    dve.wait_ge(s_gu_hi, n(1, off + 1))
                    nc.vector.tensor_tensor(gu[:, p, 1, :, :].rearrange("p k n -> p (k n)"),
                                            raw_gu[:, r, :, :].rearrange("p k n -> p (k n)"),
                                            gu[:, p, 0, :, :].rearrange("p k n -> p (k n)"), ALU.subtract).then_inc(s_gu_lo, 1)

                def d_hi(off):
                    r, p = (j + off) % NRAW, (j + off) % 2
                    dve.wait_ge(s_ew_in[r], 48 * c(NRAW, off))
                    after(dve, s_y_made, n(1, off - 3))
                    nc.vector.tensor_copy(dn[:, r, 0, :], raw_d[:, r, :]).then_inc(s_d_hi, 1)
                if not looped and e == 0:
                    d_hi(0)
                    lo(0)
                if before:
                    dve.wait_ge(s_hid_hi, n(1))
                    nc.vector.tensor_tensor(hidT[:, 1, :, :], ph[(j - 1) % 2][0:FC, 0:FT * P].rearrange("p (c s) -> p c s", c=FT),
                                            hidT[:, 0, :, :], ALU.subtract).then_inc(s_hid_lo, 1)
                if ahead:
                    d_hi(1)
                    lo(1)
                if here:
                    dve.wait_ge(s_rows_in[j % NRAW], 16 * c(NRAW))
                    after(dve, s_y_added, 16 * n(1, -NRAW + 1))
                    row_f = rows[:, j % NRAW, :].bitcast(F32)
                    nc.vector.tensor_copy(w_slot[:, j % NRAW, :], row_f[:, bass.ds(n(1) + DIM, 1)])
                    tok = row_f[:, ROW // 2 - 2:ROW // 2 - 1]
                    nc.vector.tensor_scalar(empty[:, :], tok, 0.0, empty_row[:, 0:1], ALU.is_equal, ALU.mult).then_inc(s_empty, 1)
                    dve.wait_ge(s_empty, n(1, 1))
                    nc.vector.scalar_tensor_tensor(target[:, j % NRAW, :], tok, -1.0, empty[:, :], ALU.add, ALU.add).then_inc(s_target, 1)
                    dve.wait_ge(s_silu, n(1, 1))
                    after(dve, s_hid_turned, n(1, -1))
                    nc.vector.tensor_tensor(hid[:, j % 2, :], sg[:, :], pgu[j % 2][:, FF:2 * FF], ALU.mult).then_inc(s_hid, 1)
                if before:
                    p = (j - 1) % 2
                    dve.wait_ge(s_y_made, n(1))
                    r = (j - 1) % NRAW
                    dve.wait_ge(s_target, n(1))
                    nc.vector.tensor_scalar(ybuf[:, r, :], py[p][:, :], w_slot[:, r, 0:1], None, ALU.mult).then_inc(s_y_out, 1)
            walk(dve, body)

        @block.gpsimd
        def _(pool):
            def body(n, c, j, looped):
                e = n(1)
                if looped or e < E:
                    r, p = j % NRAW, j % 2
                    pool.wait_ge(s_d_hi, n(1, 1))
                    nc.gpsimd.tensor_tensor(dn[:, r, 1, :], raw_d[:, r, :], dn[:, r, 0, :], ALU.subtract).then_inc(s_d_lo, 1)
                if looped or e >= 1:
                    r = (j - 1) % NRAW
                    pool.wait_ge(s_y_out, n(1))
                    after(pool, s_y_added, 16 * n(1, -1))
                    after(pool, s_pause, n(1, -1))
                    nc.gpsimd.tensor_tensor(pool_pause3[:, :], mhalf[0:1, 0:1], mhalf[0:1, 1:2], ALU.add).then_inc(s_pause, 1)
                    nc.gpsimd.indirect_dma_start(
                        acc_d, bass.IndirectOffsetOnAxis(ap=target[:, r, :], axis=0), ybuf[:, r, :], None,
                        bounds_check=TOKENS + CAP - 1, oob_is_err=True, compute_op=ALU.add).then_inc(s_y_added, 16)
            walk(pool, body)


_INS = ['x', 'ctx_2048', 'g_xattn', 'g_ffn', 'L0_xattn_q_w', 'L0_xattn_q_b', 'L0_xattn_k_w', 'L0_xattn_k_b',
        'L0_xattn_v_w', 'L0_xattn_v_b', 'L0_xattn_ki_w', 'L0_xattn_ki_b', 'L0_xattn_vi_w', 'L0_xattn_vi_b',
        'L0_xattn_o_w', 'L0_xattn_o_b', 'L0_xattn_nq_s', 'L0_xattn_nkt_s', 'L0_xattn_nki_s', 'L0_ffn_gate_w',
        'L0_ffn_wg', 'L0_ffn_wu', 'L0_ffn_wd']


def kernel(**inputs):
    import numpy as _np
    import concourse.bacc as _bacc
    from concourse import mybir as _mybir
    from concourse.bass_utils import run_bass_kernel_spmd as _run

    nc = _bacc.Bacc("TRN2", target_bir_lowering=False, num_devices=1)
    arrays, args = {}, []
    for name in _INS:
        a = _np.ascontiguousarray(inputs[name])
        arrays[f"in_{name}"] = a
        args.append(nc.dram_tensor(f"in_{name}", a.shape, _mybir.dt.from_np(a.dtype), kind="ExternalInput").ap())
    args.append(nc.dram_tensor("out_y", (B, S, DIM), F32, kind="ExternalOutput").ap())
    build(nc, *args)
    r = _run(nc, [arrays], core_ids=[0])
    return r.results[0]["out_y"]
```

```python
from contextlib import ExitStack

import concourse.bass as bass
from concourse import mybir

ALU = mybir.AluOpType
ACT = mybir.ActivationFunctionType
AX = mybir.AxisListType
F32 = mybir.dt.float32
BF16 = mybir.dt.bfloat16
U32 = mybir.dt.uint32
U16 = mybir.dt.uint16

P = 128
B, S, DIM = 8, 112, 512
LCTX, N_IMG = 375, 257
N_TXT = LCTX - N_IMG
H, D = 16, 128
INNER = H * D
KT = DIM // P
CH = LCTX // 3
NREM = CH - N_TXT
HG = 4
NG = H // HG
E, TOPK, FF, CAP = 64, 8, 192, 128
FC = 96
FT = FF // FC
SLOTS = E * CAP
TOKENS = B * S
ROW = 2 * DIM + 2 * E + 4
LN_EPS, RMS_EPS = 1e-5, 1e-6
VEC = 8
W_STAGES = 3
NCHUNK = 4


def build(nc, x, ctx_in, g_xattn, g_ffn, q_w, q_b, k_w, k_b, v_w, v_b, ki_w, ki_b, vi_w, vi_b,
          o_w, o_b, nq_s, nkt_s, nki_s, gate_w, wg, wu, wd, out):
    with ExitStack() as top:
        build_in(nc, top, x, ctx_in, g_xattn, g_ffn, q_w, q_b, k_w, k_b, v_w, v_b, ki_w, ki_b,
                 vi_w, vi_b, o_w, o_b, nq_s, nkt_s, nki_s, gate_w, wg, wu, wd, out)


def after(eng, sem, value):
    if not isinstance(value, int) or value > 0:
        eng.wait_ge(sem, value)


def build_in(nc, top, x, ctx_in, g_xattn, g_ffn, q_w, q_b, k_w, k_b, v_w, v_b, ki_w, ki_b,
             vi_w, vi_b, o_w, o_b, nq_s, nkt_s, nki_s, gate_w, wg, wu, wd, out):
    def sem(name):
        return top.enter_context(nc.semaphore(name))

    def dram(name, shape, dt):
        return nc.dram_tensor(name, shape, dt, kind="Internal").ap()

    ctxT_d = dram("ctxT_d", [B, P, 2 * KT * LCTX], BF16)
    pt_d = dram("pt_d", [B * NG, P, HG * 6 * S], BF16)
    vrem_d = dram("vrem_d", [NG, B * NREM, 2 * 512], BF16)
    vbias_d = dram("vbias_d", [2, NG, 2, 512], BF16)
    xin_d = dram("xin_d", [SLOTS, ROW], U16)
    acc_d = [dram(f"acc{i}_d", [TOKENS + CAP, DIM], F32) for i in range(2)]

    def sb(stack, name, shape, dt, side=None):
        return stack.enter_context(nc.sbuf_tensor(name, shape, dt, side=side))

    ident = sb(top, "ident", [P, P], F32)
    identb = sb(top, "identb", [P, P], BF16)
    ones = sb(top, "ones", [P, P], F32)
    onesb = sb(top, "onesb", [S, S], BF16)
    trib = sb(top, "trib", [S, S], BF16)
    cols = sb(top, "cols", [P, VEC * H], F32)
    kb_scaled = sb(top, "kb_scaled", [P, 2, H], F32)
    vecs_raw = sb(top, "vecs_raw", [P, P], F32)
    slots_left = sb(top, "slots_left", [S, E], F32)
    xd = sb(top, "xd", [S, ROW], U16)
    idx = sb(top, "idx", [S, TOPK], U32)
    eid_i = sb(top, "eid_i", [S, E], mybir.dt.int32)
    zeros = sb(top, "zeros", [P, ROW], U16)
    tok1 = sb(top, "tok1", [P, 1], F32)
    empty_row = sb(top, "empty_row", [P, 1], F32)
    tok_i = sb(top, "tok_i", [P, 1], mybir.dt.int32)
    mhalf = sb(top, "mhalf", [P, 4], F32)
    ln_eps = sb(top, "ln_eps", [P, 1], F32)
    tg = sb(top, "tg", [P, 2], F32)
    g_raw = sb(top, "g_raw", [P, 2], F32)

    s_const = sem("s_const")
    s_vecs_in = sem("s_vecs_in")
    s_vecs_turned = sem("s_vecs_turned")
    s_cols = sem("s_cols")
    s_g_in = sem("s_g_in")
    s_tanh = sem("s_tanh")
    s_zeroed = sem("s_zeroed")
    s_w_in = [sem(f"s_w_in{i}") for i in range(W_STAGES)]
    s_w_hi = [sem(f"s_w_hi{i}") for i in range(W_STAGES)]
    s_w_lo = [sem(f"s_w_lo{i}") for i in range(W_STAGES)]
    s_ctx_in = sem("s_ctx_in")
    s_x_in = sem("s_x_in")
    s_ctx_turned = sem("s_ctx_turned")
    s_ctx_hi = sem("s_ctx_hi")
    s_ctx_lo = sem("s_ctx_lo")
    s_ctx_saved = sem("s_ctx_saved")
    s_ln_stats = sem("s_ln_stats")
    s_ln_aggr = sem("s_ln_aggr")
    s_ln_var = sem("s_ln_var")
    s_ln_rstd = sem("s_ln_rstd")
    s_xn = sem("s_xn")
    s_xn_turned = sem("s_xn_turned")
    s_xn_hi = sem("s_xn_hi")
    s_xn_lo = sem("s_xn_lo")
    s_k_made = sem("s_k_made")
    s_q_made = sem("s_q_made")
    s_k_out = sem("s_k_out")
    s_k_hi = sem("s_k_hi")
    s_kb_scaled = sem("s_kb_scaled")
    s_q_out = sem("s_q_out")
    s_kq_hi = sem("s_kq_hi")
    s_kq_split = sem("s_kq_split")
    s_square = sem("s_square")
    s_squared = sem("s_squared")
    s_sums = sem("s_sums")
    s_ms = sem("s_ms")
    s_rms = sem("s_rms")
    s_rdiag = sem("s_rdiag")
    s_rrow = sem("s_rrow")
    s_rrow_out = sem("s_rrow_out")
    s_rem_in = sem("s_rem_in")
    s_rem_turned = sem("s_rem_turned")
    s_rem_hi = sem("s_rem_hi")
    s_rem_lo = sem("s_rem_lo")
    s_vrem_made = sem("s_vrem_made")
    s_vrem_hi = sem("s_vrem_hi")
    s_vrem_lo = sem("s_vrem_lo")
    s_vrem_saved = [sem(f"s_vrem_saved{i}") for i in range(2)]
    s_ctxT_in = sem("s_ctxT_in")
    s_v_made = sem("s_v_made")
    s_v_hi = sem("s_v_hi")
    s_v_lo = sem("s_v_lo")
    s_vb_in = sem("s_vb_in")
    s_vb_sum = sem("s_vb_sum")
    s_vb_parts = sem("s_vb_parts")
    s_vb_saved = sem("s_vb_saved")
    s_s_made = sem("s_s_made")
    s_s_scaled = sem("s_s_scaled")
    s_nmax = sem("s_nmax")
    s_exp = sem("s_exp")
    s_rcp = sem("s_rcp")
    s_p = sem("s_p")
    s_p_turned = sem("s_p_turned")
    s_p_hi = sem("s_p_hi")
    s_p_lo = sem("s_p_lo")
    s_p_saved = [sem(f"s_p_saved{i}") for i in range(4)]

    K_SLOT, KI_SLOT, Q_SLOT = 0, 1, 2
    V_SLOT, VI_SLOT, O_SLOT = 0, 1, 2
    w_hi = [sb(top, f"w_hi{i}", [P, KT, INNER], BF16) for i in range(2)]
    w_lo = [sb(top, f"w_lo{i}", [P, KT, INNER], BF16) for i in range(2)]
    ctx_place = sb(top, "ctx_place", [P, 2 * KT * LCTX], F32)
    ctxT = ctx_place[:, :].bitcast(BF16).rearrange("p (b a k l) -> p b a k l", b=2, a=2, k=KT)
    NRAW = 8
    NR3 = 4
    RAW_N = KT * 2 * FF + FT * DIM
    raw = [part[slot][:, :, :].rearrange("p k n -> p (k n)").bitcast(F32) for slot in (V_SLOT, VI_SLOT)
           for part in (w_hi, w_lo)]
    raw.append(ctx_place[:, :])
    s_ew_in = [sem(f"s_ew_in{i}") for i in range(NRAW)]
    kv = sb(top, "kv", [P, NG, 3, 2, 512], BF16)
    kv_flat = kv[:, :, :, :, :].rearrange("p g c a n -> p (g c a n)")
    kT = kv_flat.rearrange("p (h a l) -> p h a l", h=H, a=2)
    GU_N, DN_N = KT * 2 * FF, FT * DIM
    gu = [kv_flat[:, p * 2 * GU_N:(p + 1) * 2 * GU_N].rearrange("p (a n) -> p a n", a=2) for p in range(2)]
    dn = [kv_flat[0:FC, 4 * GU_N + r * 2 * DN_N:4 * GU_N + (r + 1) * 2 * DN_N].rearrange("p (a n) -> p a n", a=2)
          for r in range(2)]
    EARLY = 2
    s_gu_hi = sem("s_gu_hi")
    s_gu_lo = sem("s_gu_lo")
    s_d_hi = sem("s_d_hi")
    s_d_lo = sem("s_d_lo")

    def raw_gu(r):
        return raw[r][:, 0:KT * 2 * FF]

    def raw_d(r):
        return raw[r][0:FC, KT * 2 * FF:RAW_N]

    def load_expert_weights(sp, e, r):
        gu_k = raw_gu(r).rearrange("p (k n) -> p k n", k=KT)
        sp.dma_start(gu_k[:, :, 0:FF], wg[e].rearrange("(p c) i -> p c i", c=KT)).then_inc(s_ew_in[r], 16)
        sp.dma_start(gu_k[:, :, FF:2 * FF], wu[e].rearrange("(p c) i -> p c i", c=KT)).then_inc(s_ew_in[r], 16)
        sp.dma_start(raw_d(r), wd[e].rearrange("(p c) n -> p (c n)", c=FT)).then_inc(s_ew_in[r], 16)

    def early_hi(act, e):
        act.wait_ge(s_ew_in[e], 48)
        nc.scalar.copy(gu[e][:, 0, :], raw_gu(e)).then_inc(s_gu_hi, 1)
        nc.scalar.copy(dn[e][:, 0, :], raw_d(e)).then_inc(s_d_hi, 1)

    with ExitStack() as mem:
        w_hi.append(sb(mem, "w_hi2", [P, KT, INNER], BF16))
        w_lo.append(sb(mem, "w_lo2", [P, KT, INNER], BF16))
        NR = B * NREM

        def split_matmul(pe, dst, lhs, rhs, first, last):
            pe.matmul(dst, lhs[0], rhs[0], start=first, stop=False)
            pe.matmul(dst, lhs[0], rhs[1], start=False, stop=False)
            return pe.matmul(dst, lhs[1], rhs[0], start=False, stop=last)

        def make_values(pe, bank, par, g, c):
            rows = N_TXT if c == 0 else CH
            w = V_SLOT if c == 0 else VI_SLOT
            for k in range(KT):
                mm = split_matmul(pe, bank[0:rows, :],
                                  (ctxT[:, par, 0, k, c * CH:c * CH + rows], ctxT[:, par, 1, k, c * CH:c * CH + rows]),
                                  (w_hi[w][:, k, g * 512:(g + 1) * 512], w_lo[w][:, k, g * 512:(g + 1) * 512]),
                                  k == 0, k == KT - 1)
            mm.then_inc(s_v_made, 1)

        def values_hi(act, bank, b, g, c):
            rows = N_TXT if c == 0 else CH
            act.wait_ge(s_v_made, 3 * (b * NG + g) + c + 1)
            nc.scalar.copy(kv[0:rows, g, c, 0, :], bank[0:rows, :]).then_inc(s_v_hi, 1)

        def values_lo(dve, bank, b, g, c):
            rows = N_TXT if c == 0 else CH
            dve.wait_ge(s_v_hi, 3 * (b * NG + g) + c + 1)
            nc.vector.tensor_tensor(kv[0:rows, g, c, 1, :], bank[0:rows, :], kv[0:rows, g, c, 0, :],
                                    ALU.subtract).then_inc(s_v_lo, 1)

        with nc.Block() as block, ExitStack() as ph1, ExitStack() as ps1:
            w_raw = [sb(ph1, f"w_raw{i}", [P, INNER], F32) for i in range(W_STAGES)]
            ctx_raw = sb(ph1, "ctx_raw", [P, 3, DIM], F32)
            x_raw = sb(ph1, "x_raw", [S, DIM], F32)
            stats = sb(ph1, "stats", [S, 6], F32)
            mv = sb(ph1, "mv", [S, 2], F32)
            rstd = sb(ph1, "rstd", [S, 1], F32)
            xn = sb(ph1, "xn", [S, DIM], F32)
            xnT = sb(ph1, "xnT", [P, 2, 2, KT, S], BF16)
            qT = sb(ph1, "qT", [P, H, 2, S], BF16)
            RKQ = 2
            kq = sb(ph1, "kq", [P, RKQ, LCTX + S], F32)
            sq = sb(ph1, "sq", [P, LCTX + S], F32)
            sq_sum = sb(ph1, "sq_sum", [P, LCTX + S], F32)
            ms = sb(ph1, "ms", [P, 4], F32)
            rms = sb(ph1, "rms", [P, 4], F32)
            q_scale = sb(ph1, "q_scale", [S, 1], F32)
            rdiag = sb(ph1, "rdiag", [CH, 3, CH], F32)
            rrow = sb(ph1, "rrow", [S, LCTX], F32)
            RS = 4
            prob = sb(ph1, "prob", [S, RS, LCTX], F32)
            pause = sb(ph1, "pause", [1, 1], F32)
            pause_ln = sb(ph1, "pause_ln", [1, 1], F32)
            mx = sb(ph1, "mx", [S, RS, 2], F32)
            nmx = sb(ph1, "nmx", [S, RS, 2], F32)
            psum_row = sb(ph1, "psum_row", [S, RS, 2], F32)
            rcp = sb(ph1, "rcp", [S, RS, 2], F32)
            ptb = sb(ph1, "ptb", [P, 4, 2, 3 * S], BF16)
            vb_f = prob[0:NG, :, :].rearrange("g r l -> g (r l)")
            vb_b = vb_f[:, 512:1024].bitcast(BF16)
            rem_raw = ctx_raw[0:B * NREM, 0, :]
            vrem = ctx_raw[0:B * NREM, 1:3, :].rearrange("r i n -> r (i n)").bitcast(BF16).rearrange(
                "r (i a n) -> r i a n", i=2, a=2)
            remT = xnT[:, 0, :, :, :].rearrange("p a k s -> p a (k s)")[:, :, 0:KT * B * NREM]

            def pb(name, shape, dt=F32):
                return ps1.enter_context(nc.psum_tensor(name, shape, dt))

            pk = [pb(f"pk{i}", [P, 512]) for i in range(2)]
            pq = pb("pq", [P, 512])
            ps = [pb(f"ps{i}", [P, 512]) for i in range(2)]
            pt = [pb(f"pt{i}", [P, 512]) for i in range(2)]
            pm = pb("pm", [P, 512])
            FIRST_BANKS = [ps[0], ps[1], pt[0], pt[1], pq]

            w_plan = [(w, slot, c) for c in range(NCHUNK) for w, slot in
                      [(k_w, K_SLOT), (ki_w, KI_SLOT), (q_w, Q_SLOT)]]
            w_plan += [(w, slot, c) for c in range(NCHUNK) for w, slot in [(vi_w, VI_SLOT), (v_w, V_SLOT)]]
            w_plan += [(o_w, O_SLOT, c) for c in range(NCHUNK)]
            W_HALF = 3 * NCHUNK

            def w_part(part, n):
                w, slot, c = w_plan[n]
                if w is o_w:
                    return part[slot][:, c, :].rearrange("p (h n) -> p h n", n=DIM)
                return part[slot][:, :, c * 512:(c + 1) * 512]

            def w_staged(n):
                return w_raw[n % W_STAGES][:, :].rearrange("p (k n) -> p k n", n=512)

            def load_weights(sp, n):
                w, slot, c = w_plan[n]
                if w is o_w:
                    src = w.rearrange("(c h d) n -> c d h n", c=NCHUNK, d=D)[c]
                else:
                    src = w.rearrange("(k p) (c n) -> c p k n", p=P, n=512)[c]
                after(sp, s_w_lo[n % W_STAGES], n // W_STAGES)
                sp.dma_start(w_staged(n), src).then_inc(s_w_in[n % W_STAGES], 16)

            def weights_hi(act, n):
                act.wait_ge(s_w_in[n % W_STAGES], 16 * (n // W_STAGES + 1))
                nc.scalar.copy(w_part(w_hi, n), w_staged(n)).then_inc(s_w_hi[n % W_STAGES], 1)

            def weights_lo(eng, n):
                eng.wait_ge(s_w_hi[n % W_STAGES], n // W_STAGES + 1)
                eng.tensor_tensor(w_part(w_lo, n), w_staged(n), w_part(w_hi, n),
                                  ALU.subtract).then_inc(s_w_lo[n % W_STAGES], 1)

            def pool_splits(n):
                return n % 3 != 0

            def weight_ready(pe, n):
                pe.wait_ge(s_w_lo[n % W_STAGES], n // W_STAGES + 1)

            def vec(v, h):
                return cols[:, v * H + h:v * H + h + 1]
            QB, KB, KIB, NQ, NKT, NKI, VB, VIB = range(VEC)

            LAG = 4

            def lagging(step, eng, b, score, h):
                if score and h >= LAG:
                    step(eng, b - 1, h - LAG)
                elif score and not (isinstance(b, int) and b == 1):
                    step(eng, b - 2, H + h - LAG)
            EXP_LAG, NORM_LAG = 1, 2
            LN_AT, LN_POWER_AT = (4, 10), 5

            def is_last(b):
                return isinstance(b, int) and b == B - 1

            def all_batches(eng, batch):
                batch(eng, 0, 0, True, False)
                batch(eng, 1, 1, True, True)
                with eng.Fori(1, B // 2 - 1) as i:
                    batch(eng, i * 2, 0, True, True)
                    batch(eng, i * 2 + 1, 1, True, True)
                batch(eng, B - 2, 0, True, True)
                batch(eng, B - 1, 1, True, True)
                batch(eng, B, 0, False, True)

            TURN_AT = [4, 6, 8, 10]
            TURN_X_AT = 12

            def load_batch(sp, b):
                after(sp, s_ctx_turned, b * KT)
                sp.dma_start(ctx_raw[0:N_TXT, 0, :], ctx_in[b, N_IMG:LCTX, :]).then_inc(s_ctx_in, 16)
                sp.dma_start(ctx_raw[N_TXT:CH, 0, :], ctx_in[b, 2 * CH:N_IMG, :]).then_inc(s_ctx_in, 16)
                sp.dma_start(ctx_raw[0:CH, 1:3, :],
                             ctx_in[b, 0:2 * CH, :].rearrange("(c p) d -> p c d", p=CH)).then_inc(s_ctx_in, 16)
                after(sp, s_xn, b)
                sp.dma_start(x_raw[:, :], x[b]).then_inc(s_x_in, 16)

            def save_batch(sp, b, par):
                sp.wait_ge(s_ctx_lo, b * KT + KT)
                sp.dma_start(ctxT_d[b], ctxT[:, par, :, :, :].rearrange("p a k l -> p (a k l)")).then_inc(s_ctx_saved, 16)

            def zero_rows(sp, b):
                sp.wait_ge(s_ctx_saved, 16 * b + 16)
                sp.dma_start(xin_d.rearrange("(g a p) n -> g p a n", g=B, p=P)[b],
                             zeros[:, :].unsqueeze(1).broadcast_to([P, SLOTS // B // P, ROW])).then_inc(s_zeroed, 16)

            def save_prob(sp, b, h):
                    sp.wait_ge(s_p_lo, b * H + h + 1)
                    sp.dma_start(pt_d[b * NG + h // HG][:, (h % HG) * 6 * S:(h % HG + 1) * 6 * S],
                                 ptb[:, h % 4, :, :].rearrange("p a s -> p (a s)")).then_inc(s_p_saved[h % 4], 16)

            def sp_batch1(sp, b, par, project, score):
                save_batch(sp, b, par)
                if score:
                    load_batch(sp, b + 1)
                zero_rows(sp, b)
                for h in range(H):
                    lagging(save_prob, sp, b, score, h)

            REM_AT = 1
            VREM_AT = [2, 4, 6, 7]
            V_AT = {4: 0, 5: 1, 6: 2, 8: 3, 9: 4, 10: 5, 12: 6, 13: 7, 14: 8}
            V_TAIL = {12: 9, 14: 10}

            @block.sync
            def _(sp):
                load_batch(sp, 0)
                for n in range(W_HALF):
                    load_weights(sp, n)
                    if n == W_STAGES - 1:
                        vectors = [q_b, k_b, ki_b, nq_s, nkt_s, nki_s, v_b, vi_b]
                        for v, a in enumerate(vectors):
                            sp.dma_start(vecs_raw[v * H:(v + 1) * H, :], a.rearrange("(h d) -> h d", d=D)).then_inc(s_vecs_in, 16)
                        for i, g in enumerate([g_xattn, g_ffn]):
                            sp.dma_start(g_raw[:, i:i + 1], g.rearrange("(a b) -> a b", a=1).broadcast_to([P, 1])).then_inc(s_g_in, 16)
                        for i, v in enumerate([v_b, vi_b]):
                            sp.dma_start(vb_f[:, i * 512:(i + 1) * 512], v.rearrange("(g n) -> g n", g=NG)).then_inc(s_vb_in, 16)
                    if n == 5:
                        load_batch(sp, 1)
                sp.wait_ge(s_const, 1)
                sp.dma_start(acc_d[0][TOKENS:TOKENS + CAP, :], zeros[:, 0:2 * DIM].bitcast(F32)).then_inc(s_zeroed, 16)
                sp.dma_start(acc_d[1].rearrange("(a p) n -> p a n", p=P),
                             zeros[:, 0:2 * DIM].bitcast(F32).unsqueeze(1).broadcast_to(
                                 [P, (TOKENS + CAP) // P, DIM])).then_inc(s_zeroed, 16)
                sp.dma_start(vbias_d[:, :, 1, :], zeros[0:2, 0:512].bitcast(BF16).unsqueeze(1).broadcast_to(
                    [2, NG, 512])).then_inc(s_zeroed, 16)
                sp_batch1(sp, 0, 0, True, False)
                for i in range(2):
                    sp.wait_ge(s_vb_parts, 2)
                    sp.dma_start(vbias_d[i, :, 0, :], vb_b[:, i * 512:(i + 1) * 512]).then_inc(s_vb_saved, 16)
                sp_batch1(sp, 1, 1, True, True)
                with sp.Fori(1, B // 2 - 1) as i:
                    sp_batch1(sp, i * 2, 0, True, True)
                    sp_batch1(sp, i * 2 + 1, 1, True, True)
                sp_batch1(sp, B - 2, 0, True, True)
                save_batch(sp, B - 1, 1)
                for n in range(W_HALF, W_HALF + W_STAGES):
                    load_weights(sp, n)
                zero_rows(sp, B - 1)
                sp.wait_ge(s_ctx_turned, B * KT)
                for b in range(B):
                    sp.dma_start(rem_raw[b * NREM:(b + 1) * NREM, :], ctx_in[b, 2 * CH:N_IMG, :]).then_inc(s_rem_in, 16)
                for h in range(H):
                    lagging(save_prob, sp, B - 1, True, h)
                sp.wait_ge(s_k_made, (B - 1) * H)
                sp.wait_ge(s_ctx_saved, 16 * (B - 1))
                sp.dma_start(ctxT[:, 0, :, :, :].rearrange("p a k l -> p (a k l)"), ctxT_d[0]).then_inc(s_ctxT_in, 16)
                for h in range(H):
                    if h > 0 and W_HALF + W_STAGES + h - 1 < 2 * W_HALF:
                        load_weights(sp, W_HALF + W_STAGES + h - 1)
                    lagging(save_prob, sp, B, True, h)
                    if h in VREM_AT:
                        g = VREM_AT.index(h)
                        sp.wait_ge(s_vrem_lo, g + 1)
                        sp.dma_start(vrem_d[g], vrem[:, g % 2, :, :].rearrange("p a n -> p (a n)")).then_inc(s_vrem_saved[g % 2], 16)
                for h in range(H - LAG, H):
                    save_prob(sp, B - 1, h)
                for i in range(2):
                    sp.wait_ge(s_vrem_saved[i], 16 * NG // 2)
                sp.wait_ge(s_vb_saved, 32)
                sp.wait_ge(s_ctx_saved, 16 * B)
                sp.wait_ge(s_zeroed, 16 * (B + 3))
                for i in range(4):
                    sp.wait_ge(s_p_saved[i], 16 * B * H // 4)

            @block.gpsimd
            def _(pool):
                nc.gpsimd.memset(zeros[:, :], 0).then_inc(s_const, 1)
                nc.gpsimd.memset(ident[:, :], 0.0).then_inc(s_const, 1)
                nc.gpsimd.memset(ones[:, :], 1.0).then_inc(s_const, 1)
                nc.gpsimd.memset(onesb[:, :], 1.0).then_inc(s_const, 1)
                nc.gpsimd.memset(ptb[:, :, :, :], 0.0).then_inc(s_const, 1)
                nc.gpsimd.memset(ms[:, :], 1.0).then_inc(s_const, 1)
                nc.gpsimd.memset(mhalf[:, :], -0.5)
                nc.gpsimd.memset(ln_eps[:, :], LN_EPS)
                pool.wait_ge(s_const, 6)
                nc.gpsimd.affine_select(out=ident[:, :], in_=ident[:, :], compare_op=ALU.not_equal, fill=1.0,
                                        base=0, pattern=[[-1, P]], channel_multiplier=1).then_inc(s_const, 1)
                nc.gpsimd.affine_select(out=trib[:, :], in_=onesb[:, :], compare_op=ALU.is_ge, fill=0.0,
                                        base=-1, pattern=[[1, S]], channel_multiplier=-1).then_inc(s_const, 1)
                nc.gpsimd.iota(eid_i[:, :], pattern=[[-CAP, E]], base=SLOTS, channel_multiplier=0).then_inc(s_const, 1)
                nc.gpsimd.iota(tok_i[:, :], pattern=[[0, 1]], base=1, channel_multiplier=1).then_inc(s_const, 1)
                pool.wait_ge(s_const, 10)
                nc.gpsimd.tensor_copy(identb[:, :], ident[:, :]).then_inc(s_const, 1)
                nc.gpsimd.tensor_copy(slots_left[:, :], eid_i[:, :]).then_inc(s_const, 1)
                nc.gpsimd.tensor_copy(tok1[:, :], tok_i[:, :]).then_inc(s_const, 1)
                pool.wait_ge(s_const, 13)
                nc.gpsimd.tensor_scalar(empty_row[:, :], tok1[:, :], float(TOKENS), 1.0, ALU.add, ALU.mult).then_inc(s_const, 1)
                pool.wait_ge(s_const, 14)
                nc.gpsimd.memset(ptb[P - 32:P, :, 0, 0:S], 1.0).then_inc(s_const, 1)
                pool.wait_ge(s_const, 15)

                def ln_power(b):
                    pool.wait_ge(s_ln_aggr, b + 1)
                    nc.gpsimd.tensor_tensor(rstd[:, :], mv[:, 1:2], ln_eps[0:S, :], ALU.add).then_inc(s_ln_var, 1)
                    pool.wait_ge(s_ln_var, b + 1)
                    nc.gpsimd.tensor_tensor(rstd[:, :], rstd[:, :], mhalf[0:S, 0:1], ALU.pow).then_inc(s_ln_rstd, 1)


                def squares(b, ln_next):
                    for h in range(H):
                        n = b * H + h
                        pool.wait_ge(s_k_out, n + 1)
                        pool.wait_ge(s_q_out, n + 1)
                        src = kq[:, h % RKQ, :]
                        if h == 0:
                            after(pool, s_sums, b)
                            nc.gpsimd.tensor_tensor(sq_sum[:, :], src, src, ALU.mult).then_inc(s_squared, 1)
                        else:
                            pool.wait_ge(s_squared, n)
                            nc.gpsimd.tensor_tensor(sq[:, :], src, src, ALU.mult).then_inc(s_square, 1)
                            pool.wait_ge(s_square, b * (H - 1) + h)
                            nc.gpsimd.tensor_tensor(sq_sum[:, :], sq_sum[:, :], sq[:, :], ALU.add).then_inc(s_squared, 1)
                        if ln_next and h == LN_POWER_AT:
                            ln_power(b + 1)
                    pool.wait_ge(s_ms, b + 1)
                    nc.gpsimd.tensor_tensor(rms[:, :], ms[:, :], mhalf[:, :], ALU.pow).then_inc(s_rms, 1)

                ln_power(0)
                squares(0, True)
                with pool.Fori(1, B - 1) as b:
                    squares(b, True)
                squares(B - 1, False)
                for n in range(W_HALF, 2 * W_HALF):
                    if pool_splits(n):
                        weights_lo(nc.gpsimd, n)

            def turn_ctx(pe, b, k, bank):
                pe.wait_ge(s_ctx_in, 48 * b + 48)
                for c in range(3):
                    mm = pe.transpose(bank[:, c * CH:(c + 1) * CH],
                                      ctx_raw[0:CH, c, k * P:(k + 1) * P], ident[0:CH, 0:CH])
                mm.then_inc(s_ctx_turned, 1)

            def turn_x(pe, b, bank):
                pe.wait_ge(s_xn, b + 1)
                for k in range(KT):
                    mm = pe.transpose(bank[:, k * S:(k + 1) * S], xn[:, k * P:(k + 1) * P], ident[0:S, 0:S])
                mm.then_inc(s_xn_turned, 1)

            def turn_next(pe, b, h):
                if h in TURN_AT:
                    k = TURN_AT.index(h)
                    if k == 0 and isinstance(b, int) and b == 0:
                        pe.wait_ge(s_cols, 1)
                    elif k == 0:
                        pe.wait_ge(s_rrow_out, b)
                    else:
                        pe.wait_ge(s_ctx_lo, (b + 1) * KT + k)
                    turn_ctx(pe, b + 1, k, pm)
                if h == TURN_X_AT:
                    pe.wait_ge(s_ctx_lo, (b + 2) * KT)
                    turn_x(pe, b + 1, pm)

            def project_head(pe, b, par, h):
                n = b * H + h
                first = h % HG == 0 and isinstance(b, int) and b == 0
                if first:
                    weight_ready(pe, h // HG * W_STAGES + K_SLOT)
                    weight_ready(pe, h // HG * W_STAGES + KI_SLOT)
                if h == 0:
                    pe.wait_ge(s_ctx_lo, b * KT + KT)
                after(pe, s_k_hi, n - 1)
                for slot, lo, hi in [(K_SLOT, 0, N_TXT), (KI_SLOT, N_TXT, LCTX)]:
                    for k in range(KT):
                        mm = split_matmul(pe, pk[h % 2][:, lo:hi],
                                          (w_hi[slot][:, k, h * D:(h + 1) * D], w_lo[slot][:, k, h * D:(h + 1) * D]),
                                          (ctxT[:, par, 0, k, lo:hi], ctxT[:, par, 1, k, lo:hi]), k == 0, k == KT - 1)
                mm.then_inc(s_k_made, 1)
                if first:
                    weight_ready(pe, h // HG * W_STAGES + Q_SLOT)
                if h == 0:
                    pe.wait_ge(s_xn_lo, b + 1)
                after(pe, s_q_out, n)
                for k in range(KT):
                    mm = split_matmul(pe, pq[:, 0:S],
                                      (w_hi[Q_SLOT][:, k, h * D:(h + 1) * D], w_lo[Q_SLOT][:, k, h * D:(h + 1) * D]),
                                      (xnT[:, par, 0, k, :], xnT[:, par, 1, k, :]), k == 0, k == KT - 1)
                mm.then_inc(s_q_made, 1)

            def score_head(pe, b, h):
                n = b * H + h
                pe.wait_ge(s_kq_split, n + 1)
                after(pe, s_s_scaled, n - 1)
                mm = split_matmul(pe, ps[h % 2][0:S, 0:LCTX], (qT[:, h, 0, :], qT[:, h, 1, :]),
                                  (kT[:, h, 0, 0:LCTX], kT[:, h, 1, 0:LCTX]), True, True)
                mm.then_inc(s_s_made, 1)

            def turn_probs(pe, b, h):
                n = b * H + h
                pe.wait_ge(s_p, n + 1)
                after(pe, s_p_lo, n - 1)
                for c in range(3):
                    mm = pe.transpose(pt[h % 2][0:CH, c * S:(c + 1) * S],
                                      prob[:, h % RS, c * CH:(c + 1) * CH], ident[0:S, 0:S])
                mm.then_inc(s_p_turned, 1)

            def sum_squares(pe, b):
                pe.wait_ge(s_squared, (b + 1) * H)
                after(pe, s_rrow_out, b)
                if not is_last(b):
                    pe.wait_ge(s_xn_lo, b + 2)
                for c in range(3):
                    pe.matmul(pm[0:CH, c:c + 1], sq_sum[:, c * CH:(c + 1) * CH], ones[:, 0:1], start=True, stop=True)
                pe.matmul(pm[0:S, 3:4], sq_sum[:, LCTX:LCTX + S], ones[:, 0:1], start=True, stop=True).then_inc(s_sums, 1)

            def key_row(pe, b):
                pe.wait_ge(s_rdiag, b + 1)
                pe.matmul(pm[0:S, 0:LCTX], ones[0:CH, 0:S], rdiag[:, :, :].rearrange("p c l -> p (c l)"),
                          start=True, stop=True).then_inc(s_rrow, 1)

            def values_piece(pe, g, c):
                n = 3 * g + c
                if n == 0:
                    pe.wait_ge(s_ctxT_in, 16)
                if c == 0:
                    weight_ready(pe, W_HALF + 2 * g + 1)
                after(pe, s_v_lo, n - 1)
                make_values(pe, pk[n % 2], 0, g, c)

            def first_values(pe, h):
                if h == REM_AT:
                    pe.wait_ge(s_rem_in, 16 * B)
                    pe.wait_ge(s_rrow_out, B)
                    for k in range(KT):
                        mm = pe.transpose(pm[:, k * NR:(k + 1) * NR], rem_raw[:, k * P:(k + 1) * P], ident[0:NR, 0:NR])
                    mm.then_inc(s_rem_turned, 1)
                if h in VREM_AT:
                    g = VREM_AT.index(h)
                    pe.wait_ge(s_rem_lo, 1)
                    weight_ready(pe, W_HALF + 2 * g)
                    if g == 0:
                        pe.wait_ge(s_q_out, B * H)
                        pe.wait_ge(s_k_hi, B * H)
                    after(pe, s_vrem_lo, g)
                    for k in range(KT):
                        mm = split_matmul(pe, pq[0:NR, :],
                                          (remT[:, 0, k * NR:(k + 1) * NR], remT[:, 1, k * NR:(k + 1) * NR]),
                                          (w_hi[VI_SLOT][:, k, g * 512:(g + 1) * 512],
                                           w_lo[VI_SLOT][:, k, g * 512:(g + 1) * 512]), k == 0, k == KT - 1)
                    mm.then_inc(s_vrem_made, 1)
                if h in V_AT:
                    values_piece(pe, V_AT[h] // 3, V_AT[h] % 3)

            def pe_batch(pe, b, par, project, score):
                ahead = project and not is_last(b)
                if project:
                    project_head(pe, b, par, 0)
                lagging(turn_probs, pe, b, score, 0)
                if score:
                    score_head(pe, b - 1, 0)
                    sum_squares(pe, b - 1)
                if project:
                    project_head(pe, b, par, 1)
                lagging(turn_probs, pe, b, score, 1)
                if score:
                    score_head(pe, b - 1, 1)
                    key_row(pe, b - 1)
                for h in range(1, H):
                    if h > 1:
                        lagging(turn_probs, pe, b, score, h)
                    if score and h > 1:
                        score_head(pe, b - 1, h)
                    if project and h + 1 < H:
                        project_head(pe, b, par, h + 1)
                    if ahead:
                        turn_next(pe, b, h)
                    if not project:
                        first_values(pe, h)
                if not project:
                    for h in range(H - LAG, H):
                        turn_probs(pe, b - 1, h)
                        if h in V_TAIL:
                            values_piece(pe, V_TAIL[h] // 3, V_TAIL[h] % 3)

            @block.tensor
            def _(pe):
                pe.wait_ge(s_const, 7)
                for k in range(KT):
                    turn_ctx(pe, 0, k, FIRST_BANKS[k])
                turn_x(pe, 0, FIRST_BANKS[KT])
                pe.wait_ge(s_vecs_in, 16 * VEC)
                pe.transpose(pm[:, 0:P], vecs_raw[:, :], ident[:, :]).then_inc(s_vecs_turned, 1)
                pe.wait_ge(s_ctx_lo, KT)
                pe.wait_ge(s_xn_lo, 1)
                all_batches(pe, pe_batch)

            def act_ctx(act, b, par, k, bank):
                act.wait_ge(s_ctx_turned, b * KT + k + 1)
                if k == 0:
                    after(act, s_ctx_saved, 16 * (b - 1))
                nc.scalar.copy(ctxT[:, par, 0, k, :], bank[:, 0:LCTX]).then_inc(s_ctx_hi, 1)

            def act_x(act, b, par, bank):
                act.wait_ge(s_xn_turned, b + 1)
                nc.scalar.copy(xnT[:, par, 0, :, :].rearrange("p k s -> p (k s)"), bank[:, 0:KT * S]).then_inc(s_xn_hi, 1)

            def act_next(act, b, par, h):
                if h - 1 in TURN_AT:
                    act_ctx(act, b + 1, 1 - par, TURN_AT.index(h - 1), pm)
                if h - 1 == TURN_X_AT:
                    act_x(act, b + 1, 1 - par, pm)

            def act_project(act, b, h, score):
                n = b * H + h
                act.wait_ge(s_k_made, n + 1)
                after(act, s_kq_split, n - RKQ + 1)
                after(act, s_squared, n - RKQ + 1)
                parts = [(0, N_TXT, KB, NKT, 0), (N_TXT, LCTX, KIB, NKI, 1)]
                for lo, hi, bias, _, _ in parts:
                    last = nc.scalar.activation(kq[:, h % RKQ, lo:hi], pk[h % 2][:, lo:hi], ACT.Identity,
                                                bias=vec(bias, h))
                last.then_inc(s_k_out, 1)
                if score:
                    act.wait_ge(s_s_made, n - H + 1)
                for lo, hi, _, scale, i in parts:
                    last = nc.scalar.activation(kT[:, h, 0, lo:hi], pk[h % 2][:, lo:hi], ACT.Identity,
                                                bias=kb_scaled[:, i, h:h + 1], scale=vec(scale, h))
                last.then_inc(s_k_hi, 1)
                act.wait_ge(s_q_made, n + 1)
                nc.scalar.activation(kq[:, h % RKQ, LCTX:LCTX + S], pq[:, 0:S], ACT.Identity,
                                     bias=vec(QB, h)).then_inc(s_q_out, 1)

            def act_exp(act, b, h):
                n = b * H + h
                act.wait_ge(s_nmax, n + 1)
                r = h % RS
                nc.scalar.activation(prob[:, r, 0:N_TXT], prob[:, r, 0:N_TXT], ACT.Exp, bias=nmx[:, r, 0:1],
                                     scale=q_scale[:, 0:1], accum_out=psum_row[:, r, 0:1])
                nc.scalar.activation(prob[:, r, N_TXT:LCTX], prob[:, r, N_TXT:LCTX], ACT.Exp, bias=nmx[:, r, 1:2],
                                     scale=q_scale[:, 0:1], accum_out=psum_row[:, r, 1:2]).then_inc(s_exp, 1)

            def act_probs_hi(act, b, h):
                n = b * H + h
                act.wait_ge(s_p_turned, n + 1)
                after(act, s_p_saved[h % 4], 16 * (b * (H // 4) + h // 4))
                nc.scalar.copy(ptb[0:CH, h % 4, 0, :], pt[h % 2][0:CH, 0:3 * S]).then_inc(s_p_hi, 1)

            def act_first_values(act, h):
                if h == REM_AT:
                    act.wait_ge(s_rem_turned, 1)
                    nc.scalar.copy(remT[:, 0, :], pm[:, 0:KT * NR]).then_inc(s_rem_hi, 1)
                if h in VREM_AT:
                    g = VREM_AT.index(h)
                    act.wait_ge(s_vrem_made, g + 1)
                    after(act, s_vrem_saved[g % 2], 16 * (g // 2))
                    nc.scalar.copy(vrem[:, g % 2, 0, :], pq[0:NR, :]).then_inc(s_vrem_hi, 1)
                if h in V_AT:
                    values_hi(act, pk[V_AT[h] % 2], 0, V_AT[h] // 3, V_AT[h] % 3)

            def act_batch(act, b, par, project, score):
                ahead = project and not is_last(b)
                for h in range(H):
                    if not score:
                        split_ahead(act, weights_hi, h)
                    if project:
                        act_project(act, b, h, score)
                    if score and h == 0:
                        act.wait_ge(s_rrow, b)
                        nc.scalar.copy(rrow[:, :], pm[0:S, 0:LCTX]).then_inc(s_rrow_out, 1)
                    if ahead:
                        act_next(act, b, par, h)
                    if not project and h < W_HALF:
                        weights_hi(act, W_HALF + h)
                    if score and h >= EXP_LAG:
                        act_exp(act, b - 1, h - EXP_LAG)
                    lagging(act_probs_hi, act, b, score, h)
                    if not project:
                        act_first_values(act, h)
                if score:
                    for h in range(H - EXP_LAG, H):
                        act_exp(act, b - 1, h)
                if not project:
                    for h in range(H - LAG, H):
                        act_probs_hi(act, b - 1, h)
                        if h in V_TAIL:
                            values_hi(act, pk[V_TAIL[h] % 2], 0, V_TAIL[h] // 3, V_TAIL[h] % 3)

            def split_ahead(eng, split, h):
                if h % HG < W_STAGES and h // HG + 1 < NG:
                    split(eng, (h // HG + 1) * W_STAGES + h % HG)

            @block.scalar
            def _(act):
                for k in range(KT):
                    act_ctx(act, 0, 0, k, FIRST_BANKS[k])
                act_x(act, 0, 0, FIRST_BANKS[KT])
                for n in range(W_STAGES):
                    weights_hi(act, n)
                act.wait_ge(s_g_in, 32)
                nc.scalar.activation(tg[:, :], g_raw[:, :], ACT.Tanh).then_inc(s_tanh, 1)
                act.wait_ge(s_vecs_turned, 1)
                nc.scalar.copy(cols[:, :], pm[:, 0:P]).then_inc(s_cols, 1)
                act.wait_ge(s_cols, 1)
                act.wait_ge(s_kb_scaled, 1)
                act.wait_ge(s_const, 15)
                all_batches(act, act_batch)

            def dve_norms(dve, b):
                dve.wait_ge(s_sums, b + 1)
                nc.vector.tensor_scalar(ms[0:CH, 0:3], pm[0:CH, 0:3], 1.0 / INNER, RMS_EPS, ALU.mult, ALU.add)
                nc.vector.tensor_scalar(ms[0:S, 3:4], pm[0:S, 3:4], 1.0 / INNER, RMS_EPS, ALU.mult, ALU.add).then_inc(s_ms, 1)
                dve.wait_ge(s_rms, b + 1)
                for c in range(3):
                    nc.vector.tensor_scalar(rdiag[:, c, :], ident[0:CH, 0:CH], rms[0:CH, c:c + 1], None,
                                            ALU.mult)
                nc.vector.tensor_scalar(q_scale[:, :], rms[0:S, 3:4], float(D) ** -0.5, None,
                                        ALU.mult).then_inc(s_rdiag, 1)

            def dve_x_stats(dve, b):
                dve.wait_ge(s_x_in, 16 * b + 16)
                nc.vector.bn_stats(stats[:, :], x_raw[:, :]).then_inc(s_ln_stats, 1)
                dve.wait_ge(s_ln_stats, b + 1)
                nc.vector.memset(pause_ln[:, :], 0.0)
                nc.vector.bn_aggr(mv[:, :], stats[:, :]).then_inc(s_ln_aggr, 1)

            def dve_x_normalise(dve, b):
                dve.wait_ge(s_ln_rstd, b + 1)
                after(dve, s_xn_turned, b)
                nc.vector.tensor_scalar(xn[:, :], x_raw[:, :], mv[:, 0:1], rstd[:, 0:1], ALU.subtract,
                                        ALU.mult).then_inc(s_xn, 1)

            def dve_ctx(dve, b, par, k, bank):
                dve.wait_ge(s_ctx_hi, b * KT + k + 1)
                nc.vector.tensor_tensor(ctxT[:, par, 1, k, :], bank[:, 0:LCTX], ctxT[:, par, 0, k, :],
                                        ALU.subtract).then_inc(s_ctx_lo, 1)

            def dve_x(dve, b, par, bank):
                dve.wait_ge(s_xn_hi, b + 1)
                nc.vector.tensor_tensor(xnT[:, par, 1, :, :].rearrange("p k s -> p (k s)"), bank[:, 0:KT * S],
                                        xnT[:, par, 0, :, :].rearrange("p k s -> p (k s)"),
                                        ALU.subtract).then_inc(s_xn_lo, 1)

            def dve_next(dve, b, par, h):
                if h - 1 in TURN_AT:
                    dve_ctx(dve, b + 1, 1 - par, TURN_AT.index(h - 1), pm)
                if h - 1 == TURN_X_AT:
                    dve_x(dve, b + 1, 1 - par, pm)

            def dve_scale(dve, b, h):
                n = b * H + h
                r = h % RS
                dve.wait_ge(s_s_made, n + 1)
                after(dve, s_p_turned, n - RS + 1)
                if isinstance(n, int) and n == 0:
                    dve.wait_ge(s_vb_saved, 32)
                nc.vector.memset(pause[:, :], 0.0)
                nc.vector.tensor_tensor_reduce(out=prob[:, r, 0:N_TXT], in0=ps[h % 2][0:S, 0:N_TXT],
                                               in1=rrow[:, 0:N_TXT], scale=1.0, scalar=-3.0e38, op0=ALU.mult,
                                               op1=ALU.max, accum_out=mx[:, r, 0:1])
                nc.vector.tensor_tensor_reduce(out=prob[:, r, N_TXT:LCTX], in0=ps[h % 2][0:S, N_TXT:LCTX],
                                               in1=rrow[:, N_TXT:LCTX], scale=1.0, scalar=-3.0e38, op0=ALU.mult,
                                               op1=ALU.max, accum_out=mx[:, r, 1:2]).then_inc(s_s_scaled, 1)
                dve.wait_ge(s_s_scaled, n + 1)
                nc.vector.tensor_scalar(nmx[:, r, :], mx[:, r, :], q_scale[:, 0:1], -1.0, ALU.mult,
                                        ALU.mult).then_inc(s_nmax, 1)

            def dve_split(dve, b, h, score):
                n = b * H + h
                src = kq[:, h % RKQ, :]
                parts = [(kT[:, h, :, 0:N_TXT], src[:, 0:N_TXT], vec(NKT, h)),
                         (kT[:, h, :, N_TXT:LCTX], src[:, N_TXT:LCTX], vec(NKI, h)),
                         (qT[:, h, :, :], src[:, LCTX:LCTX + S], vec(NQ, h))]
                if score:
                    dve.wait_ge(s_s_made, n - H + 1)
                dve.wait_ge(s_q_out, n + 1)
                dst, v, scale = parts[2]
                nc.vector.tensor_scalar(dst[:, 0, :], v, scale, None, ALU.mult).then_inc(s_kq_hi, 1)
                dve.wait_ge(s_k_hi, n + 1)
                dve.wait_ge(s_kq_hi, n + 1)
                for dst, v, scale in parts:
                    last = nc.vector.scalar_tensor_tensor(dst[:, 1, :], v, scale, dst[:, 0, :], ALU.mult,
                                                          ALU.subtract)
                last.then_inc(s_kq_split, 1)

            def dve_normalise(dve, b, h):
                n = b * H + h
                r = h % RS
                dve.wait_ge(s_exp, n + 1)
                nc.vector.reciprocal(rcp[:, r, :], psum_row[:, r, :]).then_inc(s_rcp, 1)
                dve.wait_ge(s_rcp, n + 1)
                nc.vector.tensor_scalar(prob[:, r, 0:N_TXT], prob[:, r, 0:N_TXT], rcp[:, r, 0:1], None, ALU.mult)
                nc.vector.tensor_scalar(prob[:, r, N_TXT:LCTX], prob[:, r, N_TXT:LCTX], rcp[:, r, 1:2], None,
                                        ALU.mult).then_inc(s_p, 1)

            def dve_probs_lo(dve, b, h):
                n = b * H + h
                dve.wait_ge(s_p_hi, n + 1)
                nc.vector.tensor_tensor(ptb[0:CH, h % 4, 1, :], pt[h % 2][0:CH, 0:3 * S], ptb[0:CH, h % 4, 0, :],
                                        ALU.subtract).then_inc(s_p_lo, 1)

            def dve_first_values(dve, h):
                if h == REM_AT:
                    dve.wait_ge(s_rem_hi, 1)
                    nc.vector.tensor_tensor(remT[:, 1, :], pm[:, 0:KT * NR], remT[:, 0, :], ALU.subtract).then_inc(s_rem_lo, 1)
                if h in VREM_AT:
                    g = VREM_AT.index(h)
                    dve.wait_ge(s_vrem_hi, g + 1)
                    nc.vector.tensor_tensor(vrem[:, g % 2, 1, :], pq[0:NR, :], vrem[:, g % 2, 0, :],
                                            ALU.subtract).then_inc(s_vrem_lo, 1)
                if h in V_AT:
                    values_lo(dve, pk[V_AT[h] % 2], 0, V_AT[h] // 3, V_AT[h] % 3)

            def value_biases(dve):
                dve.wait_ge(s_vb_in, 32)
                nc.vector.tensor_tensor(vb_f[:, 0:512], vb_f[:, 0:512], vb_f[:, 512:1024], ALU.add).then_inc(s_vb_sum, 1)
                dve.wait_ge(s_vb_sum, 1)
                nc.vector.tensor_copy(vb_b[:, 0:512], vb_f[:, 0:512]).then_inc(s_vb_parts, 1)
                dve.wait_ge(s_vb_parts, 1)
                nc.vector.tensor_tensor(vb_b[:, 512:1024], vb_f[:, 0:512], vb_b[:, 0:512], ALU.subtract).then_inc(s_vb_parts, 1)

            def dve_batch(dve, b, par, project, score):
                ahead = project and not is_last(b)
                if score:
                    dve_norms(dve, b - 1)
                for h in range(H):
                    if not score:
                        split_ahead(dve, lambda _, n: weights_lo(nc.vector, n), h)
                    if score and h == 0:
                        if project:
                            dve_split(dve, b, h, score)
                        dve.wait_ge(s_rrow_out, b)
                    if score:
                        dve_scale(dve, b - 1, h)
                    if project and (h > 0 or not score):
                        dve_split(dve, b, h, score)
                    if ahead:
                        dve_next(dve, b, par, h)
                    if not score and h == H - 1:
                        value_biases(dve)
                    if score and h >= NORM_LAG:
                        dve_normalise(dve, b - 1, h - NORM_LAG)
                    lagging(dve_probs_lo, dve, b, score, h)
                    if ahead and h == LN_AT[0]:
                        dve_x_stats(dve, b + 1)
                    if ahead and h == LN_AT[1]:
                        dve_x_normalise(dve, b + 1)
                    n = W_HALF + h
                    if not project and h < W_HALF and not pool_splits(n):
                        weights_lo(nc.vector, n)
                    if not project:
                        dve_first_values(dve, h)
                if score:
                    for h in range(H - NORM_LAG, H):
                        dve_normalise(dve, b - 1, h)
                if not project:
                    for h in range(H - LAG, H):
                        dve_probs_lo(dve, b - 1, h)
                        if h in V_TAIL:
                            values_lo(dve, pk[V_TAIL[h] % 2], 0, V_TAIL[h] // 3, V_TAIL[h] % 3)

            @block.vector
            def _(dve):
                dve.wait_ge(s_const, 7)
                dve_x_stats(dve, 0)
                dve_x_normalise(dve, 0)
                for k in range(KT):
                    dve_ctx(dve, 0, 0, k, FIRST_BANKS[k])
                dve_x(dve, 0, 0, FIRST_BANKS[KT])
                for n in range(W_STAGES):
                    weights_lo(nc.vector, n)
                dve.wait_ge(s_cols, 1)
                nc.vector.tensor_tensor(kb_scaled[:, 0, :], cols[:, KB * H:(KB + 1) * H],
                                        cols[:, NKT * H:(NKT + 1) * H], ALU.mult)
                nc.vector.tensor_tensor(kb_scaled[:, 1, :], cols[:, KIB * H:(KIB + 1) * H],
                                        cols[:, NKI * H:(NKI + 1) * H], ALU.mult).then_inc(s_kb_scaled, 1)
                all_batches(dve, dve_batch)

        s_gw_in = sem("s_gw_in")
        s_gw_turned = sem("s_gw_turned")
        s_gwT = sem("s_gwT")
        s_vb_rows_in = sem("s_vb_rows_in")
        s_ob_in = sem("s_ob_in")
        s_obrow = sem("s_obrow")
        s_p_in = [sem(f"s_p_in{i}") for i in range(2)]
        s_vrem_in = [sem(f"s_vrem_in{i}") for i in range(2)]
        s_att = sem("s_att")
        s_att_hi = sem("s_att_hi")
        s_att_lo = sem("s_att_lo")
        s_o_made = sem("s_o_made")
        s_xr_in = sem("s_xr_in")
        s_xr = sem("s_xr")
        s_x2 = sem("s_x2")
        s_x2_saved = sem("s_x2_saved")
        s_x2_stats = sem("s_x2_stats")
        s_x2_aggr = sem("s_x2_aggr")
        s_x2_var = sem("s_x2_var")
        s_x2_rstd = sem("s_x2_rstd")
        s_xn2 = sem("s_xn2")
        s_xd_hi = sem("s_xd_hi")
        s_xd = sem("s_xd")
        s_xn2_turned = sem("s_xn2_turned")
        s_xn2T = sem("s_xn2T")
        s_logits = sem("s_logits")
        s_lmax = sem("s_lmax")
        s_lnmax = sem("s_lnmax")
        s_lexp = sem("s_lexp")
        s_route = sem("s_route")
        s_sel = sem("s_sel")
        s_pos = sem("s_pos")
        s_idx = sem("s_idx")
        s_dispatched = sem("s_dispatched")
        ROUTE_STEPS = 8

        late = [sb(top, f"raw{i}", [P, RAW_N], F32, side="right") for i in range(NRAW - len(raw))]
        LATE_FIRST = len(raw)
        raw += [place[:, :] for place in late]
        with nc.Block() as block, ExitStack() as ph2, ExitStack() as ps2:
            gw_raw = sb(ph2, "gw_raw", [E, DIM], F32)
            gwT = sb(ph2, "gwT", [P, KT, E], F32)
            obrow = sb(ph2, "obrow", [S, DIM], F32)
            pin = sb(ph2, "pin", [P, 2, HG, 2, 3 * S], BF16)
            outT = sb(ph2, "outT", [P, H, 2, S], BF16)
            xr_in = sb(ph2, "xr_in", [S, DIM], F32)
            xr = sb(ph2, "xr", [S, DIM], F32)
            x2 = sb(ph2, "x2", [S, DIM], F32)
            stats2 = sb(ph2, "stats2", [S, 6], F32)
            mv2 = sb(ph2, "mv2", [S, 2], F32)
            rstd2 = sb(ph2, "rstd2", [S, 1], F32)
            xn2 = sb(ph2, "xn2", [S, DIM], F32)
            xd_hi = xd[:, 0:DIM].bitcast(BF16).rearrange("s (c p) -> s c p", c=KT)
            xd_lo = xd[:, DIM:2 * DIM].bitcast(BF16).rearrange("s (c p) -> s c p", c=KT)
            xd_w = xd[:, 2 * DIM:2 * DIM + 2 * E].bitcast(F32)
            xd_tok = xd[:, ROW - 4:ROW - 2].bitcast(F32)
            tokf = sb(ph2, "tokf", [S, 1], F32)
            xn2T = sb(ph2, "xn2T", [P, KT * S], F32)
            lmax = sb(ph2, "lmax", [S, 2], F32)
            ex = sb(ph2, "ex", [S, E], F32)
            top8 = sb(ph2, "top8", [S, TOPK], F32)
            left = sb(ph2, "left", [S, E], F32)
            selb = sb(ph2, "selb", [S, E], BF16)
            cumb = sb(ph2, "cumb", [S, E], BF16)
            wsum = sb(ph2, "wsum", [S, 3], F32)
            slot = sb(ph2, "slot", [S, E], F32)
            val = sb(ph2, "val", [S, E], F32)
            key = sb(ph2, "key", [S, E], F32)
            key8 = sb(ph2, "key8", [S, TOPK], F32)
            pause = sb(ph2, "pause2", [1, 1], F32)
            pool_pause = sb(ph2, "pool_pause", [1, 2], F32)

            def pb2(name, shape, dt=F32):
                return ps2.enter_context(nc.psum_tensor(name, shape, dt))
            pv = [pb2(f"pv{i}", [P, 512]) for i in range(2)]
            pa = [pb2(f"pa{i}", [P, 512]) for i in range(2)]
            po = pb2("po", [P, 512])
            pg = pb2("pg", [P, 512])
            pl = pb2("pl", [P, 512])
            pp = pb2("pp", [P, 512])
            def load_group(sp, b, g):
                n = b * NG + g
                after(sp, s_att, n - 1)
                sp.dma_start(pin[:, g % 2, :, :, :].rearrange("p h a s -> p (h a s)"), pt_d[n]).then_inc(s_p_in[g % 2], 16)
                sp.dma_start(kv[N_TXT:CH, g, 0, :, :].rearrange("p a n -> p (a n)"),
                             vrem_d.rearrange("g (b r) n -> b g r n", b=B)[b, g]).then_inc(s_vrem_in[g % 2], 16)

            def load_values(sp, b, par):
                after(sp, s_v_made, 12 * (b - 1))
                sp.dma_start(ctxT[:, par, :, :, :].rearrange("p a k l -> p (a k l)"), ctxT_d[b]).then_inc(s_ctxT_in, 16)

            def save_route(sp, b):
                sp.wait_ge(s_x2, b + 1)
                sp.dma_start(acc_d[0][0:TOKENS, :].rearrange("(b s) n -> b s n", b=B)[b], x2[:, :]).then_inc(s_x2_saved, 16)

            def load_x(sp, b):
                after(sp, s_xr, b)
                sp.dma_start(xr_in[:, :], x[b]).then_inc(s_xr_in, 16)

            def sp_batch(sp, b, par, values, route):
                if isinstance(b, int) and b == B - 2:
                    for r in range(LATE_FIRST, NRAW):
                        load_expert_weights(sp, r, r)
                if values:
                    if route:
                        load_group(sp, b, 0)
                    load_group(sp, b, 1)
                    if not (isinstance(b, int) and b == B - 1):
                        load_values(sp, b + 1, 1 - par)
                if route:
                    load_x(sp, b - 1)
                if not values:
                    sp.wait_ge(s_v_made, 12 * B)
                    for e in range(2):
                        load_expert_weights(sp, e, e)
                if values:
                    load_group(sp, b, 2)
                    load_group(sp, b, 3)
                if route:
                    save_route(sp, b - 1)
                if not values:
                    for e in range(2, LATE_FIRST):
                        load_expert_weights(sp, e, e)

            def all_batches2(eng, batch):
                batch(eng, 0, 0, True, False)
                batch(eng, 1, 1, True, True)
                with eng.Fori(1, B // 2 - 1) as i:
                    batch(eng, i * 2, 0, True, True)
                    batch(eng, i * 2 + 1, 1, True, True)
                batch(eng, B - 2, 0, True, True)
                batch(eng, B - 1, 1, True, True)
                batch(eng, B, 0, False, True)

            @block.sync
            def _(sp):
                load_group(sp, 0, 0)
                sp.dma_start(kv[CH:CH + 2, :, 0, :, :].rearrange("p g a n -> p g (a n)"),
                             vbias_d.rearrange("i g a n -> i g (a n)")).then_inc(s_vb_rows_in, 16)
                sp.dma_start(obrow[:, :], o_b.rearrange("(a n) -> a n", a=1).broadcast_to([S, DIM])).then_inc(s_ob_in, 16)
                sp.dma_start(gw_raw[:, :], gate_w).then_inc(s_gw_in, 16)
                all_batches2(sp, sp_batch)
                sp.wait_ge(s_x2_saved, 16 * B)

            def project_values(pe, b, par, g, first=0):
                for c in range(first, 3):
                    after(pe, s_v_lo, 3 * (b * NG + g) + c - 1)
                    make_values(pe, pv[(3 * g + c) % 2], par, g, c)

            def attend(pe, b, g):
                n = b * NG + g
                pe.wait_ge(s_v_lo, 3 * n + 3)
                pe.wait_ge(s_p_in[g % 2], 16 * (b * (NG // 2) + g // 2 + 1))
                pe.wait_ge(s_vrem_in[g % 2], 16 * (b * (NG // 2) + g // 2 + 1))
                after(pe, s_att_lo, n - 1)
                for hh in range(HG):
                    for c in range(3):
                        rows = CH + 2 if c == 0 else CH
                        mm = split_matmul(pe, pa[g % 2][:, hh * S:(hh + 1) * S],
                                          (kv[0:rows, g, c, 0, hh * D:(hh + 1) * D],
                                           kv[0:rows, g, c, 1, hh * D:(hh + 1) * D]),
                                          (pin[0:rows, g % 2, hh, 0, c * S:(c + 1) * S],
                                           pin[0:rows, g % 2, hh, 1, c * S:(c + 1) * S]), c == 0, c == 2)
                mm.then_inc(s_att, 1)

            def project_out(pe, b):
                pe.wait_ge(s_att_lo, NG * b + NG)
                after(pe, s_x2, b)
                for h in range(H):
                    mm = split_matmul(pe, po[0:S, :], (outT[:, h, 0, :], outT[:, h, 1, :]),
                                      (w_hi[O_SLOT][:, h // HG, (h % HG) * 512:(h % HG + 1) * 512],
                                       w_lo[O_SLOT][:, h // HG, (h % HG) * 512:(h % HG + 1) * 512]), h == 0, h == H - 1)
                mm.then_inc(s_o_made, 1)

            def turn_route(pe, b):
                pe.wait_ge(s_xn2, b + 1)
                after(pe, s_xn2T, b)
                for k in range(KT):
                    mm = pe.transpose(pg[:, k * S:(k + 1) * S], xn2[:, k * P:(k + 1) * P], ident[0:S, 0:S])
                mm.then_inc(s_xn2_turned, 1)

            def make_logits(pe, b):
                pe.wait_ge(s_xn2T, b + 1)
                if isinstance(b, int) and b == 0:
                    pe.wait_ge(s_gwT, 1)
                else:
                    pe.wait_ge(s_lexp, b)
                for k in range(KT):
                    mm = pe.matmul(pl[0:S, 0:E], xn2T[:, k * S:(k + 1) * S], gwT[:, k, :], start=k == 0,
                                   stop=k == KT - 1)
                mm.then_inc(s_logits, 1)

            def make_positions(pe, b):
                pe.wait_ge(s_sel, b + 1)
                pe.matmul(pp[0:S, 0:E], trib[:, :], selb[:, :], start=True, stop=False)
                pe.matmul(pp[0:S, 0:E], onesb[:, :], cumb[:, :], start=False, stop=True).then_inc(s_pos, 1)

            def pe_batch2(pe, b, par, values, route):
                if values and not route:
                    project_values(pe, b, par, NG - 1, 2)
                    pe.wait_ge(s_gw_in, 16)
                    for k in range(KT):
                        mm = pe.transpose(pl[:, k * E:(k + 1) * E], gw_raw[:, k * P:(k + 1) * P], ident[0:E, 0:E])
                    mm.then_inc(s_gw_turned, 1)
                    pe.wait_ge(s_vb_rows_in, 16)
                    for g in range(NG):
                        attend(pe, b, g)
                    return
                if values:
                    pe.wait_ge(s_ctxT_in, 16 * b + 16)
                    project_values(pe, b, par, 0)
                project_out(pe, b - 1)
                if values:
                    project_values(pe, b, par, 1)
                    attend(pe, b, 0)
                turn_route(pe, b - 1)
                if values:
                    project_values(pe, b, par, 2)
                make_logits(pe, b - 1)
                if values:
                    attend(pe, b, 1)
                    project_values(pe, b, par, 3)
                make_positions(pe, b - 1)
                if values:
                    attend(pe, b, 2)
                    attend(pe, b, 3)

            @block.tensor
            def _(pe):
                all_batches2(pe, pe_batch2)

            def act_values(act, b, g, first=0):
                for c in range(first, 3):
                    values_hi(act, pv[(3 * g + c) % 2], b, g, c)

            def act_attend(act, b, g):
                act.wait_ge(s_att, b * NG + g + 1)
                nc.scalar.copy(outT[:, g * HG:(g + 1) * HG, 0, :],
                               pa[g % 2][:, 0:HG * S].rearrange("p (h s) -> p h s", h=HG)).then_inc(s_att_hi, 1)

            def act_batch2(act, b, par, values, route):
                if values and not route:
                    act_values(act, b, NG - 1, 2)
                    act.wait_ge(s_gw_turned, 1)
                    nc.scalar.copy(gwT[:, :, :].rearrange("p k e -> p (k e)"), pl[:, 0:KT * E]).then_inc(s_gwT, 1)
                    for g in range(NG):
                        act_attend(act, b, g)
                    return
                if values:
                    act_values(act, b, 0)
                    act_values(act, b, 1)
                    act_attend(act, b, 0)
                if route:
                    act.wait_ge(s_xn2_turned, b)
                    nc.scalar.copy(xn2T[:, :], pg[:, 0:KT * S]).then_inc(s_xn2T, 1)
                if values:
                    act_values(act, b, 2)
                if route:
                    act.wait_ge(s_lnmax, b)
                    nc.scalar.activation(ex[:, :], pl[0:S, 0:E], ACT.Exp, bias=lmax[:, 1:2]).then_inc(s_lexp, 1)
                if values:
                    act_attend(act, b, 1)
                    act_values(act, b, 3)
                    act_attend(act, b, 2)
                    act_attend(act, b, 3)

            @block.scalar
            def _(act):
                all_batches2(act, act_batch2)
                act.wait_ge(s_att, B * NG)
                early_hi(act, 0)

            def dve_values(dve, b, g, first=0):
                for c in range(first, 3):
                    values_lo(dve, pv[(3 * g + c) % 2], b, g, c)

            def dve_attend(dve, b, g):
                dve.wait_ge(s_att_hi, b * NG + g + 1)
                nc.vector.tensor_tensor(outT[:, g * HG:(g + 1) * HG, 1, :],
                                        pa[g % 2][:, 0:HG * S].rearrange("p (h s) -> p h s", h=HG),
                                        outT[:, g * HG:(g + 1) * HG, 0, :], ALU.subtract).then_inc(s_att_lo, 1)

            def dve_residual(dve, b):
                dve.wait_ge(s_o_made, b + 1)
                dve.wait_ge(s_xr, b + 1)
                after(dve, s_x2_saved, 16 * b)
                nc.vector.scalar_tensor_tensor(x2[:, :], po[0:S, :], tg[0:S, 0:1], xr[:, :], ALU.mult,
                                               ALU.add).then_inc(s_x2, 1)
                dve.wait_ge(s_x2, b + 1)
                nc.vector.bn_stats(stats2[:, :], x2[:, :]).then_inc(s_x2_stats, 1)
                dve.wait_ge(s_x2_stats, b + 1)
                nc.vector.memset(pause[:, :], 0.0)
                nc.vector.bn_aggr(mv2[:, :], stats2[:, :]).then_inc(s_x2_aggr, 1)

            def dve_normalise2(dve, b):
                dve.wait_ge(s_x2_rstd, b + 1)
                after(dve, s_xn2_turned, b)
                nc.vector.tensor_scalar(xn2[:, :], x2[:, :], mv2[:, 0:1], rstd2[:, 0:1], ALU.subtract,
                                        ALU.mult).then_inc(s_xn2, 1)
                dve.wait_ge(s_xn2, b + 1)
                after(dve, s_dispatched, 16 * TOPK * b)
                by_tile = xn2[:, :].rearrange("s (p c) -> s c p", c=KT)
                nc.vector.tensor_copy(xd_hi, by_tile)
                nc.vector.tensor_copy(xd_tok, tokf[:, :]).then_inc(s_xd_hi, 1)
                dve.wait_ge(s_xd_hi, b + 1)
                nc.vector.tensor_scalar(tokf[:, :], tokf[:, :], float(S), None, ALU.add)
                nc.vector.tensor_tensor(xd_lo, by_tile, xd_hi, ALU.subtract).then_inc(s_xd, 1)

            def dve_select(dve, b):
                dve.wait_ge(s_logits, b + 1)
                nc.vector.tensor_reduce(lmax[:, 0:1], pl[0:S, 0:E], AX.X, ALU.max).then_inc(s_lmax, 1)
                dve.wait_ge(s_lmax, b + 1)
                nc.vector.tensor_scalar(lmax[:, 1:2], lmax[:, 0:1], -1.0, None, ALU.mult).then_inc(s_lnmax, 1)

            def dve_choose(dve, b, link):
                dve.wait_ge(s_lexp, b + 1)
                nc.vector.memset(pause[:, :], 0.0)
                link(nc.vector.max(top8[:, :], ex[:, :]))
                nc.vector.memset(pause[:, :], 0.0)
                link(nc.vector.match_replace(left[:, :], top8[:, :], ex[:, :], -1.0))
                nc.vector.tensor_reduce(wsum[:, 0:1], top8[:, :], AX.X, ALU.add)
                if not (isinstance(b, int) and b == 0):
                    dve.wait_ge(s_pos, b)
                    link(nc.vector.tensor_tensor(cumb[:, :], cumb[:, :], selb[:, :], ALU.add))
                else:
                    link(nc.vector.memset(cumb[:, :], 0.0))
                nc.vector.tensor_scalar(selb[:, :], left[:, :], 0.0, None, ALU.is_lt).then_inc(s_sel, 1)
                link(nc.vector.reciprocal(wsum[:, 1:2], wsum[:, 0:1]))
                link(nc.vector.tensor_scalar(wsum[:, 2:3], wsum[:, 1:2], tg[0:S, 1:2], None, ALU.mult))

            def dve_slots(dve, b, link):
                dve.wait_ge(s_pos, b + 1)
                nc.vector.tensor_tensor(slot[:, :], slots_left[:, :], pp[0:S, 0:E], ALU.subtract)
                link(nc.vector.scalar_tensor_tensor(val[:, :], pp[0:S, 0:E], float(CAP), selb[:, :], ALU.is_lt, ALU.mult))
                nc.vector.scalar_tensor_tensor(xd_w, ex[:, :], wsum[:, 2:3], val[:, :], ALU.mult, ALU.mult)
                link(nc.vector.tensor_tensor(key[:, :], slot[:, :], val[:, :], ALU.mult))
                nc.vector.memset(pause[:, :], 0.0)
                link(nc.vector.max(key8[:, :], key[:, :]))
                nc.vector.tensor_scalar(idx[:, :], key8[:, :], -1.0, float(SLOTS), ALU.mult, ALU.add).then_inc(s_idx, 1)

            def linker(dve, b):
                count = [0]

                def link(ins):
                    count[0] += 1
                    assert count[0] <= ROUTE_STEPS
                    ins.then_inc(s_route, 1)
                    dve.wait_ge(s_route, b * ROUTE_STEPS + count[0])
                return link, count

            def dve_batch2(dve, b, par, values, route):
                if values and not route:
                    dve_values(dve, b, NG - 1, 2)
                    for g in range(NG):
                        dve_attend(dve, b, g)
                    return
                if values:
                    dve_values(dve, b, 0)
                if route:
                    dve_residual(dve, b - 1)
                if values:
                    dve_values(dve, b, 1)
                if route:
                    dve_normalise2(dve, b - 1)
                if values:
                    dve_attend(dve, b, 0)
                    dve_values(dve, b, 2)
                if route:
                    dve_select(dve, b - 1)
                if values:
                    dve_attend(dve, b, 1)
                if route:
                    link, count = linker(dve, b - 1)
                    dve_choose(dve, b - 1, link)
                if values:
                    dve_values(dve, b, 3)
                if route:
                    dve_slots(dve, b - 1, link)
                    assert count[0] == ROUTE_STEPS
                if values:
                    dve_attend(dve, b, 2)
                    dve_attend(dve, b, 3)

            @block.vector
            def _(dve):
                dve.wait_ge(s_tanh, 1)
                nc.vector.memset(xd[:, ROW - 4:ROW], 0)
                nc.vector.tensor_copy(tokf[:, :], tok1[0:S, :])
                dve.wait_ge(s_ob_in, 16)
                nc.vector.tensor_scalar(obrow[:, :], obrow[:, :], tg[0:S, 0:1], None, ALU.mult).then_inc(s_obrow, 1)
                all_batches2(dve, dve_batch2)

            def pool_route(pool, b):
                pool.wait_ge(s_xr_in, 16 * b + 16)
                after(pool, s_x2, b)
                nc.gpsimd.tensor_tensor(xr[:, :], xr_in[:, :], obrow[:, :], ALU.add).then_inc(s_xr, 1)
                pool.wait_ge(s_x2_aggr, b + 1)
                nc.gpsimd.tensor_tensor(rstd2[:, :], mv2[:, 1:2], ln_eps[0:S, :], ALU.add).then_inc(s_x2_var, 1)
                pool.wait_ge(s_x2_var, b + 1)
                nc.gpsimd.tensor_tensor(rstd2[:, :], rstd2[:, :], mhalf[0:S, 0:1], ALU.pow).then_inc(s_x2_rstd, 1)
                if isinstance(b, int) and b == B - 1:
                    return
                pool.wait_ge(s_xd, b + 1)
                pool.wait_ge(s_idx, b + 1)
                nc.gpsimd.tensor_tensor(pool_pause[:, 0:1], mhalf[0:1, 0:1], mhalf[0:1, 1:2], ALU.add)
                for k in range(TOPK):
                    nc.gpsimd.indirect_dma_start(
                        xin_d, bass.IndirectOffsetOnAxis(ap=idx[:, k:k + 1], axis=0),
                        xd[:, :], None,
                        bounds_check=SLOTS - 1, oob_is_err=False).then_inc(s_dispatched, 16)

            @block.gpsimd
            def _(pool):
                pool.wait_ge(s_obrow, 1)
                pool_route(pool, 0)
                with pool.Fori(1, B - 1) as b:
                    pool_route(pool, b)
                pool_route(pool, B - 1)
                pool.wait_ge(s_dispatched, 16 * TOPK * (B - 1))

    s_rows_in = [sem(f"s_rows_in{i}") for i in range(NR3)]
    s_rows_turned = sem("s_rows_turned")
    s_rowsT = sem("s_rowsT")
    s_gu_made = sem("s_gu_made")
    s_silu = sem("s_silu")
    s_hid = sem("s_hid")
    s_hid_turned = sem("s_hid_turned")
    s_hid_hi = sem("s_hid_hi")
    s_hid_lo = sem("s_hid_lo")
    s_y_made = sem("s_y_made")
    s_y_out = sem("s_y_out")
    s_empty = sem("s_empty")
    s_target = sem("s_target")
    s_y_added = [sem(f"s_y_added{i}") for i in range(2)]
    s_out_added = sem("s_out_added")
    s_last_rows = [sem(f"s_last_rows{k}") for k in range(TOPK)]
    s_pause = sem("s_pause")
    s_out = sem("s_out")
    with nc.Block() as block, ExitStack() as ph3, ExitStack() as ps3:
        for r in range(2, NR3):
            place = sb(ph3, f"dn{r}", [FC, 2, DN_N], BF16)
            dn.append(place[:, :, :])
        rows = sb(ph3, "rows", [P, NR3, ROW], U16)
        empty = sb(ph3, "empty", [P, 2], F32)
        target = sb(ph3, "target", [P, NR3, 1], U32)
        w_slot = sb(ph3, "w_slot", [P, NR3, 1], F32)
        pool_pause3 = sb(ph3, "pool_pause3", [1, 1], F32)
        rowsT = sb(ph3, "rowsT", [P, 2, 2 * KT, P], BF16)
        silu_first = sb(ph3, "silu_first", [1, 1], F32)
        sg = sb(ph3, "sg", [P, FF], F32)
        hid = sb(ph3, "hid", [P, 2, FF], F32)
        hidT = sb(ph3, "hidT", [FC, 2, FT, P], BF16)
        ybuf = sb(ph3, "ybuf", [P, NR3, DIM], F32)

        def pb3(name, shape, dt=F32):
            return ps3.enter_context(nc.psum_tensor(name, shape, dt))
        px = [pb3(f"px{i}", [P, 2 * KT, P], BF16) for i in range(2)]
        pgu = [pb3(f"pgu{i}", [P, 512]) for i in range(2)]
        ph = [pb3(f"ph{i}", [P, 512]) for i in range(2)]
        py = [pb3(f"py{i}", [P, 512]) for i in range(2)]

        UNROLL = 8
        FIRST = 7
        LAST = E - 2
        assert (LAST - FIRST + 1) % UNROLL == 0

        def count_of(e_base, j, size):
            if isinstance(e_base, int):
                return (e_base * UNROLL + j) // size + 1
            return e_base * (UNROLL // size) + (j // size + 1)

        def walk(eng, body):
            def turn(i, j):
                body(lambda a, off=0: (i * UNROLL + j + off) * a if isinstance(i, int) else i * (UNROLL * a) + (j + off) * a,
                     lambda size, off=0: count_of(i, j + off, size), j, not isinstance(i, int))
            for e in range(FIRST):
                turn(0, e)
            with eng.Fori(0, (LAST - FIRST + 1) // UNROLL) as i:
                for j in range(FIRST, FIRST + UNROLL):
                    turn(i, j)
            for e in range(LAST + 1, E + 1):
                turn(0, e)

        @block.sync
        def _(sp):
            ROWS_AHEAD, WEIGHTS_AHEAD = NR3 - 1, NRAW - 1

            def load_rows(e, j):
                after(sp, s_target, e - NR3 + 1)
                after(sp, s_rows_turned, e - NR3 + 1)
                if isinstance(e, int) and e < TOPK:
                    sp.wait_ge(s_last_rows[e], 16)
                sp.dma_start(rows[:, j % NR3, :], xin_d.rearrange("(e c) n -> e c n", c=CAP)[e]).then_inc(s_rows_in[j % NR3], 16)

            def load_weights_ring(e, j):
                after(sp, s_gu_lo, e - NRAW + 1)
                after(sp, s_d_lo, e - NRAW + 1)
                load_expert_weights(sp, e, j % NRAW)

            def body(e, j, looped):
                if looped or e + ROWS_AHEAD < E:
                    load_rows(e + ROWS_AHEAD, j + ROWS_AHEAD)
                if looped or NRAW + EARLY <= e + WEIGHTS_AHEAD < E:
                    load_weights_ring(e + WEIGHTS_AHEAD, j + WEIGHTS_AHEAD)
            for e in range(ROWS_AHEAD):
                load_rows(e, e)
            for e in range(NRAW, NRAW + EARLY):
                load_weights_ring(e, e)
            for e in range(FIRST):
                body(e, e, False)
            turns = (E - WEIGHTS_AHEAD - FIRST) // UNROLL
            with sp.Fori(0, turns) as i:
                for j in range(FIRST, FIRST + UNROLL):
                    body(i * UNROLL + j, j, True)
            for e in range(FIRST + turns * UNROLL, E + 1):
                body(e, e, False)
            sp.wait_ge(s_y_added[0], 16 * E // 2)
            sp.dma_start(out.rearrange("b s n -> (b s) n"), acc_d[0][0:TOKENS, :]).then_inc(s_out, 16)

        @block.tensor
        def _(pe):
            def turn_rows(n, c, j):
                pe.wait_ge(s_rows_in[j % NR3], c * 16)
                after(pe, s_rowsT, n(1, -1))
                for q in range(2 * KT):
                    mm = pe.transpose(px[j % 2][:, q, :], rows[:, j % NR3, q * P:(q + 1) * P].bitcast(BF16), identb[:, :])
                mm.then_inc(s_rows_turned, 1)

            def body(n, c, j, looped):
                e = n(1)
                here, before, ahead = looped or e < E, looped or e >= 1, looped or e + 1 < E
                if not looped and e == 0:
                    turn_rows(n, c(NR3), j)
                if before:
                    pe.wait_ge(s_hid, n(1))
                    after(pe, s_hid_lo, n(1, -2))
                    for q in range(FT):
                        hv = hid[:, (j - 1) % 2, :].rearrange("s (p c) -> s c p", c=FT)
                        mm = pe.transpose(ph[(j - 1) % 2][0:FC, q * P:(q + 1) * P], hv[:, q, :], ident[:, :])
                    mm.then_inc(s_hid_turned, 1)
                if ahead:
                    turn_rows(lambda a, off=0: n(a, 1 + off), c(NR3, 1), j + 1)
                if here:
                    pe.wait_ge(s_rowsT, n(1, 1))
                    pe.wait_ge(s_gu_lo, n(1, 1))
                    after(pe, s_hid, n(1, -1))
                    for k in range(KT):
                        tile = slice(k * 2 * FF, (k + 1) * 2 * FF)
                        mm = split_matmul(pe, pgu[j % 2][:, 0:2 * FF],
                                          (rowsT[:, j % 2, k, :], rowsT[:, j % 2, KT + k, :]),
                                          (gu[j % 2][:, 0, tile], gu[j % 2][:, 1, tile]), k == 0, k == KT - 1)
                    mm.then_inc(s_gu_made, 1)
                if before:
                    p = (j - 1) % 2
                    pe.wait_ge(s_hid_lo, n(1))
                    pe.wait_ge(s_d_lo, n(1))
                    after(pe, s_y_out, n(1, -2))
                    for q in range(FT):
                        mm = split_matmul(pe, py[p][:, :], (hidT[:, 0, q, :], hidT[:, 1, q, :]),
                                          (dn[(j - 1) % NR3][:, 0, q * DIM:(q + 1) * DIM],
                                           dn[(j - 1) % NR3][:, 1, q * DIM:(q + 1) * DIM]),
                                          q == 0, q == FT - 1)
                    mm.then_inc(s_y_made, 1)
            walk(pe, body)

        @block.scalar
        def _(act):
            for e in range(1, EARLY):
                early_hi(act, e)
            nc.scalar.activation(silu_first[:, :], mhalf[0:1, 0:1], ACT.Silu)

            def body(n, c, j, looped):
                e = n(1)
                here, before, ahead = looped or e < E, looped or e >= 1, looped or e + 1 < E

                def hi(off):
                    r, p = (j + off) % NRAW, (j + off) % 2
                    act.wait_ge(s_ew_in[r], 48 * c(NRAW, off))
                    after(act, s_gu_made, n(1, off - 1))
                    nc.scalar.copy(gu[p][:, 0, :],
                                   raw_gu(r)).then_inc(s_gu_hi, 1)

                def turned(off):
                    p = (j + off) % 2
                    act.wait_ge(s_rows_turned, n(1, off + 1))
                    after(act, s_gu_made, n(1, off - 1))
                    nc.scalar.copy(rowsT[:, p, :, :], px[p][:, :, :]).then_inc(s_rowsT, 1)
                if not looped and e == 0:
                    turned(0)
                if before:
                    act.wait_ge(s_hid_turned, n(1))
                    after(act, s_y_made, n(1, -1))
                    nc.scalar.copy(hidT[:, 0, :, :], ph[(j - 1) % 2][0:FC, 0:FT * P].rearrange("p (c s) -> p c s", c=FT)).then_inc(s_hid_hi, 1)
                if looped or EARLY <= e + 1 < E:
                    hi(1)
                if ahead:
                    turned(1)
                if here:
                    act.wait_ge(s_gu_made, n(1, 1))
                    after(act, s_hid, n(1))
                    nc.scalar.activation(sg[:, :], pgu[j % 2][:, 0:FF], ACT.Silu).then_inc(s_silu, 1)
            walk(act, body)

        @block.vector
        def _(dve):
            for e in range(EARLY):
                dve.wait_ge(s_gu_hi, e + 1)
                nc.vector.tensor_tensor(gu[e][:, 1, :], raw_gu(e), gu[e][:, 0, :], ALU.subtract).then_inc(s_gu_lo, 1)
                dve.wait_ge(s_d_hi, e + 1)
                nc.vector.tensor_tensor(dn[e][:, 1, :], raw_d(e), dn[e][:, 0, :], ALU.subtract).then_inc(s_d_lo, 1)
            def body(n, c, j, looped):
                e = n(1)
                here, before, ahead = looped or e < E, looped or e >= 1, looped or e + 1 < E

                def lo(off, half):
                    r, p = (j + off) % NRAW, (j + off) % 2
                    part = slice(half * KT * FF, (half + 1) * KT * FF)
                    if half == 0:
                        dve.wait_ge(s_gu_hi, n(1, off + 1))
                    last = nc.vector.tensor_tensor(gu[p][:, 1, part],
                                                   raw_gu(r)[:, part],
                                                   gu[p][:, 0, part], ALU.subtract)
                    if half == 1:
                        last.then_inc(s_gu_lo, 1)

                def d_hi(off):
                    r, p = (j + off) % NRAW, (j + off) % 2
                    dve.wait_ge(s_ew_in[r], 48 * c(NRAW, off))
                    after(dve, s_y_made, n(1, off - 3))
                    nc.vector.tensor_copy(dn[(j + off) % NR3][:, 0, :], raw_d(r)).then_inc(s_d_hi, 1)
                if before:
                    dve.wait_ge(s_hid_hi, n(1))
                    nc.vector.tensor_tensor(hidT[:, 1, :, :], ph[(j - 1) % 2][0:FC, 0:FT * P].rearrange("p (c s) -> p c s", c=FT),
                                            hidT[:, 0, :, :], ALU.subtract).then_inc(s_hid_lo, 1)
                split = looped or EARLY <= e + 1 < E
                if split:
                    d_hi(1)
                    lo(1, 0)
                if here:
                    dve.wait_ge(s_silu, n(1, 1))
                    after(dve, s_hid_turned, n(1, -1))
                    nc.vector.tensor_tensor(hid[:, j % 2, :], sg[:, :], pgu[j % 2][:, FF:2 * FF], ALU.mult).then_inc(s_hid, 1)
                if split:
                    lo(1, 1)
                if here:
                    dve.wait_ge(s_rows_in[j % NR3], 16 * c(NR3))
                    after(dve, s_y_added[j % 2], 16 * (c(2) - NR3 // 2))
                    row_f = rows[:, j % NR3, :].bitcast(F32)
                    nc.vector.tensor_copy(w_slot[:, j % NR3, :], row_f[:, bass.ds(n(1) + DIM, 1)])
                    tok = row_f[:, ROW // 2 - 2:ROW // 2 - 1]
                    nc.vector.tensor_scalar(empty[:, j % 2:j % 2 + 1], tok, 0.0, empty_row[:, 0:1], ALU.is_equal, ALU.mult).then_inc(s_empty, 1)
                    dve.wait_ge(s_empty, n(1, 1))
                    nc.vector.scalar_tensor_tensor(target[:, j % NR3, :], tok, -1.0, empty[:, j % 2:j % 2 + 1], ALU.add, ALU.add).then_inc(s_target, 1)
                if before:
                    p = (j - 1) % 2
                    dve.wait_ge(s_y_made, n(1))
                    r = (j - 1) % NR3
                    dve.wait_ge(s_target, n(1))
                    nc.vector.tensor_scalar(ybuf[:, r, :], py[p][:, :], w_slot[:, r, 0:1], None, ALU.mult).then_inc(s_y_out, 1)
            walk(dve, body)

        @block.gpsimd
        def _(pool):
            pool.wait_ge(s_xd, B)
            pool.wait_ge(s_idx, B)
            for k in range(TOPK):
                nc.gpsimd.indirect_dma_start(
                    xin_d, bass.IndirectOffsetOnAxis(ap=idx[:, k:k + 1], axis=0),
                    xd[:, :], None,
                    bounds_check=SLOTS - 1, oob_is_err=False).then_inc(s_last_rows[k], 16)

            def body(n, c, j, looped):
                e = n(1)
                if looped or EARLY <= e < E:
                    r = j % NRAW
                    pool.wait_ge(s_d_hi, n(1, 1))
                    nc.gpsimd.tensor_tensor(dn[j % NR3][:, 1, :], raw_d(r), dn[j % NR3][:, 0, :], ALU.subtract).then_inc(s_d_lo, 1)
                if looped or e >= 1:
                    r = (j - 1) % NR3
                    pool.wait_ge(s_y_out, n(1))
                    after(pool, s_y_added[r % 2], 16 * (c(2, -1) - 1))
                    after(pool, s_pause, n(1, -1))
                    nc.gpsimd.tensor_tensor(pool_pause3[:, :], mhalf[0:1, 0:1], mhalf[0:1, 1:2], ALU.add).then_inc(s_pause, 1)
                    nc.gpsimd.indirect_dma_start(
                        acc_d[r % 2], bass.IndirectOffsetOnAxis(ap=target[:, r, :], axis=0), ybuf[:, r, :], None,
                        bounds_check=TOKENS + CAP - 1, oob_is_err=True, compute_op=ALU.add).then_inc(s_y_added[r % 2], 16)
            walk(pool, body)
            pool.wait_ge(s_out, 16)
            pool.wait_ge(s_y_added[1], 16 * E // 2)
            nc.gpsimd.dma_start(out.rearrange("b s n -> (b s) n"), acc_d[1][0:TOKENS, :],
                                accum_op=ALU.add, max_dma_last_dim=4 * DIM).then_inc(s_out_added, 16)
            pool.wait_ge(s_out_added, 16)


_INS = ['x', 'ctx_2048', 'g_xattn', 'g_ffn', 'L0_xattn_q_w', 'L0_xattn_q_b', 'L0_xattn_k_w', 'L0_xattn_k_b',
        'L0_xattn_v_w', 'L0_xattn_v_b', 'L0_xattn_ki_w', 'L0_xattn_ki_b', 'L0_xattn_vi_w', 'L0_xattn_vi_b',
        'L0_xattn_o_w', 'L0_xattn_o_b', 'L0_xattn_nq_s', 'L0_xattn_nkt_s', 'L0_xattn_nki_s', 'L0_ffn_gate_w',
        'L0_ffn_wg', 'L0_ffn_wu', 'L0_ffn_wd']


def kernel(**inputs):
    import numpy as _np
    import concourse.bacc as _bacc
    from concourse import mybir as _mybir
    from concourse.bass_utils import run_bass_kernel_spmd as _run

    nc = _bacc.Bacc("TRN2", target_bir_lowering=False, num_devices=1)
    arrays, args = {}, []
    for name in _INS:
        a = _np.ascontiguousarray(inputs[name])
        arrays[f"in_{name}"] = a
        args.append(nc.dram_tensor(f"in_{name}", a.shape, _mybir.dt.from_np(a.dtype), kind="ExternalInput").ap())
    args.append(nc.dram_tensor("out_y", (B, S, DIM), F32, kind="ExternalOutput").ap())
    build(nc, *args)
    r = _run(nc, [arrays], core_ids=[0])
    return r.results[0]["out_y"]
```
